# Optimizing a Trainium2 kernel written in Bass

```python
import numpy as np
import jax
import jax.numpy as jnp

def _softmax(x, axis=-1):
    return jax.nn.softmax(x, axis=axis)

def _gelu(x):
    return jax.nn.gelu(x, approximate=True)

def _silu(x):
    return jax.nn.silu(x)

def _sigmoid(x):
    return jax.nn.sigmoid(x)

def _layernorm(x, axis=-1, eps=1e-05):
    m = jnp.mean(x, axis=axis, keepdims=True)
    v = jnp.var(x, axis=axis, keepdims=True)
    return (x - m) / jnp.sqrt(v + eps)

def _scatter_add(tgt, idx, src, axis=0):
    return tgt.at[idx].add(src)

def _segment_sum(src, seg, n):
    return jax.ops.segment_sum(src, seg, n)
kernel_name = 'mk_lm_tower_d1_tok_ids1024_r4_6be53a'

def setup_inputs(seed: int=0):
    np.random.seed(seed)
    _w = jnp.asarray

    def _rec_inputs():
        import jax
        import jax.numpy as jnp
        _rk = jax.random.key(seed)
        x = jax.random.randint(jax.random.fold_in(_rk, 1), (8, 512), 0, 31999, jnp.int32)
        _lenS = jnp.full((8,), 512, jnp.int32)
        return (x, _lenS)
    x, _lenS = _rec_inputs()

    def _L0_tok_setup():
        import jax, jax.numpy as jnp
        import numpy as np
        L, D, DF, V = (6, 256, 1024, 8000)
        B, T = (4, 512)
        EPS = 1e-05

        def pos_encoding(t_len, d_model):
            i = jnp.arange(d_model, dtype=jnp.float32)
            pos = jnp.arange(t_len, dtype=jnp.float32)[:, None]
            even = jnp.arange(d_model) % 2 == 0
            sin_part = jnp.sin(pos / 10.0 ** (4.0 * i / d_model))
            cos_part = jnp.cos(pos / 10.0 ** (4.0 * (i - 1.0) / d_model))
            return jnp.where(even[None, :], sin_part, cos_part)

        def layernorm(x, g, b):
            m = jnp.mean(x, axis=-1, keepdims=True)
            v = jnp.mean(jnp.square(x - m), axis=-1, keepdims=True)
            return (x - m) * jax.lax.rsqrt(v + EPS) * g + b

        def encoder(x, embed, ln1_g, ln1_b, ln2_g, ln2_b, W1, b1, W2, b2):
            h = embed[x]
            h = h + pos_encoding(h.shape[1], h.shape[2])
            scale = 1.0 / jnp.sqrt(jnp.asarray(D, dtype=h.dtype))
            for l in range(L):
                scores = jnp.einsum('btd,bsd->bts', h, h) * scale
                probs = jax.nn.softmax(scores, axis=-1)
                mha = jnp.einsum('bts,bsd->btd', probs, h)
                h1 = layernorm(h + mha, ln1_g[l], ln1_b[l])
                ff = jnp.maximum(h1 @ W1[l] + b1[l], 0.0) @ W2[l] + b2[l]
                h = layernorm(h1 + ff, ln2_g[l], ln2_b[l])
            return h
        key = jax.random.key(seed)
        ks = jax.random.split(key, 8)
        embed = jax.random.normal(ks[0], (V, D), dtype=jnp.float32) * 0.02
        W1 = jax.random.normal(ks[1], (L, D, DF), dtype=jnp.float32) * 0.02
        b1 = jnp.zeros((L, DF), dtype=jnp.float32)
        W2 = jax.random.normal(ks[2], (L, DF, D), dtype=jnp.float32) * 0.02
        b2 = jnp.zeros((L, D), dtype=jnp.float32)
        ln1_g = jnp.ones((L, D), dtype=jnp.float32)
        ln1_b = jnp.zeros((L, D), dtype=jnp.float32)
        ln2_g = jnp.ones((L, D), dtype=jnp.float32)
        ln2_b = jnp.zeros((L, D), dtype=jnp.float32)
        x = jax.random.randint(ks[3], (B, T), 0, V, dtype=jnp.int64 if jax.config.read('jax_enable_x64') else jnp.int32)
        src_batch_lens = jax.random.randint(ks[4], (B,), 1, T, dtype=jnp.int32)
        return {'x': x, 'src_batch_lens': src_batch_lens, 'embed': embed, 'ln1_g': ln1_g, 'ln1_b': ln1_b, 'ln2_g': ln2_g, 'ln2_b': ln2_b, 'W1': W1, 'b1': b1, 'W2': W2, 'b2': b2}
    _L0_tok_all = _L0_tok_setup()
    _L0_tok_in = {k: v for k, v in _L0_tok_all.items() if k in ('embed', 'ln1_g', 'ln1_b', 'ln2_g', 'ln2_b', 'W1', 'b1', 'W2', 'b2')}
    del _L0_tok_all

    def _L0_attn_setup():
        import jax, jax.numpy as jnp
        import numpy as np
        NUM_HEADS = 16
        WINDOW_SIZE = 64
        key = jax.random.key(seed)
        ks = jax.random.split(key, 5)
        B, S, H = (2, 512, 256)
        scale = 0.02
        return {'x': jax.random.normal(ks[0], (B, S, H), dtype=jnp.float32), 'Wq': jax.random.normal(ks[1], (H, H), dtype=jnp.float32) * scale, 'bq': jnp.zeros((H,), dtype=jnp.float32), 'Wk': jax.random.normal(ks[2], (H, H), dtype=jnp.float32) * scale, 'bk': jnp.zeros((H,), dtype=jnp.float32), 'Wv': jax.random.normal(ks[3], (H, H), dtype=jnp.float32) * scale, 'bv': jnp.zeros((H,), dtype=jnp.float32), 'Wo': jax.random.normal(ks[4], (H, H), dtype=jnp.float32) * scale, 'bo': jnp.zeros((H,), dtype=jnp.float32)}
    _L0_attn_all = _L0_attn_setup()
    _L0_attn_in = {k: v for k, v in _L0_attn_all.items() if k in ('Wq', 'bq', 'Wk', 'bk', 'Wv', 'bv', 'Wo', 'bo')}
    del _L0_attn_all

    def _L0_ffn_setup():
        import jax, jax.numpy as jnp
        import numpy as np
        B, S, H = (2, 256, 256)
        E, F = (16, 128)
        G, TOPK_G, TOPK = (4, 2, 4)
        N_SHARED = 2
        ROUTE_SCALE = 1.0
        FS = N_SHARED * F

        def _gate(x, w_gate):
            T = x.shape[0]
            scores = jax.nn.sigmoid(x @ w_gate.T)
            sv = scores.reshape(T, G, E // G)
            group_scores = jax.lax.top_k(sv, 2)[0].sum(-1)
            top_groups = jax.lax.top_k(group_scores, TOPK_G)[1]
            allowed = jnp.zeros((T, G), dtype=bool).at[jnp.arange(T)[:, None], top_groups].set(True)
            masked = jnp.where(allowed[:, :, None], sv, -jnp.inf).reshape(T, E)
            _, idx = jax.lax.top_k(masked, TOPK)
            w = jnp.take_along_axis(scores, idx, axis=1)
            w = w / (w.sum(-1, keepdims=True) + 1e-06) * ROUTE_SCALE
            return (w, idx)

        def _swiglu(x, w1, w3, w2):
            return jax.nn.silu(x @ w1.T) * (x @ w3.T) @ w2.T
        key = jax.random.key(seed)
        ks = jax.random.split(key, 8)
        scale = 0.02
        return {'hidden_states': jax.random.normal(ks[0], (B, S, H), dtype=jnp.float32), 'w_gate': jax.random.normal(ks[1], (E, H), dtype=jnp.float32) * scale, 'w1_e': jax.random.normal(ks[2], (E, F, H), dtype=jnp.float32) * scale, 'w3_e': jax.random.normal(ks[3], (E, F, H), dtype=jnp.float32) * scale, 'w2_e': jax.random.normal(ks[4], (E, H, F), dtype=jnp.float32) * scale, 'w1_s': jax.random.normal(ks[5], (FS, H), dtype=jnp.float32) * scale, 'w3_s': jax.random.normal(ks[6], (FS, H), dtype=jnp.float32) * scale, 'w2_s': jax.random.normal(ks[7], (H, FS), dtype=jnp.float32) * scale}
    _L0_ffn_all = _L0_ffn_setup()
    _L0_ffn_in = {k: v for k, v in _L0_ffn_all.items() if k in ('w_gate', 'w1_e', 'w3_e', 'w2_e', 'w1_s', 'w3_s', 'w2_s')}
    del _L0_ffn_all
    return {'x': x, '_lenS': _lenS, 'L0_tok_embed': _L0_tok_in['embed'], 'L0_tok_ln1_g': _L0_tok_in['ln1_g'], 'L0_tok_ln1_b': _L0_tok_in['ln1_b'], 'L0_tok_ln2_g': _L0_tok_in['ln2_g'], 'L0_tok_ln2_b': _L0_tok_in['ln2_b'], 'L0_tok_W1': _L0_tok_in['W1'], 'L0_tok_b1': _L0_tok_in['b1'], 'L0_tok_W2': _L0_tok_in['W2'], 'L0_tok_b2': _L0_tok_in['b2'], 'L0_attn_Wq': _L0_attn_in['Wq'], 'L0_attn_bq': _L0_attn_in['bq'], 'L0_attn_Wk': _L0_attn_in['Wk'], 'L0_attn_bk': _L0_attn_in['bk'], 'L0_attn_Wv': _L0_attn_in['Wv'], 'L0_attn_bv': _L0_attn_in['bv'], 'L0_attn_Wo': _L0_attn_in['Wo'], 'L0_attn_bo': _L0_attn_in['bo'], 'L0_ffn_w_gate': _L0_ffn_in['w_gate'], 'L0_ffn_w1_e': _L0_ffn_in['w1_e'], 'L0_ffn_w3_e': _L0_ffn_in['w3_e'], 'L0_ffn_w2_e': _L0_ffn_in['w2_e'], 'L0_ffn_w1_s': _L0_ffn_in['w1_s'], 'L0_ffn_w3_s': _L0_ffn_in['w3_s'], 'L0_ffn_w2_s': _L0_ffn_in['w2_s']}

def reference(x, _lenS, L0_tok_embed, L0_tok_ln1_g, L0_tok_ln1_b, L0_tok_ln2_g, L0_tok_ln2_b, L0_tok_W1, L0_tok_b1, L0_tok_W2, L0_tok_b2, L0_attn_Wq, L0_attn_bq, L0_attn_Wk, L0_attn_bk, L0_attn_Wv, L0_attn_bv, L0_attn_Wo, L0_attn_bo, L0_ffn_w_gate, L0_ffn_w1_e, L0_ffn_w3_e, L0_ffn_w2_e, L0_ffn_w1_s, L0_ffn_w3_s, L0_ffn_w2_s):
    import jax
    import jax.numpy as jnp

    def _L0_tok_ref(x, src_batch_lens, embed, ln1_g, ln1_b, ln2_g, ln2_b, W1, b1, W2, b2):
        import jax, jax.numpy as jnp
        import numpy as np
        L, D, DF, V = (6, 256, 1024, 8000)
        B, T = (4, 512)
        EPS = 1e-05

        def pos_encoding(t_len, d_model):
            i = jnp.arange(d_model, dtype=jnp.float32)
            pos = jnp.arange(t_len, dtype=jnp.float32)[:, None]
            even = jnp.arange(d_model) % 2 == 0
            sin_part = jnp.sin(pos / 10.0 ** (4.0 * i / d_model))
            cos_part = jnp.cos(pos / 10.0 ** (4.0 * (i - 1.0) / d_model))
            return jnp.where(even[None, :], sin_part, cos_part)

        def layernorm(x, g, b):
            m = jnp.mean(x, axis=-1, keepdims=True)
            v = jnp.mean(jnp.square(x - m), axis=-1, keepdims=True)
            return (x - m) * jax.lax.rsqrt(v + EPS) * g + b

        def encoder(x, embed, ln1_g, ln1_b, ln2_g, ln2_b, W1, b1, W2, b2):
            h = embed[x]
            h = h + pos_encoding(h.shape[1], h.shape[2])
            scale = 1.0 / jnp.sqrt(jnp.asarray(D, dtype=h.dtype))
            for l in range(L):
                scores = jnp.einsum('btd,bsd->bts', h, h) * scale
                probs = jax.nn.softmax(scores, axis=-1)
                mha = jnp.einsum('bts,bsd->btd', probs, h)
                h1 = layernorm(h + mha, ln1_g[l], ln1_b[l])
                ff = jnp.maximum(h1 @ W1[l] + b1[l], 0.0) @ W2[l] + b2[l]
                h = layernorm(h1 + ff, ln2_g[l], ln2_b[l])
            return h
        return encoder(x, embed, ln1_g, ln1_b, ln2_g, ln2_b, W1, b1, W2, b2)

    def _L0_attn_ref(x, Wq, bq, Wk, bk, Wv, bv, Wo, bo):
        import jax, jax.numpy as jnp
        import numpy as np
        NUM_HEADS = 16
        WINDOW_SIZE = 64
        B, S, Hs = x.shape
        nh = NUM_HEADS
        hd = Hs // nh
        half_w = WINDOW_SIZE // 2
        q = (x @ Wq + bq).reshape(B, S, nh, hd)
        k = (x @ Wk + bk).reshape(B, S, nh, hd)
        v = (x @ Wv + bv).reshape(B, S, nh, hd)
        scores = jnp.einsum('bqhd,bkhd->bhqk', q, k) / jnp.sqrt(jnp.asarray(hd, x.dtype))
        idx = jnp.arange(S)
        band = jnp.abs(idx[:, None] - idx[None, :]) <= half_w
        scores = jnp.where(band[None, None, :, :], scores, -jnp.inf)
        attn = jax.nn.softmax(scores, axis=-1)
        out = jnp.einsum('bhqk,bkhd->bqhd', attn, v).reshape(B, S, Hs)
        return out @ Wo + bo

    def _L0_ffn_ref(hidden_states, w_gate, w1_e, w3_e, w2_e, w1_s, w3_s, w2_s):
        import jax, jax.numpy as jnp
        import numpy as np
        B, S, H = (2, 256, 256)
        E, F = (16, 128)
        G, TOPK_G, TOPK = (4, 2, 4)
        N_SHARED = 2
        ROUTE_SCALE = 1.0
        FS = N_SHARED * F

        def _gate(x, w_gate):
            T = x.shape[0]
            scores = jax.nn.sigmoid(x @ w_gate.T)
            sv = scores.reshape(T, G, E // G)
            group_scores = jax.lax.top_k(sv, 2)[0].sum(-1)
            top_groups = jax.lax.top_k(group_scores, TOPK_G)[1]
            allowed = jnp.zeros((T, G), dtype=bool).at[jnp.arange(T)[:, None], top_groups].set(True)
            masked = jnp.where(allowed[:, :, None], sv, -jnp.inf).reshape(T, E)
            _, idx = jax.lax.top_k(masked, TOPK)
            w = jnp.take_along_axis(scores, idx, axis=1)
            w = w / (w.sum(-1, keepdims=True) + 1e-06) * ROUTE_SCALE
            return (w, idx)

        def _swiglu(x, w1, w3, w2):
            return jax.nn.silu(x @ w1.T) * (x @ w3.T) @ w2.T
        shape = hidden_states.shape
        x = hidden_states.reshape(-1, H)
        weights, idx = _gate(x, w_gate)
        combine = (jax.nn.one_hot(idx, E, dtype=x.dtype) * weights[..., None]).sum(1)
        g = jax.nn.silu(jnp.einsum('th,efh->tef', x, w1_e))
        u = jnp.einsum('th,efh->tef', x, w3_e)
        routed = jnp.einsum('tef,ehf,te->th', g * u, w2_e, combine)
        shared = _swiglu(x, w1_s, w3_s, w2_s)
        return (routed + shared).reshape(shape)
    h = _L0_tok_ref(x, _lenS, L0_tok_embed, L0_tok_ln1_g, L0_tok_ln1_b, L0_tok_ln2_g, L0_tok_ln2_b, L0_tok_W1, L0_tok_b1, L0_tok_W2, L0_tok_b2)
    h = h + _L0_attn_ref(_layernorm(h, axis=-1), L0_attn_Wq, L0_attn_bq, L0_attn_Wk, L0_attn_bk, L0_attn_Wv, L0_attn_bv, L0_attn_Wo, L0_attn_bo)
    h = h + _L0_ffn_ref(_layernorm(h, axis=-1), L0_ffn_w_gate, L0_ffn_w1_e, L0_ffn_w3_e, L0_ffn_w2_e, L0_ffn_w1_s, L0_ffn_w3_s, L0_ffn_w2_s)
    return h

_drawn_inputs = setup_inputs


def setup_inputs(seed=0):
    import zlib

    import numpy as np

    out = dict(_drawn_inputs(seed))
    spreads = {'L0_tok_ln1_g': (1.0, 0.2),
     'L0_tok_ln1_b': (0.0, 0.1),
     'L0_tok_ln2_g': (1.0, 0.2),
     'L0_tok_ln2_b': (0.0, 0.1),
     'L0_tok_b1': (0.0, 0.1),
     'L0_tok_b2': (0.0, 0.1),
     'L0_attn_bq': (0.0, 0.8),
     'L0_attn_bk': (0.0, 0.8),
     'L0_attn_bv': (0.0, 0.1),
     'L0_attn_bo': (0.0, 0.1)}
    factors = {'L0_attn_Wq': 8.0,
     'L0_attn_Wk': 8.0,
     'L0_ffn_w_gate': 8.0,
     'L0_ffn_w1_e': 8.0,
     'L0_ffn_w3_e': 8.0,
     'L0_ffn_w2_e': 8.0,
     'L0_ffn_w1_s': 3.796,
     'L0_ffn_w3_s': 3.509,
     'L0_ffn_w2_s': 3.67}
    for name, (base, spread) in spreads.items():
        noise = np.random.default_rng([zlib.crc32(name.encode()), seed]).standard_normal(out[name].shape)
        drawn = base * np.exp(spread * noise) if base else spread * noise
        out[name] = jnp.asarray(drawn.astype(out[name].dtype))
    for name, factor in factors.items():
        out[name] = (out[name] * factor).astype(out[name].dtype)
    return out
```

```python
from contextlib import ExitStack

import numpy as np
import concourse.bass as bass
from concourse import mybir

F32 = mybir.dt.float32
F32R = mybir.dt.float32r
I32 = mybir.dt.int32
U32 = mybir.dt.uint32
ALU = mybir.AluOpType
ACT = mybir.ActivationFunctionType
AX_X = mybir.AxisListType.X

P = 128
LAYERS, D, DF, V = 6, 256, 1024, 8000
BATCH, T = 8, 512
TT = T // P
KD = D // P
KF = DF // P
EPS = 1e-5


def passes(pe, out, a, b, first=True, last=True):
    pe.matmul(out, a[1], b[0], start=first, stop=False)
    pe.matmul(out, a[0], b[1], start=False, stop=False)
    return pe.matmul(out, a[0], b[0], start=False, stop=last)


def encoder(nc, ins, state, hidden):
    ctx = ExitStack()
    with ctx:
        def sb(name, shape, dt=F32):
            return ctx.enter_context(nc.sbuf_tensor(name, shape, dt))

        def sem(name):
            return ctx.enter_context(nc.semaphore(name))

        ident = sb("ident", [P, P])
        pos = sb("pos", [P, TT, D])
        ids = sb("ids", [P, BATCH * TT], I32)
        neg = sb("neg", [P, BATCH * TT], I32)
        rows = sb("rows", [P, BATCH * TT], U32)
        emb = sb("emb", [P, 4, D])
        hraw = [sb(f"hraw{i}", [P, TT, D]) for i in range(2)]
        v_hi, v_lo = sb("v_hi", [P, TT, D], F32R), sb("v_lo", [P, TT, D], F32R)
        hT_hi, hT_lo = sb("hT_hi", [P, KD, T], F32R), sb("hT_lo", [P, KD, T], F32R)
        probs = [sb(f"probs{i}", [P, T]) for i in range(2)]
        pT_hi = [sb(f"pT_hi{i}", [P, TT, P], F32R) for i in range(2)]
        pT_lo = [sb(f"pT_lo{i}", [P, TT, P], F32R) for i in range(2)]
        h1 = [sb(f"h1_{i}", [P, TT, D]) for i in range(2)]
        h1b = sb("h1b", [P, TT, D])
        h1T_hi, h1T_lo = sb("h1T_hi", [P, KD, T], F32R), sb("h1T_lo", [P, KD, T], F32R)
        x1, x2 = sb("x1", [P, 2, D]), sb("x2", [P, 2, D])
        hid = [sb(f"hid{i}", [P, T]) for i in range(2)]
        hid_hi, hid_lo = sb("hid_hi", [P, KF, T], F32R), sb("hid_lo", [P, KF, T], F32R)
        w1_raw, w2_raw = sb("w1_raw", [P, KD, DF]), sb("w2_raw", [P, KF, D])
        w1_hi, w1_lo = sb("w1_hi", [P, KD, DF], F32R), sb("w1_lo", [P, KD, DF], F32R)
        w2_hi, w2_lo = sb("w2_hi", [P, KF, D], F32R), sb("w2_lo", [P, KF, D], F32R)
        g1, be1 = sb("g1", [P, D]), sb("be1", [P, D])
        g2, be2, b2 = sb("g2", [P, D]), sb("be2", [P, D]), sb("b2", [P, D])
        b1 = sb("b1", [P, KF])
        negmax, rowsum, rinv = sb("negmax", [P, TT]), sb("rowsum", [P, TT]), sb("rinv", [P, TT])
        st1, mv1, ve1, rs1 = sb("st1", [P, TT, 6]), sb("mv1", [P, TT, 2]), sb("ve1", [P, TT]), sb("rs1", [P, TT])
        st2, mv2, ve2, rs2 = sb("st2", [P, TT, 6]), sb("mv2", [P, TT, 2]), sb("ve2", [P, TT]), sb("rs2", [P, TT])
        minus_half = sb("minus_half", [P, 1])

        ps_s = [ctx.enter_context(nc.psum_tensor(f"ps_s{i}", [P, T], F32)) for i in range(2)]
        ps_pT = ctx.enter_context(nc.psum_tensor("ps_pT", [P, TT, P], F32))
        ps_mha = ctx.enter_context(nc.psum_tensor("ps_mha", [P, D], F32))
        ps_hid = [ctx.enter_context(nc.psum_tensor(f"ps_hid{i}", [P, T], F32)) for i in range(2)]
        ps_ff0 = ctx.enter_context(nc.psum_tensor("ps_ff0", [P, D], F32))
        ps_h1T = ctx.enter_context(nc.psum_tensor("ps_h1T", [P, KD, 2, P], F32))
        ps_hT = [ps_s[j][:, :].rearrange("p (k i t) -> p k i t", k=KD, i=2) for j in range(2)]
        ps_ff = [ps_ff0[:, :], ps_hid[1][:, 0:D]]

        consts_in, ids_in = sem("consts_in"), sem("ids_in")
        h_stored = sem("h_stored")
        h_in = [sem("h_in0"), sem("h_in1")]
        w1_in, w2_in = sem("w1_in"), sem("w2_in")
        ln1_in, ln2_in, b1_in = sem("ln1_in"), sem("ln2_in"), sem("b1_in")
        gathered = [sem(f"gathered{i}") for i in range(4)]
        rows_step, rows_ready, half_ready = sem("rows_step"), sem("rows_ready"), sem("half_ready")
        first_ready, state_ready = sem("first_ready"), sem("state_ready")
        hT_ps, hT_hi_ready, hT_lo_ready = sem("hT_ps"), sem("hT_hi_ready"), sem("hT_lo_ready")
        v_hi_ready, v_lo_ready = sem("v_hi_ready"), sem("v_lo_ready")
        scores, negmax_ready, probs_ready = sem("scores"), sem("negmax_ready"), sem("probs_ready")
        pT_ps, pT_hi_ready, pT_lo_ready = sem("pT_ps"), sem("pT_hi_ready"), sem("pT_lo_ready")
        mha_ps, rinv_ready, x1_ready, st1_ready = sem("mha_ps"), sem("rinv_ready"), sem("x1_ready"), sem("st1_ready")
        mv1_ready, ve1_ready, rs1_ready = sem("mv1_ready"), sem("ve1_ready"), sem("rs1_ready")
        n1_ready, h1_ready = sem("n1_ready"), sem("h1_ready")
        h1T_ps, h1T_hi_ready, h1T_lo_ready = sem("h1T_ps"), sem("h1T_hi_ready"), sem("h1T_lo_ready")
        h1b_ready = sem("h1b_ready")
        hid_ps, hid_ready, hid_hi_ready, hid_lo_ready = sem("hid_ps"), sem("hid_ready"), sem("hid_hi_ready"), sem("hid_lo_ready")
        ff_ps, x2_ready, st2_ready = sem("ff_ps"), sem("x2_ready"), sem("st2_ready")
        mv2_ready, ve2_ready, rs2_ready, n2_ready = sem("mv2_ready"), sem("ve2_ready"), sem("rs2_ready"), sem("n2_ready")
        w1_hi_ready, w1_lo_ready = sem("w1_hi_ready"), sem("w1_lo_ready")
        w2_hi_ready, w2_lo_ready = sem("w2_hi_ready"), sem("w2_lo_ready")

        def schedule(eng, start, step, split):
            start()
            step(0, 0, 0, 1, 0, 0, 1, ffn=False)

            def six_steps(l):
                with eng.Fori(0, 3) as p:
                    step(8 * l + 2 * p + 1, 32 * l + 8 * p + 4, 1, 2 * p + 2, l, l, 4 * l + p + 2)
                    step(8 * l + 2 * p + 2, 32 * l + 8 * p + 8, 0, 2 * p + 3, l, l, 4 * l + p + 2)

            with eng.Fori(0, LAYERS - 1) as l:
                six_steps(l)
                step(8 * l + 7, 32 * l + 28, 1, 0, l, l, 4 * l + 5)
                step(8 * l + 8, 32 * l + 32, 0, 1, l + 1, l, 4 * l + 5, layer_end=True)
                split(8 * l + 8, 32 * l + 32, l + 1)
            l = LAYERS - 1
            six_steps(l)
            step(8 * l + 7, 32 * l + 28, 1, 0, l, l, None, prep=False)
            step(8 * l + 8, 32 * l + 32, 0, 1, l, l, None, attn=False, prep=False)

        def wait(eng, s, value):
            if not isinstance(value, int) or value > 0:
                eng.wait_ge(s, value)

        block = ctx.enter_context(nc.Block())

        @block.sync
        def _(sp):
            def vectors(l, which):
                if which == 1:
                    pairs, s = ((g1, "ln1_g"), (be1, "ln1_b")), ln1_in
                else:
                    pairs, s = ((g2, "ln2_g"), (be2, "ln2_b"), (b2, "b2")), ln2_in
                for dst, name in pairs:
                    sp.dma_start(dst[:, :], ins[name][bass.ds(l, 1), :].broadcast_to([P, D])).then_inc(s, 16)

            def bias1(l):
                sp.dma_start(b1[:, :], ins["b1"][bass.ds(l, 1), :, :].rearrange("l p f -> (l p) f")).then_inc(b1_in, 16)

            def weights(l):
                sp.dma_start(w1_raw[:, :, :], ins["w1"][bass.ds(l, 1), :, :].rearrange("l (k p) f -> p (l k) f", p=P)).then_inc(w1_in, 16)
                sp.dma_start(w2_raw[:, :, :], ins["w2"][bass.ds(l, 1), :, :].rearrange("l (k p) f -> p (l k) f", p=P)).then_inc(w2_in, 16)

            def load_h(t, par, b):
                if isinstance(t, int) and t <= 0:
                    sp.wait_ge(first_ready, t + 8)
                else:
                    sp.wait_ge(state_ready, t)
                wait(sp, x1_ready, t)
                sp.dma_start(hraw[1 - par][:, :, :], state[:, bass.ds(b, 1), :, :].rearrange("p b t d -> p (b t) d")).then_inc(h_in[1 - par], 16)

            def start():
                sp.dma_start(ids[:, :], ins["x"]).then_inc(ids_in, 16)
                sp.dma_start(pos[:, :, :], ins["pos"].rearrange("(t p) d -> p t d", p=P)).then_inc(consts_in, 16)
                sp.dma_start(ident[:, :], ins["ident"]).then_inc(consts_in, 16)
                weights(0)
                vectors(0, 1)
                vectors(0, 2)
                bias1(0)
                load_h(-4, 1, 0)

            start()
            load_h(0, 0, 1)
            with sp.Fori(1, LAYERS) as l:
                t0 = (l - 1) * 32
                sp.wait_ge(w1_hi_ready, l)
                sp.wait_ge(w1_lo_ready, l)
                sp.wait_ge(w2_hi_ready, l)
                sp.wait_ge(w2_lo_ready, l)
                weights(l)
                with sp.Fori(0, 3) as p:
                    load_h(t0 + 8 * p + 4, 1, 2 * p + 2)
                    load_h(t0 + 8 * p + 8, 0, 2 * p + 3)
                load_h(t0 + 28, 1, 0)
                sp.wait_ge(h1_ready, t0 + 32)
                vectors(l, 1)
                load_h(t0 + 32, 0, 1)
                sp.wait_ge(hid_ready, t0 * 2 + 64)
                bias1(l)
                sp.wait_ge(state_ready, t0 + 56)
                vectors(l, 2)
            t0 = (LAYERS - 1) * 32
            with sp.Fori(0, 3) as p:
                load_h(t0 + 8 * p + 4, 1, 2 * p + 2)
                load_h(t0 + 8 * p + 8, 0, 2 * p + 3)
            with sp.Fori(0, BATCH) as b:
                sp.wait_ge(state_ready, t0 + 28 + 4 * b)
                sp.dma_start(hidden[bass.ds(b, 1), :, :, :].rearrange("b p t d -> p (b t) d"), state[:, bass.ds(b, 1), :, :].rearrange("p b t d -> p (b t) d")).then_inc(h_stored, 16)
            sp.wait_ge(h_stored, 16 * BATCH)

        @block.gpsimd
        def _(pool):
            def added(n):
                pool.wait_ge(first_ready if n <= 8 else state_ready, n if n <= 8 else n - 8)

            def embed():
                pool.memset(minus_half[:, :], -0.5).then_inc(half_ready, 1)
                pool.wait_ge(rows_ready, 1)
                pool.wait_ge(consts_in, 32)
                for i in range(BATCH * TT + 3):
                    if i < BATCH * TT:
                        if i >= 4:
                            added(i - 3)
                        pool.indirect_dma_start(
                            out=emb[:, i % 4, :], out_offset=None, in_=ins["embed"],
                            in_offset=bass.IndirectOffsetOnAxis(ap=rows[:, i:i + 1], axis=0)).then_inc(gathered[i % 4], 16)
                    if i >= 3:
                        j = i - 3
                        pool.wait_ge(gathered[j % 4], 16 * (j // 4 + 1))
                        pool.tensor_tensor(state[:, j // TT, j % TT, :], emb[:, j % 4, :], pos[:, j % TT, :], ALU.add).then_inc(first_ready if j < 8 else state_ready, 1)

            def v_low(u, t, par, n):
                wait(pool, mha_ps, t + 4)
                pool.wait_ge(v_hi_ready, u + 2)
                pool.tensor_tensor(v_lo[:, :, :], hraw[1 - par][:, :, :], v_hi[:, :, :].bitcast(F32), ALU.subtract).then_inc(v_lo_ready, 1)

            def add_bias2(u, t, par, lf):
                pool.wait_ge(h1_ready, t)
                pool.wait_ge(ln2_in, (lf + 1) * 48)
                wait(pool, x2_ready, t - 4)
                pool.tensor_tensor(h1b[:, :, :], h1[1 - par][:, :, :], b2[:, :].unsqueeze(1).broadcast_to([P, TT, D]), ALU.add).then_inc(h1b_ready, 1)

            def hid_low(t, f):
                pool.wait_ge(hid_hi_ready, 2 * t - 8 + f + 1)
                if f == 0:
                    wait(pool, ff_ps, t - 4)
                pool.tensor_tensor(hid_lo[:, f, :], hid[f % 2][:, :], hid_hi[:, f, :].bitcast(F32), ALU.subtract).then_inc(hid_lo_ready, 1)

            def rstd1(t, i):
                pool.wait_ge(ve1_ready, t + i + 1)
                pool.tensor_tensor(rs1[:, i:i + 1], ve1[:, i:i + 1], minus_half[:, :], ALU.pow).then_inc(rs1_ready, 1)

            def rstd2(t, i):
                pool.wait_ge(ve2_ready, t - 4 + i + 1)
                pool.tensor_tensor(rs2[:, i:i + 1], ve2[:, i:i + 1], minus_half[:, :], ALU.pow).then_inc(rs2_ready, 1)

            def step(u, t, par, b, la, lf, n, attn=True, ffn=True, prep=True, layer_end=False):
                for i in range(TT):
                    if ffn:
                        hid_low(t, 2 * i)
                        hid_low(t, 2 * i + 1)
                    if ffn and i == 1:
                        add_bias2(u, t, par, lf)
                    if attn and i >= 1:
                        rstd1(t, i - 1)
                if attn:
                    rstd1(t, 3)
                if prep:
                    v_low(u, t, par, n)
                if ffn:
                    for i in range(TT):
                        rstd2(t, i)

            def start():
                embed()
                pool.wait_ge(half_ready, 1)
                v_low(-1, -4, 1, 1)

            schedule(pool, start, step, lambda u, t, l: None)

        @block.scalar
        def _(act):
            def relu(t, f, lf):
                act.wait_ge(hid_ps, 2 * t - 8 + f + 1)
                wait(act, hid_lo_ready, 2 * t - 8 + max(f - 1, 0))
                if f == 0:
                    act.wait_ge(b1_in, (lf + 1) * 16)
                act.activation(hid[f % 2][:, :], ps_hid[f % 2][:, :], ACT.Relu, bias=b1[:, f:f + 1]).then_inc(hid_ready, 1)
                if f == 0:
                    wait(act, ff_ps, t - 4)
                act.wait_ge(hid_ready, 2 * t - 8 + f + 1)
                act.activation(hid_hi[:, f, :], hid[f % 2][:, :], ACT.Copy).then_inc(hid_hi_ready, 1)

            def exp(t, i):
                act.wait_ge(negmax_ready, t + i + 1)
                wait(act, pT_ps, t + i - 1)
                act.activation(probs[i % 2][:, :], ps_s[i % 2][:, :], ACT.Exp, bias=negmax[:, i:i + 1],
                               accum_out=rowsum[:, i:i + 1]).then_inc(probs_ready, 1)

            def pT_high(t, i):
                act.wait_ge(pT_ps, t + i + 1)
                wait(act, mha_ps, t + i - 1)
                act.activation(pT_hi[i % 2][:, :, :], ps_pT[:, :, :], ACT.Copy).then_inc(pT_hi_ready, 1)

            def h1T_high(u, j):
                act.wait_ge(h1T_ps, 2 * u + j + 1)
                wait(act, hid_ps, 8 * u)
                act.activation(h1T_hi[:, :, 2 * j * P:(2 * j + 2) * P], ps_h1T[:, :, :, :].rearrange("p k i t -> p k (i t)"), ACT.Copy).then_inc(h1T_hi_ready, 1)

            def hT_high(u, t, j):
                act.wait_ge(hT_ps, 2 * u + 2 + j + 1)
                wait(act, scores, t + 4)
                act.activation(hT_hi[:, :, 2 * j * P:(2 * j + 2) * P], ps_hT[j].rearrange("p k i t -> p k (i t)"), ACT.Copy, scale=0.25).then_inc(hT_hi_ready, 1)

            def v_high(u, t, par, n):
                act.wait_ge(h_in[1 - par], 16 * n)
                wait(act, mha_ps, t + 4)
                act.activation(v_hi[:, :, :], hraw[1 - par][:, :, :], ACT.Copy).then_inc(v_hi_ready, 1)

            def split_w1(l):
                act.wait_ge(w1_in, 16 * l + 16)
                act.activation(w1_hi[:, :, :], w1_raw[:, :, :], ACT.Copy).then_inc(w1_hi_ready, 1)

            def split_w2(l):
                act.wait_ge(w2_in, 16 * l + 16)
                act.activation(w2_hi[:, :, :], w2_raw[:, :, :], ACT.Copy).then_inc(w2_hi_ready, 1)

            def step(u, t, par, b, la, lf, n, attn=True, ffn=True, prep=True, layer_end=False):
                for i in range(TT):
                    if attn:
                        if i >= 1:
                            pT_high(t, i - 1)
                        exp(t, i)
                    if ffn:
                        relu(t, 2 * i, lf)
                        relu(t, 2 * i + 1, lf)
                if attn:
                    pT_high(t, 3)
                if layer_end:
                    act.wait_ge(hid_ps, 2 * t)
                    split_w1(lf + 1)
                if attn:
                    h1T_high(u, 0)
                if prep:
                    v_high(u, t, par, n)
                    hT_high(u, t, 0)
                    hT_high(u, t, 1)
                if attn:
                    h1T_high(u, 1)

            def start():
                split_w1(0)
                split_w2(0)
                v_high(-1, -4, 1, 1)
                for j in range(2):
                    hT_high(-1, -4, j)

            def split(u, t, l):
                act.wait_ge(ff_ps, t)
                split_w2(l)

            schedule(act, start, step, split)

        @block.vector
        def _(dve):
            def neg_max(t, i):
                dve.wait_ge(scores, t + i + 1)
                wait(dve, probs_ready, t + i - 3)
                dve.tensor_reduce(negmax[:, i:i + 1], ps_s[i % 2][:, :], AX_X, ALU.max, negate=True).then_inc(negmax_ready, 1)

            def pT_low(t, i):
                dve.wait_ge(pT_hi_ready, t + i + 1)
                wait(dve, mha_ps, t + i - 1)
                dve.tensor_tensor(pT_lo[i % 2][:, :, :], ps_pT[:, :, :], pT_hi[i % 2][:, :, :].bitcast(F32), ALU.subtract).then_inc(pT_lo_ready, 1)

            def residual1(t, par, i):
                dve.wait_ge(probs_ready, t + i + 1)
                dve.reciprocal(rinv[:, i:i + 1], rowsum[:, i:i + 1]).then_inc(rinv_ready, 1)
                dve.wait_ge(mha_ps, t + i + 1)
                dve.wait_ge(rinv_ready, t + i + 1)
                dve.scalar_tensor_tensor(out=x1[:, i % 2, :], in0=ps_mha[:, :], scalar=rinv[:, i:i + 1],
                                         in1=hraw[par][:, i, :], op0=ALU.mult, op1=ALU.add).then_inc(x1_ready, 1)
                dve.wait_ge(x1_ready, t + i + 1)
                dve.bn_stats(st1[:, i, :], x1[:, i % 2, :]).then_inc(st1_ready, 1)
                dve.wait_ge(st1_ready, t + i + 1)
                dve.memset(ve1[:, i:i + 1], EPS)
                dve.bn_aggr(mv1[:, i, :], st1[:, i, :]).then_inc(mv1_ready, 1)
                dve.wait_ge(mv1_ready, t + i + 1)
                dve.tensor_tensor(ve1[:, i:i + 1], mv1[:, i, 1:2], ve1[:, i:i + 1], ALU.add).then_inc(ve1_ready, 1)

            def norm1(t, par, i, la):
                if i == 0:
                    dve.wait_ge(ln1_in, (la + 1) * 32)
                dve.scalar_tensor_tensor(out=x1[:, i % 2, :], in0=x1[:, i % 2, :], scalar=mv1[:, i, 0:1],
                                         in1=g1[:, :], op0=ALU.subtract, op1=ALU.mult).then_inc(n1_ready, 1)
                dve.wait_ge(n1_ready, t + i + 1)
                dve.wait_ge(rs1_ready, t + i + 1)
                dve.scalar_tensor_tensor(out=h1[par][:, i, :], in0=x1[:, i % 2, :], scalar=rs1[:, i:i + 1],
                                         in1=be1[:, :], op0=ALU.mult, op1=ALU.add).then_inc(h1_ready, 1)

            def h1T_low(u, j):
                dve.wait_ge(h1T_hi_ready, 2 * u + j + 1)
                sl = slice(2 * j * P, (2 * j + 2) * P)
                dve.tensor_tensor(h1T_lo[:, :, sl], ps_h1T[:, :, :, :].rearrange("p k i t -> p k (i t)"), h1T_hi[:, :, sl].bitcast(F32), ALU.subtract).then_inc(h1T_lo_ready, 1)

            def hT_low(u, j):
                dve.wait_ge(hT_hi_ready, 2 * u + 2 + j + 1)
                sl = slice(2 * j * P, (2 * j + 2) * P)
                dve.scalar_tensor_tensor(out=hT_lo[:, :, sl], in0=ps_hT[j].rearrange("p k i t -> p k (i t)"), scalar=0.25,
                                         in1=hT_hi[:, :, sl].bitcast(F32), op0=ALU.mult, op1=ALU.subtract).then_inc(hT_lo_ready, 1)

            def residual2(u, t, i):
                n = t - 4 + i + 1
                dve.wait_ge(ff_ps, n)
                if i == 0:
                    dve.wait_ge(h1b_ready, u)
                dve.tensor_tensor(x2[:, i % 2, :], ps_ff[i % 2], h1b[:, i, :], ALU.add).then_inc(x2_ready, 1)
                dve.wait_ge(x2_ready, n)
                dve.bn_stats(st2[:, i, :], x2[:, i % 2, :]).then_inc(st2_ready, 1)
                dve.wait_ge(st2_ready, n)
                dve.memset(ve2[:, i:i + 1], EPS)
                dve.bn_aggr(mv2[:, i, :], st2[:, i, :]).then_inc(mv2_ready, 1)
                dve.wait_ge(mv2_ready, n)
                dve.tensor_tensor(ve2[:, i:i + 1], mv2[:, i, 1:2], ve2[:, i:i + 1], ALU.add).then_inc(ve2_ready, 1)

            def norm2(t, b, i, lf):
                n = t - 4 + i + 1
                if i == 0:
                    dve.wait_ge(ln2_in, (lf + 1) * 48)
                dve.scalar_tensor_tensor(out=x2[:, i % 2, :], in0=x2[:, i % 2, :], scalar=mv2[:, i, 0:1],
                                         in1=g2[:, :], op0=ALU.subtract, op1=ALU.mult).then_inc(n2_ready, 1)
                dve.wait_ge(n2_ready, n)
                dve.wait_ge(rs2_ready, n)
                at = (b + 6) % 8 if isinstance(b, int) else b - 2
                dve.scalar_tensor_tensor(out=state[:, bass.ds(at, 1), i, :].rearrange("p b d -> p (b d)"), in0=x2[:, i % 2, :],
                                         scalar=rs2[:, i:i + 1], in1=be2[:, :], op0=ALU.mult, op1=ALU.add).then_inc(state_ready, 1)

            def split_w1(l):
                dve.wait_ge(w1_hi_ready, l + 1)
                dve.tensor_tensor(w1_lo[:, :, :], w1_raw[:, :, :], w1_hi[:, :, :].bitcast(F32), ALU.subtract).then_inc(w1_lo_ready, 1)

            def split_w2(l):
                dve.wait_ge(w2_hi_ready, l + 1)
                dve.tensor_tensor(w2_lo[:, :, :], w2_raw[:, :, :], w2_hi[:, :, :].bitcast(F32), ALU.subtract).then_inc(w2_lo_ready, 1)

            def start():
                dve.wait_ge(ids_in, 16)
                dve.tensor_scalar(neg[:, :], ids[:, :], 0, V, ALU.is_lt, ALU.mult).then_inc(rows_step, 1)
                dve.wait_ge(rows_step, 1)
                dve.tensor_tensor(ids[:, :], ids[:, :], neg[:, :], ALU.add).then_inc(rows_step, 1)
                dve.wait_ge(rows_step, 2)
                dve.tensor_scalar(rows[:, :], ids[:, :], 0, V - 1, ALU.max, ALU.min).then_inc(rows_ready, 1)
                split_w1(0)
                split_w2(0)
                for j in range(2):
                    hT_low(-1, j)

            def step(u, t, par, b, la, lf, n, attn=True, ffn=True, prep=True, layer_end=False):
                if attn:
                    neg_max(t, 0)
                    neg_max(t, 1)
                    pT_low(t, 0)
                    residual1(t, par, 0)
                    neg_max(t, 2)
                    pT_low(t, 1)
                    residual1(t, par, 1)
                    neg_max(t, 3)
                    norm1(t, par, 0, la)
                    pT_low(t, 2)
                    norm1(t, par, 1, la)
                    residual1(t, par, 2)
                    pT_low(t, 3)
                    norm1(t, par, 2, la)
                    h1T_low(u, 0)
                    residual1(t, par, 3)
                    norm1(t, par, 3, la)
                if layer_end:
                    split_w1(lf + 1)
                if prep:
                    hT_low(u, 0)
                if ffn:
                    residual2(u, t, 0)
                    norm2(t, b, 0, lf)
                if prep:
                    hT_low(u, 1)
                if ffn:
                    residual2(u, t, 1)
                    norm2(t, b, 1, lf)
                if attn:
                    h1T_low(u, 1)
                if ffn:
                    residual2(u, t, 2)
                    norm2(t, b, 2, lf)
                    residual2(u, t, 3)
                    norm2(t, b, 3, lf)

            schedule(dve, start, step, lambda u, t, l: split_w2(l))

        @block.tensor
        def _(pe):
            def tile_of(i):
                return slice(i * P, (i + 1) * P)

            def score(u, t, i):
                if i == 0:
                    pe.wait_ge(hT_lo_ready, 2 * u + 2)
                    pe.wait_ge(hT_hi_ready, 2 * u + 2)
                wait(pe, probs_ready, t + i - 1)
                for k in range(KD):
                    m = passes(pe, ps_s[i % 2][:, :], (hT_hi[:, k, tile_of(i)], hT_lo[:, k, tile_of(i)]),
                               (hT_hi[:, k, :], hT_lo[:, k, :]), k == 0, k == KD - 1)
                m.then_inc(scores, 1)

            def turn_probs(t, i):
                pe.wait_ge(probs_ready, t + i + 1)
                wait(pe, pT_lo_ready, t + i)
                for c in range(TT):
                    m = pe.transpose(ps_pT[:, c, :], probs[i % 2][:, tile_of(c)], ident[:, :])
                m.then_inc(pT_ps, 1)

            def mix(u, t, i):
                if i == 0:
                    pe.wait_ge(v_lo_ready, u + 1)
                    pe.wait_ge(v_hi_ready, u + 1)
                pe.wait_ge(pT_lo_ready, t + i + 1)
                wait(pe, x1_ready, t + i)
                for c in range(TT):
                    m = passes(pe, ps_mha[:, :], (pT_hi[i % 2][:, c, :], pT_lo[i % 2][:, c, :]),
                               (v_hi[:, c, :], v_lo[:, c, :]), c == 0, c == TT - 1)
                m.then_inc(mha_ps, 1)

            def turn(src, j, bank):
                for k in range(KD):
                    for i in range(2):
                        m = pe.transpose(bank[:, k, i, :], src[:, 2 * j + i, k * P:(k + 1) * P], ident[:, :])
                return m

            def turn_h1(u, t, par, j):
                pe.wait_ge(h1_ready, t + 2 * j + 2)
                wait(pe, h1T_lo_ready, 2 * u + j)
                turn(h1[par], j, ps_h1T).then_inc(h1T_ps, 1)

            def turn_h(u, t, par, j, n):
                pe.wait_ge(h_in[1 - par], 16 * n)
                wait(pe, probs_ready, t + 4)
                turn(hraw[1 - par], j, ps_hT[j]).then_inc(hT_ps, 1)

            def up(u, t, f, lf):
                if f == 0:
                    pe.wait_ge(h1T_lo_ready, 2 * u)
                    pe.wait_ge(w1_lo_ready, lf + 1)
                if f == 1:
                    wait(pe, x2_ready, t - 4)
                wait(pe, hid_ready, 2 * t - 8 + max(f - 1, 0))
                for k in range(KD):
                    m = passes(pe, ps_hid[f % 2][:, :], (w1_hi[:, k, tile_of(f)], w1_lo[:, k, tile_of(f)]),
                               (h1T_hi[:, k, :], h1T_lo[:, k, :]), k == 0, k == KD - 1)
                m.then_inc(hid_ps, 1)

            def down(t, i, lf):
                if i == 0:
                    pe.wait_ge(hid_lo_ready, 2 * t)
                    pe.wait_ge(w2_lo_ready, lf + 1)
                wait(pe, x2_ready, t - 4 + max(i - 1, 0))
                for f in range(KF):
                    m = passes(pe, ps_ff[i % 2], (hid_hi[:, f, tile_of(i)], hid_lo[:, f, tile_of(i)]),
                               (w2_hi[:, f, :], w2_lo[:, f, :]), f == 0, f == KF - 1)
                m.then_inc(ff_ps, 1)

            def step(u, t, par, b, la, lf, n, attn=True, ffn=True, prep=True, layer_end=False):
                if attn:
                    score(u, t, 0)
                if ffn:
                    up(u, t, 0, lf)
                    up(u, t, 1, lf)
                if attn:
                    score(u, t, 1)
                    turn_probs(t, 0)
                if ffn:
                    up(u, t, 2, lf)
                    up(u, t, 3, lf)
                if attn:
                    mix(u, t, 0)
                    score(u, t, 2)
                    turn_probs(t, 1)
                if ffn:
                    up(u, t, 4, lf)
                    up(u, t, 5, lf)
                if attn:
                    mix(u, t, 1)
                    score(u, t, 3)
                    turn_probs(t, 2)
                if ffn:
                    up(u, t, 6, lf)
                    up(u, t, 7, lf)
                if attn:
                    mix(u, t, 2)
                    turn_probs(t, 3)
                    turn_h1(u, t, par, 0)
                if ffn:
                    down(t, 0, lf)
                if attn:
                    mix(u, t, 3)
                if prep:
                    turn_h(u, t, par, 0, n)
                if ffn:
                    down(t, 1, lf)
                if prep:
                    turn_h(u, t, par, 1, n)
                if ffn:
                    down(t, 2, lf)
                if attn:
                    turn_h1(u, t, par, 1)
                if ffn:
                    down(t, 3, lf)

            def start():
                pe.wait_ge(consts_in, 32)
                for j in range(2):
                    turn_h(-1, -4, 1, j, 1)

            schedule(pe, start, step, lambda u, t, l: None)


HEADS, HD, HALF = 16, 16, 32
HC = HEADS // KD
QB = 64
WIN = 2 * QB
NWIN = T // QB
UNITS = TT * KD
EXPERTS, GROUPS, TOP_GROUPS, TOP = 16, 4, 2, 4
SLOTS = EXPERTS + 2
HPC = 4
OC = HEADS // HPC
GATE_OPS = 25


def window(b):
    return min(max(QB * b - HALF, 0), T - WIN)


def experts(nc, ins, hidden, out):
    ctx = ExitStack()
    with ctx:
        def sb(name, shape, dt=F32):
            return ctx.enter_context(nc.sbuf_tensor("e_" + name, shape, dt))

        def sem(name):
            return ctx.enter_context(nc.semaphore("e_" + name))

        def pair(name, shape):
            return sb(name + "_hi", shape, F32R), sb(name + "_lo", shape, F32R)

        ident = sb("ident", [P, P])
        band = sb("band", [P, 3, P])
        hmask = sb("hmask", [P, HC])
        before4, before16 = sb("before4", [P, 4, 4]), sb("before16", [P, 16, 16])
        bq, bk = sb("bq", [P, KD]), sb("bk", [P, KD])
        bv, bo = sb("bv", [P, D]), sb("bo", [P, D])
        minus_half = sb("minus_half", [P, 1])
        wq, wk, wv = pair("wq", [P, KD, D]), pair("wk", [P, KD, D]), pair("wv", [P, KD, D])
        wo = pair("wo", [P, OC, D])
        wg = pair("wg", [P, KD, EXPERTS])
        w_raw = sb("w_raw", [P, SLOTS, 3 * D])
        w13 = [pair(f"w13_{i}", [P, 2 * D]) for i in range(2)]
        w2 = [pair(f"w2_{i}", [P, D]) for i in range(3)]
        x = sb("x", [P, TT, D])
        xT = pair("xT", [P, KD, T])
        qf, kf = sb("qf", [P, KD, T]), sb("kf", [P, KD, T])
        qm = [sb(f"qm{i}", [P, HC, P]) for i in range(2)]
        vw = sb("vw", [P, NWIN, D + HD])
        s = [sb(f"s{i}", [P, HC, P]) for i in range(2)]
        pT = sb("pT", [P, HC, P])
        oT = pair("oT", [P, OC, P])
        h2, y = sb("h2", [P, TT, D]), sb("y", [P, TT, D])
        yT = pair("yT", [P, KD, T])
        yT0 = pair("yT0", [P, KD, 2 * P])
        acc = sb("acc", [P, TT, D])
        th, act_f = sb("th", [P, T]), sb("act_f", [P, T])
        act = [pair(f"act{i}", [P, T]) for i in range(2)]
        negmax, rowsum, rinv = sb("negmax", [P, 2, HC]), sb("rowsum", [P, 2, HC]), sb("rinv", [P, 2, HC])
        st, mv, ve, rs = sb("st", [P, TT, 6]), sb("mv", [P, TT, 2]), sb("ve", [P, TT]), sb("rs", [P, TT])
        sty, mvy, vey, rsy = sb("sty", [P, TT, 6]), sb("mvy", [P, TT, 2]), sb("vey", [P, TT]), sb("rsy", [P, TT])
        g_e, g_s = sb("g_e", [P, 2, EXPERTS]), sb("g_s", [P, 2, EXPERTS])
        g_two, g_top = sb("g_two", [P, 2 * GROUPS, 6]), sb("g_top", [P, 2, GROUPS])
        g_a, g_b = sb("g_a", [P, 2, 16, 16]), sb("g_b", [P, 2, 16, 16])
        g_ok, g_okm, g_m = sb("g_ok", [P, 2 * GROUPS]), sb("g_okm", [P, 2 * GROUPS]), sb("g_m", [P, 2, EXPERTS])
        g_rank, g_sum, g_w = sb("g_rank", [P, 2, EXPERTS]), sb("g_sum", [P, 2]), sb("g_w", [P, 2, EXPERTS])
        weight = sb("weight", [P, TT, SLOTS])

        ps_s = ctx.enter_context(nc.psum_tensor("e_ps_s", [P, HC, P], F32))
        ps_p = ctx.enter_context(nc.psum_tensor("e_ps_p", [P, HC, P], F32))
        ps_g = ctx.enter_context(nc.psum_tensor("e_ps_g", [P, T], F32))
        ps_u = ctx.enter_context(nc.psum_tensor("e_ps_u", [P, T], F32))
        ps_y = ctx.enter_context(nc.psum_tensor("e_ps_y", [P, 2, D], F32))
        ps_x = ctx.enter_context(nc.psum_tensor("e_ps_x", [P, T], F32))
        ps_q, ps_k = (ps_s[:, 4 * n:4 * n + 4, :].rearrange("p a t -> p (a t)") for n in range(2))
        ps_xT = [ps_p[:, 4 * j:4 * j + 4, :].rearrange("p (k i) t -> p k (i t)", k=KD) for j in range(2)]
        ps_v = [ps_p[:, 4 * j:4 * j + 4, :].rearrange("p (w a) t -> p w (a t)", w=2) for j in range(2)]
        ps_o = ps_x[:, 0:2 * P].rearrange("p (c t) -> p c t", c=2)
        ps_yT = ps_x[:, :].rearrange("p (k t) -> p k t", k=KD)
        ps_gate = ps_x[:, 0:2 * EXPERTS].rearrange("p (i e) -> p i e", i=2)

        consts_in, attn_in, x_in, out_done = sem("consts_in"), sem("attn_in"), sem("x_in"), sem("out_done")
        w_in = [sem(f"w_in{g}") for g in range(3)]
        half_ready, zeros_ready, ones_ready = sem("half_ready"), sem("zeros_ready"), sem("ones_ready")
        attn_hi, attn_lo = sem("attn_hi"), sem("attn_lo")
        st_ready, mv_ready, ve_ready, rs_ready, x_ready = sem("st_ready"), sem("mv_ready"), sem("ve_ready"), sem("rs_ready"), sem("x_ready")
        hb_ready = sem("hb_ready")
        xT_ps, xT_hi, xT_lo = sem("xT_ps"), sem("xT_hi"), sem("xT_lo")
        q_ps, k_ps, q_ready, k_ready = sem("q_ps"), sem("k_ps"), sem("q_ready"), sem("k_ready")
        v_ps, v_ready = sem("v_ps"), sem("v_ready")
        qm_ready, scores, masked, negmax_ready = sem("qm_ready"), sem("scores"), sem("masked"), sem("negmax_ready")
        probs, rinv_ready, probs_ready = sem("probs"), sem("rinv_ready"), sem("probs_ready")
        pT_ps, pT_ready = sem("pT_ps"), sem("pT_ready")
        oT_ps, oT_hi, oT_lo = sem("oT_ps"), sem("oT_hi"), sem("oT_lo")
        wo_ps, h2_ready = sem("wo_ps"), sem("h2_ready")
        sty_ready, mvy_ready, vey_ready, rsy_ready, y_ready = sem("sty_ready"), sem("mvy_ready"), sem("vey_ready"), sem("rsy_ready"), sem("y_ready")
        yT_ps, yT_hi, yT_lo = sem("yT_ps"), sem("yT_hi"), sem("yT_lo")
        moved_hi, moved_lo = sem("moved_hi"), sem("moved_lo")
        gate_ps, gate_exp, gate_step = sem("gate_ps"), sem("gate_exp"), sem("gate_step")
        w13_hi, w13_lo, w2_hi, w2_lo = sem("w13_hi"), sem("w13_lo"), sem("w2_hi"), sem("w2_lo")
        g_ps, u_ps, tanh_ready, silu_ready, act_ready = sem("g_ps"), sem("u_ps"), sem("tanh_ready"), sem("silu_ready"), sem("act_ready")
        act_hi, act_lo = sem("act_hi"), sem("act_lo")
        y_ps, acc_ready = sem("y_ps"), sem("acc_ready")

        def wait(eng, sm, value):
            if not isinstance(value, int) or value > 0:
                eng.wait_ge(sm, value)

        def schedule(eng, slots, end):
            slots(0, -1, True, False)
            end(0, -1, True, False)
            with eng.Fori(0, BATCH - 1) as v:
                slots(v + 1, v, True, True)
                end(v + 1, v, True, True)
            slots(BATCH, BATCH - 1, False, True)
            end(BATCH, BATCH - 1, False, True)

        block = ctx.enter_context(nc.Block())

        @block.sync
        def _(sp):
            def load_x(w):
                sp.dma_start(x[:, :, :], hidden[bass.ds(w, 1), :, :, :].rearrange("b p t d -> p (b t) d")).then_inc(x_in, 16)

            load_x(0)
            for dst, name in ((ident[:, :], "ident"), (band[:, :, :], "band"), (hmask[:, :], "hmask"),
                              (before4[:, :, :], "before4"), (before16[:, :, :], "before16"),
                              (bq[:, :], "bq"), (bk[:, :], "bk"), (bv[:, :], "bv"), (bo[:, :], "bo")):
                src = ins[name] if name not in ("bv", "bo") else ins[name].broadcast_to([P, D])
                sp.dma_start(dst, src).then_inc(consts_in, 16)
            for dst, name in ((s[0][:, 0:4, :], "wq"), (s[0][:, 4:8, :], "wk"), (s[1][:, 0:4, :], "wv"),
                              (pT[:, :, :], "wo"), (s[1][:, 4, 0:2 * EXPERTS], "wg")):
                sp.dma_start(dst if name == "wg" else dst.rearrange("p a t -> p (a t)"), ins[name]).then_inc(attn_in, 16)
            for g in range(3):
                sp.dma_start(w_raw[:, 6 * g:6 * g + 6, :], ins["moe"][:, 6 * g:6 * g + 6, :]).then_inc(w_in[g], 16)
            with sp.Fori(0, BATCH - 1) as v:
                sp.wait_ge(hb_ready, v + 1)
                sp.wait_ge(xT_ps, 2 * v + 2)
                load_x(v + 1)
                sp.wait_ge(acc_ready, 72 * v + 72)
                sp.dma_start(out[bass.ds(v, 1), :, :].rearrange("b (t p) d -> p (b t) d", p=P), acc[:, :, :]).then_inc(out_done, 16)
            sp.wait_ge(acc_ready, 72 * BATCH)
            sp.dma_start(out[BATCH - 1, :, :].rearrange("(t p) d -> p t d", p=P), acc[:, :, :]).then_inc(out_done, 16)
            sp.wait_ge(out_done, 16 * BATCH)

        @block.gpsimd
        def _(pool):
            pool.memset(minus_half[:, :], -0.5).then_inc(half_ready, 1)
            pool.memset(vw[:, :, D:D + HD], 0.0).then_inc(zeros_ready, 1)
            pool.memset(weight[:, :, EXPERTS:SLOTS], 1.0).then_inc(ones_ready, 1)
            pool.wait_ge(half_ready, 1)

            def rstd(w, i):
                pool.wait_ge(ve_ready, 4 * w + i + 1)
                pool.tensor_tensor(rs[:, i:i + 1], ve[:, i:i + 1], minus_half[:, :], ALU.pow).then_inc(rs_ready, 1)

            def rstd_y(w, i):
                pool.wait_ge(vey_ready, 4 * w + i + 1)
                pool.tensor_tensor(rsy[:, i:i + 1], vey[:, i:i + 1], minus_half[:, :], ALU.pow).then_inc(rsy_ready, 1)

            def add_bo(w):
                if isinstance(w, int) and w == 0:
                    pool.wait_ge(x_in, 16)
                    pool.wait_ge(consts_in, 16 * 9)
                else:
                    pool.wait_ge(x_in, 16 * w + 16)
                    pool.wait_ge(acc_ready, 72 * w - 68)
                pool.tensor_tensor(h2[:, :, :], x[:, :, :], bo[:, :].unsqueeze(1).broadcast_to([P, TT, D]), ALU.add).then_inc(hb_ready, 1)

            def mask_q(w, n):
                i, c = n // 2, n % 2
                pool.wait_ge(q_ready, 2 * w + 2)
                wait(pool, scores, 8 * w + n - 1)
                pool.tensor_tensor(qm[n % 2][:, :, :], qf[:, c, i * P:(i + 1) * P].unsqueeze(1).broadcast_to([P, HC, P]),
                                   hmask[:, :].unsqueeze(2).broadcast_to([P, HC, P]), ALU.mult).then_inc(qm_ready, 1)

            def normalize(w, n):
                pool.wait_ge(rinv_ready, 8 * w + n + 1)
                pool.tensor_tensor(s[n % 2][:, :, :], s[n % 2][:, :, :], rinv[:, n % 2, :].unsqueeze(2).broadcast_to([P, HC, P]),
                                   ALU.mult).then_inc(probs_ready, 1)

            def w_low(v, e):
                hi, lo = w13[e % 2]
                pool.wait_ge(w13_hi, 18 * v + e + 1)
                pool.tensor_tensor(lo[:, :], w_raw[:, e, 0:2 * D], hi[:, :].bitcast(F32), ALU.subtract).then_inc(w13_lo, 1)
                hi, lo = w2[e % 3]
                pool.wait_ge(w2_hi, 18 * v + e + 1)
                pool.tensor_tensor(lo[:, :], w_raw[:, e, 2 * D:3 * D], hi[:, :].bitcast(F32), ALU.subtract).then_inc(w2_lo, 1)

            def slots(w, v, attn, moe):
                if moe:
                    w_low(v, 0)
                for k in range(SLOTS):
                    if moe and k + 1 < SLOTS:
                        w_low(v, k + 1)
                    if attn:
                        if k == 0:
                            for i in range(TT):
                                rstd(w, i)
                        if k == 2:
                            add_bo(w)
                        if 0 <= k - 4 < UNITS:
                            mask_q(w, k - 4)
                        if 0 <= k - 6 < UNITS:
                            normalize(w, k - 6)
                        if k in (10, 12, 14, 16):
                            rstd_y(w, (k - 10) // 2)

            schedule(pool, slots, lambda *a: None)

        @block.scalar
        def _(act_e):
            def split_attention():
                act_e.wait_ge(attn_in, 16 * 5)
                for (hi, _), src in ((wq, s[0][:, 0:4, :]), (wk, s[0][:, 4:8, :]), (wv, s[1][:, 0:4, :]), (wo, pT[:, :, :])):
                    act_e.activation(hi[:, :, :].rearrange("p a b -> p (a b)"), src.rearrange("p a b -> p (a b)"), ACT.Copy).then_inc(attn_hi, 1)
                act_e.activation(wg[0][:, :, :].rearrange("p a b -> p (a b)"), s[1][:, 4, 0:2 * EXPERTS], ACT.Copy).then_inc(attn_hi, 1)

            def w_high(v, e):
                act_e.wait_ge(w_in[e // 6], 16)
                wait(act_e, u_ps, 18 * v + max(e - 1, 0))
                act_e.activation(w13[e % 2][0][:, :], w_raw[:, e, 0:2 * D], ACT.Copy).then_inc(w13_hi, 1)
                wait(act_e, y_ps, 36 * v + max(2 * e - 4, 0))
                act_e.activation(w2[e % 3][0][:, :], w_raw[:, e, 2 * D:3 * D], ACT.Copy).then_inc(w2_hi, 1)

            def tanh(v, e):
                act_e.wait_ge(g_ps, 18 * v + e + 1)
                wait(act_e, act_ready, 18 * v + e)
                act_e.activation(th[:, :], ps_g[:, :], ACT.Tanh, scale=0.5).then_inc(tanh_ready, 1)

            def act_high(v, e):
                act_e.wait_ge(act_ready, 18 * v + e + 1)
                wait(act_e, y_ps, 36 * v + max(2 * e - 2, 0))
                act_e.activation(act[e % 2][0][:, :], act_f[:, :], ACT.Copy).then_inc(act_hi, 1)

            def xT_high(w, j):
                act_e.wait_ge(xT_ps, 2 * w + j + 1)
                wait(act_e, v_ps, 4 * w)
                act_e.activation(xT[0][:, :, 2 * j * P:(2 * j + 2) * P], ps_xT[j], ACT.Copy).then_inc(xT_hi, 1)

            def qk(w, c):
                act_e.wait_ge(q_ps, 2 * w + c + 1)
                act_e.activation(qf[:, c, :], ps_q, ACT.Identity, bias=bq[:, c:c + 1]).then_inc(q_ready, 1)
                act_e.wait_ge(k_ps, 2 * w + c + 1)
                act_e.activation(kf[:, c, :], ps_k, ACT.Identity, bias=bk[:, c:c + 1]).then_inc(k_ready, 1)

            def exp(w, n):
                act_e.wait_ge(negmax_ready, 8 * w + n + 1)
                for h in range(HC):
                    m = act_e.activation(s[n % 2][:, h, :], s[n % 2][:, h, :], ACT.Exp, bias=negmax[:, n % 2, h:h + 1],
                                         accum_out=rowsum[:, n % 2, h:h + 1])
                m.then_inc(probs, 1)

            def pT_copy(w, n):
                act_e.wait_ge(pT_ps, 8 * w + n + 1)
                wait(act_e, oT_ps, 8 * w + n)
                act_e.activation(pT[:, :, :], ps_p[:, :, :], ACT.Copy).then_inc(pT_ready, 1)

            def oT_high(w, n):
                act_e.wait_ge(oT_ps, 8 * w + n + 1)
                wait(act_e, wo_ps, 4 * w + n // 2)
                c = n % 2
                act_e.activation(oT[0][:, 2 * c:2 * c + 2, :], ps_o, ACT.Copy).then_inc(oT_hi, 1)

            def yT_high(w, j):
                act_e.wait_ge(yT_ps, 2 * w + j + 1)
                if j == 0:
                    dst = yT0[0][:, :, :]
                else:
                    dst = yT[0][:, :, 2 * P:4 * P]
                    wait(act_e, u_ps, 18 * w)
                act_e.activation(dst, ps_yT, ACT.Copy).then_inc(yT_hi, 1)

            def move(w):
                act_e.activation(yT[0][:, :, 0:2 * P], yT0[0][:, :, :].bitcast(F32), ACT.Copy).then_inc(moved_hi, 1)

            def gate_exp_of(w, j):
                act_e.wait_ge(gate_ps, 2 * w + j + 1)
                wait(act_e, gate_step, GATE_OPS * (2 * w + j))
                act_e.activation(g_e[:, :, :], ps_gate, ACT.Exp, scale=-1.0).then_inc(gate_exp, 1)

            def slots(w, v, attn, moe):
                if moe:
                    w_high(v, 0)
                for k in range(SLOTS):
                    if moe:
                        if k + 1 < SLOTS:
                            w_high(v, k + 1)
                        tanh(v, k)
                    if attn:
                        if k == 1:
                            xT_high(w, 0)
                            xT_high(w, 1)
                        if k in (2, 3):
                            qk(w, k - 2)
                        if 0 <= k - 6 < UNITS:
                            exp(w, k - 6)
                    if moe:
                        act_high(v, k)
                    if attn:
                        if k == 15:
                            yT_high(w, 0)
                        if k == 17:
                            gate_exp_of(w, 0)
                        if 0 <= k - 8 < UNITS:
                            oT_high(w, k - 8)
                        if 0 <= k - 7 < UNITS:
                            pT_copy(w, k - 7)

            def end(w, v, attn, moe):
                if attn:
                    yT_high(w, 1)
                    move(w)
                    gate_exp_of(w, 1)

            split_attention()
            schedule(act_e, slots, end)

        @block.vector
        def _(dve):
            def split_attention():
                for n, ((hi, lo), src) in enumerate(((wq, s[0][:, 0:4, :]), (wk, s[0][:, 4:8, :]), (wv, s[1][:, 0:4, :]), (wo, pT[:, :, :]))):
                    dve.wait_ge(attn_hi, n + 1)
                    dve.tensor_tensor(lo[:, :, :].rearrange("p a b -> p (a b)"), src.rearrange("p a b -> p (a b)"),
                                      hi[:, :, :].rearrange("p a b -> p (a b)").bitcast(F32), ALU.subtract).then_inc(attn_lo, 1)
                dve.wait_ge(attn_hi, 5)
                dve.tensor_tensor(wg[1][:, :, :].rearrange("p a b -> p (a b)"), s[1][:, 4, 0:2 * EXPERTS],
                                  wg[0][:, :, :].rearrange("p a b -> p (a b)").bitcast(F32), ALU.subtract).then_inc(attn_lo, 1)

            def x_stats(w, i):
                n = 4 * w + i + 1
                dve.wait_ge(x_in, 16 * w + 16)
                dve.bn_stats(st[:, i, :], x[:, i, :]).then_inc(st_ready, 1)
                dve.wait_ge(st_ready, n)
                dve.memset(ve[:, i:i + 1], EPS)
                dve.bn_aggr(mv[:, i, :], st[:, i, :]).then_inc(mv_ready, 1)
                dve.wait_ge(mv_ready, n)
                dve.tensor_tensor(ve[:, i:i + 1], mv[:, i, 1:2], ve[:, i:i + 1], ALU.add).then_inc(ve_ready, 1)

            def x_norm(w, i):
                dve.wait_ge(rs_ready, 4 * w + i + 1)
                wait(dve, yT_ps, 2 * w)
                dve.tensor_scalar(y[:, i, :], x[:, i, :], mv[:, i, 0:1], rs[:, i:i + 1], ALU.subtract, ALU.mult).then_inc(x_ready, 1)

            def xT_low(w, j):
                dve.wait_ge(xT_hi, 2 * w + j + 1)
                sl = slice(2 * j * P, (2 * j + 2) * P)
                dve.tensor_tensor(xT[1][:, :, sl], ps_xT[j], xT[0][:, :, sl].bitcast(F32), ALU.subtract).then_inc(xT_lo, 1)

            def values(w, m):
                if m == 0:
                    wait(dve, oT_ps, 8 * w)
                    dve.wait_ge(zeros_ready, 1)
                dve.wait_ge(v_ps, 4 * w + m + 1)
                dve.tensor_tensor(vw[:, 2 * m:2 * m + 2, 0:D], ps_v[m % 2], bv[:, :].unsqueeze(1).broadcast_to([P, 2, D]), ALU.add).then_inc(v_ready, 1)

            def mask_scores(w, n):
                i = n // 2
                dve.wait_ge(scores, 8 * w + n + 1)
                wait(dve, pT_ps, 8 * w + n - 1)
                kind = 0 if i == 0 else 2 if i == TT - 1 else 1
                dve.tensor_tensor(s[n % 2][:, :, :], ps_s[:, :, :], band[:, kind, :].unsqueeze(1).broadcast_to([P, HC, P]), ALU.add).then_inc(masked, 1)

            def neg_max(w, n):
                dve.wait_ge(masked, 8 * w + n + 1)
                dve.tensor_reduce(negmax[:, n % 2, :], s[n % 2][:, :, :], AX_X, ALU.max, negate=True).then_inc(negmax_ready, 1)

            def inverse(w, n):
                dve.wait_ge(probs, 8 * w + n + 1)
                wait(dve, probs_ready, 8 * w + n - 1)
                dve.reciprocal(rinv[:, n % 2, :], rowsum[:, n % 2, :]).then_inc(rinv_ready, 1)

            def oT_low(w, n):
                dve.wait_ge(oT_hi, 8 * w + n + 1)
                c = n % 2
                dve.tensor_tensor(oT[1][:, 2 * c:2 * c + 2, :], ps_o, oT[0][:, 2 * c:2 * c + 2, :].bitcast(F32), ALU.subtract).then_inc(oT_lo, 1)

            def residual(w, i):
                n = 4 * w + i + 1
                dve.wait_ge(wo_ps, n)
                dve.wait_ge(hb_ready, w + 1)
                dve.tensor_tensor(h2[:, i, :], ps_x[:, 0:D], h2[:, i, :], ALU.add).then_inc(h2_ready, 1)
                dve.wait_ge(h2_ready, n)
                dve.bn_stats(sty[:, i, :], h2[:, i, :]).then_inc(sty_ready, 1)
                dve.wait_ge(sty_ready, n)
                dve.memset(vey[:, i:i + 1], EPS)
                dve.bn_aggr(mvy[:, i, :], sty[:, i, :]).then_inc(mvy_ready, 1)
                dve.wait_ge(mvy_ready, n)
                dve.tensor_tensor(vey[:, i:i + 1], mvy[:, i, 1:2], vey[:, i:i + 1], ALU.add).then_inc(vey_ready, 1)

            def y_norm(w, i):
                dve.wait_ge(rsy_ready, 4 * w + i + 1)
                dve.tensor_scalar(y[:, i, :], h2[:, i, :], mvy[:, i, 0:1], rsy[:, i:i + 1], ALU.subtract, ALU.mult).then_inc(y_ready, 1)

            def yT_low(w, j):
                dve.wait_ge(yT_hi, 2 * w + j + 1)
                hi, lo = (yT0[n][:, :, :] if j == 0 else yT[n][:, :, 2 * P:4 * P] for n in range(2))
                dve.tensor_tensor(lo, ps_yT, hi.bitcast(F32), ALU.subtract).then_inc(yT_lo, 1)

            def move(w):
                dve.tensor_copy(yT[1][:, :, 0:2 * P], yT0[1][:, :, :].bitcast(F32)).then_inc(moved_lo, 1)

            def silu(v, e):
                n = 18 * v + e + 1
                dve.wait_ge(tanh_ready, n)
                dve.scalar_tensor_tensor(out=th[:, :], in0=th[:, :], scalar=1.0, in1=ps_g[:, :], op0=ALU.add, op1=ALU.mult).then_inc(silu_ready, 1)
                dve.wait_ge(silu_ready, n)
                dve.wait_ge(u_ps, n)
                dve.scalar_tensor_tensor(out=act_f[:, :], in0=th[:, :], scalar=0.5, in1=ps_u[:, :], op0=ALU.mult, op1=ALU.mult).then_inc(act_ready, 1)

            def act_low(v, e):
                dve.wait_ge(act_hi, 18 * v + e + 1)
                hi, lo = act[e % 2]
                dve.tensor_tensor(lo[:, :], act_f[:, :], hi[:, :].bitcast(F32), ALU.subtract).then_inc(act_lo, 1)

            def add_expert(v, e, j):
                dve.wait_ge(y_ps, 36 * v + 2 * e + j + 1)
                if e == 0 and j == 0:
                    dve.wait_ge(ones_ready, 1)
                    wait(dve, out_done, 16 * v)
                    dve.wait_ge(gate_step, 2 * GATE_OPS * v + 2 * GATE_OPS)
                for i in (2 * j, 2 * j + 1):
                    if e > 0:
                        dve.wait_ge(acc_ready, 72 * v + 4 * e - 4 + i + 1)
                    dve.scalar_tensor_tensor(out=acc[:, i, :], in0=ps_y[:, i % 2, :], scalar=weight[:, i, e:e + 1],
                                             in1=h2[:, i, :] if e == 0 else acc[:, i, :], op0=ALU.mult, op1=ALU.add).then_inc(acc_ready, 1)

            def gate(w, j):
                start = GATE_OPS * (2 * w + j)
                done = [0]

                def then(ins, last=False):
                    done[0] += 1
                    ins.then_inc(gate_step, 1)
                    if not last:
                        dve.wait_ge(gate_step, start + done[0])

                def ranks(out_, scores_, before, size):
                    g = g_a[:, :, 0:size, 0:size]
                    e = g_b[:, :, 0:size, 0:size]
                    other = scores_.unsqueeze(2).broadcast_to([P, 2, size, size])
                    own = scores_.unsqueeze(3).broadcast_to([P, 2, size, size])
                    then(dve.tensor_tensor(g, other, own, ALU.is_gt))
                    then(dve.tensor_tensor(e, other, own, ALU.is_ge))
                    then(dve.tensor_tensor(e, e, before.unsqueeze(1).broadcast_to([P, 2, size, size]), ALU.mult))
                    then(dve.tensor_tensor(g, g, e, ALU.max))
                    then(dve.tensor_reduce(out_, g, AX_X, ALU.add))

                dve.wait_ge(gate_exp, 2 * w + j + 1)
                then(dve.tensor_scalar(g_e[:, :, :], g_e[:, :, :], 1.0, None, ALU.add))
                then(dve.reciprocal(g_s[:, :, :], g_e[:, :, :]))
                four = g_s[:, :, :].rearrange("p i (g e) -> p (i g) e", e=4)
                then(dve.tensor_tensor(g_two[:, :, 0:3], four[:, :, 0:3], four[:, :, 1:4], ALU.add))
                then(dve.tensor_tensor(g_two[:, :, 3:5], four[:, :, 0:2], four[:, :, 2:4], ALU.add))
                then(dve.tensor_tensor(g_two[:, :, 5:6], four[:, :, 0:1], four[:, :, 3:4], ALU.add))
                then(dve.tensor_reduce(g_top[:, :, :].rearrange("p i g -> p (i g)"), g_two[:, :, :], AX_X, ALU.max))
                ranks(g_rank[:, :, 0:GROUPS], g_top[:, :, :], before4[:, :, :], GROUPS)
                ok3 = g_ok[:, :].rearrange("p (i g) -> p i g", i=2)
                then(dve.tensor_scalar(ok3, g_rank[:, :, 0:GROUPS], float(TOP_GROUPS), None, ALU.is_lt))
                then(dve.tensor_scalar(g_okm[:, :], g_ok[:, :], 1.0, None, ALU.subtract))
                m4 = g_m[:, :, :].rearrange("p i (g e) -> p (i g) e", e=4)
                then(dve.tensor_tensor(m4, four, g_ok[:, :].unsqueeze(2).broadcast_to([P, 2 * GROUPS, 4]), ALU.mult))
                then(dve.tensor_tensor(m4, m4, g_okm[:, :].unsqueeze(2).broadcast_to([P, 2 * GROUPS, 4]), ALU.add))
                ranks(g_rank[:, :, :], g_m[:, :, :], before16[:, :, :], EXPERTS)
                then(dve.scalar_tensor_tensor(out=g_w[:, :, :], in0=g_rank[:, :, :], scalar=float(TOP), in1=g_s[:, :, :],
                                              op0=ALU.is_lt, op1=ALU.mult))
                then(dve.tensor_reduce(g_sum[:, :], g_w[:, :, :], AX_X, ALU.add))
                then(dve.tensor_scalar(g_sum[:, :], g_sum[:, :], 1e-6, None, ALU.add))
                then(dve.reciprocal(g_sum[:, :], g_sum[:, :]))
                ins = dve.tensor_tensor(weight[:, 2 * j:2 * j + 2, 0:EXPERTS], g_w[:, :, :],
                                        g_sum[:, :].unsqueeze(2).broadcast_to([P, 2, EXPERTS]), ALU.mult)
                then(ins, last=True)
                assert done[0] == GATE_OPS, done[0]

            def slots(w, v, attn, moe):
                for k in range(SLOTS):
                    if moe:
                        silu(v, k)
                        act_low(v, k)
                    if attn and k == 0:
                        for i in range(TT):
                            x_stats(w, i)
                        for i in range(TT):
                            x_norm(w, i)
                    if k == 0 and moe:
                        gate(v, 1)
                    if attn:
                        if k == 1:
                            xT_low(w, 0)
                            xT_low(w, 1)
                        if k in (10, 12, 14, 16):
                            residual(w, (k - 10) // 2)
                        if k == 15:
                            yT_low(w, 0)
                    if moe and k >= 1:
                        add_expert(v, k - 1, 0)
                    if attn and 0 <= k - 5 < UNITS:
                        mask_scores(w, k - 5)
                    if moe and k >= 1:
                        add_expert(v, k - 1, 1)
                    if attn:
                        if 0 <= k - 5 < UNITS:
                            neg_max(w, k - 5)
                        if 0 <= k - 6 < UNITS:
                            inverse(w, k - 6)
                        if k in (3, 4):
                            values(w, 2 * k - 6)
                            values(w, 2 * k - 5)
                        if k in (10, 12, 14, 16):
                            y_norm(w, (k - 10) // 2)
                        if k == 17:
                            gate(w, 0)
                        if 0 <= k - 8 < UNITS:
                            oT_low(w, k - 8)

            def end(w, v, attn, moe):
                if attn:
                    yT_low(w, 1)
                    move(w)
                if moe:
                    add_expert(v, SLOTS - 1, 0)
                    add_expert(v, SLOTS - 1, 1)

            split_attention()
            schedule(dve, slots, end)

        @block.tensor
        def _(pe):
            def up(v, e):
                hi, lo = w13[e % 2]
                if e == 0:
                    pe.wait_ge(yT_lo, 2 * v + 2)
                    pe.wait_ge(moved_hi, v + 1)
                    pe.wait_ge(moved_lo, v + 1)
                pe.wait_ge(w13_lo, 18 * v + e + 1)
                wait(pe, silu_ready, 18 * v + e)
                for name, (bank, done) in enumerate(((ps_g, g_ps), (ps_u, u_ps))):
                    if name == 1:
                        wait(pe, act_ready, 18 * v + e)
                    for k in range(KD):
                        c = (2 * name + k) * P
                        m = passes(pe, bank[:, :], (hi[:, c:c + P], lo[:, c:c + P]), (yT[0][:, k, :], yT[1][:, k, :]), k == 0, k == KD - 1)
                    m.then_inc(done, 1)

            def down(v, e, j):
                hi, lo = w2[e % 3]
                if j == 0:
                    pe.wait_ge(act_lo, 18 * v + e + 1)
                    pe.wait_ge(w2_lo, 18 * v + e + 1)
                wait(pe, acc_ready, 72 * v + 4 * e + 2 * j)
                for i in (2 * j, 2 * j + 1):
                    sl = slice(i * P, (i + 1) * P)
                    m = passes(pe, ps_y[:, i % 2, :], (act[e % 2][0][:, sl], act[e % 2][1][:, sl]), (hi[:, :], lo[:, :]))
                m.then_inc(y_ps, 1)

            def turn(src, j, bank):
                for k in range(KD):
                    for i in range(2):
                        m = pe.transpose(bank[:, k, i * P:(i + 1) * P], src[:, 2 * j + i, k * P:(k + 1) * P], ident[:, :])
                return m

            def turn_x(w, j):
                pe.wait_ge(x_ready, 4 * w + 2 * j + 2)
                wait(pe, pT_ready, 8 * w)
                turn(y, j, ps_xT[j]).then_inc(xT_ps, 1)

            def project(w, c):
                if c == 0:
                    pe.wait_ge(xT_lo, 2 * w + 2)
                    pe.wait_ge(attn_lo, 5)
                    wait(pe, masked, 8 * w)
                wait(pe, q_ready, 2 * w + c)
                wait(pe, k_ready, 2 * w + c)
                for (hi, lo), bank, done in ((wq, ps_q, q_ps), (wk, ps_k, k_ps)):
                    for k in range(KD):
                        m = passes(pe, bank, (hi[:, k, c * P:(c + 1) * P], lo[:, k, c * P:(c + 1) * P]), (xT[0][:, k, :], xT[1][:, k, :]), k == 0, k == KD - 1)
                    m.then_inc(done, 1)

            def values(w, n):
                wait(pe, v_ready, 4 * w + n - 1)
                for b in (2 * n, 2 * n + 1):
                    sl = slice(window(b), window(b) + WIN)
                    for k in range(KD):
                        m = passes(pe, ps_v[n % 2][:, b % 2, :], (xT[0][:, k, sl], xT[1][:, k, sl]), (wv[0][:, k, :], wv[1][:, k, :]), k == 0, k == KD - 1)
                m.then_inc(v_ps, 1)

            def score(w, n):
                i, c = n // 2, n % 2
                pe.wait_ge(qm_ready, 8 * w + n + 1)
                if n == 0:
                    pe.wait_ge(k_ready, 2 * w + 2)
                wait(pe, masked, 8 * w + n)
                for h in range(HC):
                    for b in range(2):
                        first = window(2 * i + b)
                        m = pe.matmul(ps_s[QB * b:QB * b + QB, h, :], qm[n % 2][:, h, QB * b:QB * b + QB], kf[:, c, first:first + WIN], start=True, stop=True)
                m.then_inc(scores, 1)

            def turn_probs(w, n):
                pe.wait_ge(probs_ready, 8 * w + n + 1)
                if n == 0:
                    pe.wait_ge(v_ready, 4 * w + 4)
                wait(pe, pT_ready, 8 * w + n)
                for h in range(HC):
                    m = pe.transpose(ps_p[:, h, :], s[n % 2][:, h, :], ident[:, :])
                m.then_inc(pT_ps, 1)

            def mix(w, n):
                i, c = n // 2, n % 2
                pe.wait_ge(pT_ready, 8 * w + n + 1)
                bank_x_free(w, n)
                for h in range(HC):
                    head = HC * c + h
                    for b in range(2):
                        m = pe.matmul(ps_o[32 * (h % HPC):32 * (h % HPC) + 32, h // HPC, QB * b:QB * b + QB],
                                      vw[:, 2 * i + b, HD * head:HD * head + 32], pT[:, h, QB * b:QB * b + QB], start=True, stop=True,
                                      skip_group_check=True)
                m.then_inc(oT_ps, 1)

            def bank_x_free(w, n):
                wait(pe, oT_lo, 8 * w + n)
                if n >= 2 and n % 2 == 0:
                    pe.wait_ge(h2_ready, 4 * w + n // 2)
                if n == 0:
                    wait(pe, gate_exp, 2 * w)
                if n == 7:
                    pe.wait_ge(yT_lo, 2 * w + 1)

            def project_out(w, i):
                pe.wait_ge(oT_lo, 8 * w + 2 * i + 2)
                for c in range(OC):
                    m = passes(pe, ps_x[:, 0:D], (oT[0][:, c, :], oT[1][:, c, :]), (wo[0][:, c, :], wo[1][:, c, :]), c == 0, c == OC - 1)
                m.then_inc(wo_ps, 1)

            def turn_y(w, j):
                pe.wait_ge(y_ready, 4 * w + 2 * j + 2)
                if j == 0:
                    pe.wait_ge(oT_lo, 8 * w + 7)
                else:
                    pe.wait_ge(gate_exp, 2 * w + 1)
                turn(y, j, ps_yT).then_inc(yT_ps, 1)

            def logits(w, j):
                pe.wait_ge(yT_lo, 2 * w + j + 1)
                if j == 0:
                    pe.wait_ge(h2_ready, 4 * w + 4)
                for i in range(2):
                    src, sl = (yT0, slice(i * P, (i + 1) * P)) if j == 0 else (yT, slice((2 + i) * P, (3 + i) * P))
                    for k in range(KD):
                        m = passes(pe, ps_gate[:, i, :], (src[0][:, k, sl], src[1][:, k, sl]), (wg[0][:, k, :], wg[1][:, k, :]), k == 0, k == KD - 1)
                m.then_inc(gate_ps, 1)

            def slots(w, v, attn, moe):
                for k in range(SLOTS):
                    if moe:
                        up(v, k)
                    if attn:
                        if k in (10, 12, 14, 16):
                            project_out(w, (k - 10) // 2)
                        if k == 15:
                            turn_y(w, 0)
                        if k == 17:
                            logits(w, 0)
                    if moe and k >= 1:
                        down(v, k - 1, 0)
                    if attn:
                        if k == 1:
                            turn_x(w, 0)
                            turn_x(w, 1)
                        if k in (2, 3):
                            project(w, k - 2)
                        if k in (3, 4):
                            values(w, 2 * k - 6)
                            values(w, 2 * k - 5)
                        if 0 <= k - 5 < UNITS:
                            score(w, k - 5)
                    if moe and k >= 1:
                        down(v, k - 1, 1)
                    if attn:
                        if 0 <= k - 8 < UNITS:
                            mix(w, k - 8)
                        if 0 <= k - 7 < UNITS:
                            turn_probs(w, k - 7)

            def end(w, v, attn, moe):
                if moe:
                    down(v, SLOTS - 1, 0)
                if attn:
                    turn_y(w, 1)
                if moe:
                    down(v, SLOTS - 1, 1)
                if attn:
                    logits(w, 1)

            pe.wait_ge(consts_in, 16 * 9)
            schedule(pe, slots, end)


def mixed_lm_kernel(nc, ins, out):
    hidden = nc.dram_tensor("hidden", [BATCH, P, TT, D], F32)
    with nc.sbuf_tensor("state", [P, BATCH, TT, D], F32) as state:
        encoder(nc, ins, state, hidden)
    experts(nc, ins, hidden, out)


def layout(x, _lenS, L0_tok_embed, L0_tok_ln1_g, L0_tok_ln1_b, L0_tok_ln2_g, L0_tok_ln2_b, L0_tok_W1, L0_tok_b1,
           L0_tok_W2, L0_tok_b2, L0_attn_Wq, L0_attn_bq, L0_attn_Wk, L0_attn_bk, L0_attn_Wv, L0_attn_bv, L0_attn_Wo,
           L0_attn_bo, L0_ffn_w_gate, L0_ffn_w1_e, L0_ffn_w3_e, L0_ffn_w2_e, L0_ffn_w1_s, L0_ffn_w3_s, L0_ffn_w2_s):
    def by_rows(w):
        return w.reshape(-1, P, w.shape[1]).transpose(1, 0, 2).reshape(P, -1)

    def up(w):
        return w.reshape(-1, P, KD, P).transpose(3, 0, 2, 1).reshape(P, -1, D)

    wo = np.zeros((OC, HPC, 32, D), np.float32)
    wo[:, :, :HD] = L0_attn_Wo.reshape(OC, HPC, HD, D)
    w1 = np.concatenate([L0_ffn_w1_e, L0_ffn_w1_s.reshape(2, P, D)])
    w3 = np.concatenate([L0_ffn_w3_e, L0_ffn_w3_s.reshape(2, P, D)])
    w2 = np.concatenate([L0_ffn_w2_e, L0_ffn_w2_s.reshape(D, 2, P).transpose(1, 0, 2)])
    arrays = {
        "x": x.reshape(BATCH * TT, P).T, "embed": L0_tok_embed,
        "ln1_g": L0_tok_ln1_g, "ln1_b": L0_tok_ln1_b, "ln2_g": L0_tok_ln2_g, "ln2_b": L0_tok_ln2_b,
        "w1": L0_tok_W1, "w2": L0_tok_W2, "b1": L0_tok_b1.reshape(LAYERS, KF, P).transpose(0, 2, 1), "b2": L0_tok_b2,
        "wq": by_rows(L0_attn_Wq), "wk": by_rows(L0_attn_Wk), "wv": by_rows(L0_attn_Wv),
        "wo": by_rows(wo.reshape(OC * P, D)), "wg": by_rows(L0_ffn_w_gate.T),
        "bq": L0_attn_bq.reshape(KD, P).T, "bk": L0_attn_bk.reshape(KD, P).T, "bv": L0_attn_bv[None], "bo": L0_attn_bo[None],
        "moe": np.concatenate([up(w1), up(w3), w2.transpose(2, 0, 1)], axis=2),
    }

    i = np.arange(D, dtype=np.float32)
    t = np.arange(T, dtype=np.float32)[:, None]
    f = np.float32
    sin = np.sin(t / f(10) ** (f(4) * i / f(D)))
    cos = np.cos(t / f(10) ** (f(4) * (i - f(1)) / f(D)))
    arrays["pos"] = np.where(np.arange(D) % 2 == 0, sin, cos).astype(np.float32)
    arrays["ident"] = np.eye(P, dtype=np.float32)
    band = np.zeros((P, 3, P), np.float32)
    for kind, tile in enumerate((0, 1, TT - 1)):
        for b in range(2):
            q = QB * (2 * tile + b) + np.arange(QB)[:, None]
            k = window(2 * tile + b) + np.arange(WIN)[None, :]
            band[QB * b:QB * b + QB, kind] = np.where(np.abs(q - k) <= HALF, 0.0, -1e30)
    arrays["band"] = band
    arrays["hmask"] = np.where(np.arange(P)[:, None] // HD == np.arange(HC), np.float32(HD ** -0.5), np.float32(0)).astype(np.float32)
    for n in (4, 16):
        arrays[f"before{n}"] = np.broadcast_to(np.tril(np.ones((n, n), np.float32), -1), (P, n, n))
    return {name: np.ascontiguousarray(a) for name, a in arrays.items()}


def kernel(**inputs):
    import concourse.bacc as bacc
    from concourse.bass_utils import run_bass_kernel_spmd

    nc = bacc.Bacc("TRN2", target_bir_lowering=False, num_devices=1)
    arrays = layout(**{name: np.asarray(a) for name, a in inputs.items()})
    ins = {name: nc.dram_tensor(f"in_{name}", a.shape, mybir.dt.from_np(a.dtype), kind="ExternalInput").ap() for name, a in arrays.items()}
    out = nc.dram_tensor("out", (BATCH, T, D), F32, kind="ExternalOutput").ap()
    mixed_lm_kernel(nc, ins, out)
    r = run_bass_kernel_spmd(nc, [{f"in_{name}": a for name, a in arrays.items()}], core_ids=[0])
    return r.results[0]["out"]
```

```python
from contextlib import ExitStack

import numpy as np
import concourse.bass as bass
from concourse import mybir

F32 = mybir.dt.float32
F32R = mybir.dt.float32r
I32 = mybir.dt.int32
U32 = mybir.dt.uint32
ALU = mybir.AluOpType
ACT = mybir.ActivationFunctionType
AX_X = mybir.AxisListType.X

P = 128
LAYERS, D, DF, V = 6, 256, 1024, 8000
BATCH, T = 8, 512
TT = T // P
KD = D // P
KF = DF // P
EPS = 1e-5


def passes(pe, out, a, b, first=True, last=True):
    pe.matmul(out, a[1], b[0], start=first, stop=False)
    pe.matmul(out, a[0], b[1], start=False, stop=False)
    return pe.matmul(out, a[0], b[0], start=False, stop=last)


def encoder(nc, ins, state, hidden):
    ctx = ExitStack()
    with ctx:
        def sb(name, shape, dt=F32):
            return ctx.enter_context(nc.sbuf_tensor(name, shape, dt))

        def sem(name):
            return ctx.enter_context(nc.semaphore(name))

        ident = sb("ident", [P, P])
        pos = sb("pos", [P, TT, D])
        ids = sb("ids", [P, BATCH * TT], I32)
        neg = sb("neg", [P, BATCH * TT], I32)
        rows = sb("rows", [P, BATCH * TT], U32)
        hraw = [sb(f"hraw{i}", [P, TT, D]) for i in range(2)]
        v_hi, v_lo = sb("v_hi", [P, TT, D], F32R), sb("v_lo", [P, TT, D], F32R)
        hT_hi, hT_lo = sb("hT_hi", [P, KD, T], F32R), sb("hT_lo", [P, KD, T], F32R)
        probs = [sb(f"probs{i}", [P, T]) for i in range(2)]
        pT_hi = [sb(f"pT_hi{i}", [P, TT, P], F32R) for i in range(2)]
        pT_lo = [sb(f"pT_lo{i}", [P, TT, P], F32R) for i in range(2)]
        h1 = [sb(f"h1_{i}", [P, TT, D]) for i in range(2)]
        h1b = sb("h1b", [P, TT, D])
        h1T_hi, h1T_lo = sb("h1T_hi", [P, KD, T], F32R), sb("h1T_lo", [P, KD, T], F32R)
        x1, x2 = sb("x1", [P, 2, D]), sb("x2", [P, 2, D])
        hid = [sb(f"hid{i}", [P, T]) for i in range(2)]
        hid_hi, hid_lo = sb("hid_hi", [P, KF, T], F32R), sb("hid_lo", [P, KF, T], F32R)
        w1_raw, w2_raw = sb("w1_raw", [P, KD, DF]), sb("w2_raw", [P, KF, D])
        w1_hi, w1_lo = sb("w1_hi", [P, KD, DF], F32R), sb("w1_lo", [P, KD, DF], F32R)
        w2_hi, w2_lo = sb("w2_hi", [P, KF, D], F32R), sb("w2_lo", [P, KF, D], F32R)
        g1, be1 = sb("g1", [P, D]), sb("be1", [P, D])
        g2, be2, b2 = sb("g2", [P, D]), sb("be2", [P, D]), sb("b2", [P, D])
        b1 = sb("b1", [P, KF])
        negmax, rowsum, rinv = sb("negmax", [P, TT]), sb("rowsum", [P, TT]), sb("rinv", [P, TT])
        st1, mv1, ve1, rs1 = sb("st1", [P, TT, 6]), sb("mv1", [P, TT, 2]), sb("ve1", [P, TT]), sb("rs1", [P, TT])
        st2, mv2, ve2, rs2 = sb("st2", [P, TT, 6]), sb("mv2", [P, TT, 2]), sb("ve2", [P, TT]), sb("rs2", [P, TT])
        minus_half = sb("minus_half", [P, 1])

        ps_s = [ctx.enter_context(nc.psum_tensor(f"ps_s{i}", [P, T], F32)) for i in range(2)]
        ps_pT = ctx.enter_context(nc.psum_tensor("ps_pT", [P, TT, P], F32))
        ps_mha = ctx.enter_context(nc.psum_tensor("ps_mha", [P, D], F32))
        ps_hid = [ctx.enter_context(nc.psum_tensor(f"ps_hid{i}", [P, T], F32)) for i in range(2)]
        ps_ff0 = ctx.enter_context(nc.psum_tensor("ps_ff0", [P, D], F32))
        ps_h1T = ctx.enter_context(nc.psum_tensor("ps_h1T", [P, KD, 2, P], F32))
        ps_hT = [ps_s[j][:, :].rearrange("p (k i t) -> p k i t", k=KD, i=2) for j in range(2)]
        ps_ff = [ps_ff0[:, :], ps_hid[1][:, 0:D]]

        consts_in, ids_in = sem("consts_in"), sem("ids_in")
        h_stored = sem("h_stored")
        h_in = [sem("h_in0"), sem("h_in1")]
        w1_in, w2_in = sem("w1_in"), sem("w2_in")
        ln1_in, ln2_in, b1_in = sem("ln1_in"), sem("ln2_in"), sem("b1_in")
        gathered = [sem(f"gathered{b}") for b in range(BATCH)]
        rows_step, rows_ready, half_ready = sem("rows_step"), sem("rows_ready"), sem("half_ready")
        first_ready, state_ready = sem("first_ready"), sem("state_ready")
        hT_ps, hT_hi_ready, hT_lo_ready = sem("hT_ps"), sem("hT_hi_ready"), sem("hT_lo_ready")
        v_hi_ready, v_lo_ready = sem("v_hi_ready"), sem("v_lo_ready")
        scores, negmax_ready, probs_ready = sem("scores"), sem("negmax_ready"), sem("probs_ready")
        pT_ps, pT_hi_ready, pT_lo_ready = sem("pT_ps"), sem("pT_hi_ready"), sem("pT_lo_ready")
        mha_ps, rinv_ready, x1_ready, st1_ready = sem("mha_ps"), sem("rinv_ready"), sem("x1_ready"), sem("st1_ready")
        mv1_ready, ve1_ready, rs1_ready = sem("mv1_ready"), sem("ve1_ready"), sem("rs1_ready")
        n1_ready, h1_ready = sem("n1_ready"), sem("h1_ready")
        h1T_ps, h1T_hi_ready, h1T_lo_ready = sem("h1T_ps"), sem("h1T_hi_ready"), sem("h1T_lo_ready")
        h1b_ready = sem("h1b_ready")
        hid_ps, hid_ready, hid_hi_ready, hid_lo_ready = sem("hid_ps"), sem("hid_ready"), sem("hid_hi_ready"), sem("hid_lo_ready")
        ff_ps, x2_ready, st2_ready = sem("ff_ps"), sem("x2_ready"), sem("st2_ready")
        mv2_ready, ve2_ready, rs2_ready, n2_ready = sem("mv2_ready"), sem("ve2_ready"), sem("rs2_ready"), sem("n2_ready")
        w1_hi_ready, w1_lo_ready = sem("w1_hi_ready"), sem("w1_lo_ready")
        w2_hi_ready, w2_lo_ready = sem("w2_hi_ready"), sem("w2_lo_ready")

        def schedule(eng, start, step, split):
            start()
            step(0, 0, 0, 1, 0, 0, 1, ffn=False)

            def six_steps(l):
                with eng.Fori(0, 3) as p:
                    step(8 * l + 2 * p + 1, 32 * l + 8 * p + 4, 1, 2 * p + 2, l, l, 4 * l + p + 2)
                    step(8 * l + 2 * p + 2, 32 * l + 8 * p + 8, 0, 2 * p + 3, l, l, 4 * l + p + 2)

            with eng.Fori(0, LAYERS - 1) as l:
                six_steps(l)
                step(8 * l + 7, 32 * l + 28, 1, 0, l, l, 4 * l + 5)
                step(8 * l + 8, 32 * l + 32, 0, 1, l + 1, l, 4 * l + 5, layer_end=True)
                split(8 * l + 8, 32 * l + 32, l + 1)
            l = LAYERS - 1
            six_steps(l)
            step(8 * l + 7, 32 * l + 28, 1, 0, l, l, None, prep=False)
            step(8 * l + 8, 32 * l + 32, 0, 1, l, l, None, attn=False, prep=False)

        def wait(eng, s, value):
            if not isinstance(value, int) or value > 0:
                eng.wait_ge(s, value)

        block = ctx.enter_context(nc.Block())

        @block.sync
        def _(sp):
            def vectors(l, which):
                if which == 1:
                    pairs, s = ((g1, "ln1_g"), (be1, "ln1_b")), ln1_in
                else:
                    pairs, s = ((g2, "ln2_g"), (be2, "ln2_b"), (b2, "b2")), ln2_in
                for dst, name in pairs:
                    sp.dma_start(dst[:, :], ins[name][bass.ds(l, 1), :].broadcast_to([P, D])).then_inc(s, 16)

            def bias1(l):
                sp.dma_start(b1[:, :], ins["b1"][bass.ds(l, 1), :, :].rearrange("l p f -> (l p) f")).then_inc(b1_in, 16)

            def weights(l):
                sp.dma_start(w1_raw[:, :, :], ins["w1"][bass.ds(l, 1), :, :].rearrange("l (k p) f -> p (l k) f", p=P)).then_inc(w1_in, 16)
                sp.dma_start(w2_raw[:, :, :], ins["w2"][bass.ds(l, 1), :, :].rearrange("l (k p) f -> p (l k) f", p=P)).then_inc(w2_in, 16)

            def load_h(t, par, b):
                if isinstance(t, int) and t <= 0:
                    sp.wait_ge(first_ready, t + 8)
                else:
                    sp.wait_ge(state_ready, t)
                wait(sp, x1_ready, t)
                sp.dma_start(hraw[1 - par][:, :, :], state[:, bass.ds(b, 1), :, :].rearrange("p b t d -> p (b t) d")).then_inc(h_in[1 - par], 16)

            sp.dma_start(ids[:, :], ins["x"]).then_inc(ids_in, 16)
            sp.dma_start(pos[:, :, :], ins["pos"].rearrange("(t p) d -> p t d", p=P)).then_inc(consts_in, 16)
            sp.dma_start(ident[:, :], ins["ident"]).then_inc(consts_in, 16)
            vectors(0, 1)
            load_h(-4, 1, 0)
            load_h(0, 0, 1)
            weights(0)
            vectors(0, 2)
            bias1(0)
            with sp.Fori(1, LAYERS) as l:
                t0 = (l - 1) * 32
                sp.wait_ge(w1_hi_ready, l)
                sp.wait_ge(w1_lo_ready, l)
                sp.wait_ge(w2_hi_ready, l)
                sp.wait_ge(w2_lo_ready, l)
                weights(l)
                with sp.Fori(0, 3) as p:
                    load_h(t0 + 8 * p + 4, 1, 2 * p + 2)
                    load_h(t0 + 8 * p + 8, 0, 2 * p + 3)
                load_h(t0 + 28, 1, 0)
                sp.wait_ge(h1_ready, t0 + 32)
                vectors(l, 1)
                load_h(t0 + 32, 0, 1)
                sp.wait_ge(hid_ready, t0 * 2 + 64)
                bias1(l)
                sp.wait_ge(state_ready, t0 + 56)
                vectors(l, 2)
            t0 = (LAYERS - 1) * 32
            with sp.Fori(0, 3) as p:
                load_h(t0 + 8 * p + 4, 1, 2 * p + 2)
                load_h(t0 + 8 * p + 8, 0, 2 * p + 3)
            with sp.Fori(0, BATCH) as b:
                sp.wait_ge(state_ready, t0 + 28 + 4 * b)
                sp.dma_start(hidden[bass.ds(b, 1), :, :, :].rearrange("b p t d -> p (b t) d"), state[:, bass.ds(b, 1), :, :].rearrange("p b t d -> p (b t) d")).then_inc(h_stored, 16)
            sp.wait_ge(h_stored, 16 * BATCH)

        @block.gpsimd
        def _(pool):
            def gather(b):
                for i in range(TT):
                    pool.indirect_dma_start(
                        out=state[:, b, i, :], out_offset=None, in_=ins["embed"],
                        in_offset=bass.IndirectOffsetOnAxis(ap=rows[:, b * TT + i:b * TT + i + 1], axis=0)).then_inc(gathered[b], 16)

            def v_low(u, t, par, n):
                wait(pool, mha_ps, t + 4)
                pool.wait_ge(v_hi_ready, u + 2)
                pool.tensor_tensor(v_lo[:, :, :], hraw[1 - par][:, :, :], v_hi[:, :, :].bitcast(F32), ALU.subtract).then_inc(v_lo_ready, 1)

            def add_bias2(u, t, par, lf):
                pool.wait_ge(h1_ready, t)
                pool.wait_ge(ln2_in, (lf + 1) * 48)
                wait(pool, x2_ready, t - 4)
                pool.tensor_tensor(h1b[:, :, :], h1[1 - par][:, :, :], b2[:, :].unsqueeze(1).broadcast_to([P, TT, D]), ALU.add).then_inc(h1b_ready, 1)

            def hid_low(t, f):
                pool.wait_ge(hid_hi_ready, 2 * t - 8 + f + 1)
                if f == 0:
                    wait(pool, ff_ps, t - 4)
                pool.tensor_tensor(hid_lo[:, f, :], hid[f % 2][:, :], hid_hi[:, f, :].bitcast(F32), ALU.subtract).then_inc(hid_lo_ready, 1)

            def rstd1(t, i):
                pool.wait_ge(ve1_ready, t + i + 1)
                pool.tensor_tensor(rs1[:, i:i + 1], ve1[:, i:i + 1], minus_half[:, :], ALU.pow).then_inc(rs1_ready, 1)

            def rstd2(t, i):
                pool.wait_ge(ve2_ready, t - 4 + i + 1)
                pool.tensor_tensor(rs2[:, i:i + 1], ve2[:, i:i + 1], minus_half[:, :], ALU.pow).then_inc(rs2_ready, 1)

            def step(u, t, par, b, la, lf, n, attn=True, ffn=True, prep=True, layer_end=False):
                for i in range(TT):
                    if ffn:
                        hid_low(t, 2 * i)
                        if i < TT - 1:
                            hid_low(t, 2 * i + 1)
                    else:
                        if i == 0:
                            gather(2)
                        gather(3 + i)
                    if ffn and i == 1:
                        add_bias2(u, t, par, lf)
                    if attn and i >= 1:
                        rstd1(t, i - 1)
                if ffn:
                    rstd2(t, 0)
                if attn:
                    rstd1(t, 3)
                if prep:
                    v_low(u, t, par, n)
                if not ffn:
                    gather(7)
                if ffn:
                    for i in range(1, TT):
                        rstd2(t, i)

            def start():
                pool.memset(minus_half[:, :], -0.5).then_inc(half_ready, 1)
                pool.wait_ge(rows_ready, 1)
                gather(0)
                gather(1)
                pool.wait_ge(half_ready, 1)
                v_low(-1, -4, 1, 1)

            def split(u, t, l):
                pool.wait_ge(w2_hi_ready, l + 1)
                pool.tensor_tensor(w2_lo[:, :, :], w2_raw[:, :, :], w2_hi[:, :, :].bitcast(F32), ALU.subtract).then_inc(w2_lo_ready, 1)

            schedule(pool, start, step, split)

        @block.scalar
        def _(act):
            def relu(t, f, lf):
                act.wait_ge(hid_ps, 2 * t - 8 + f + 1)
                wait(act, hid_lo_ready, 2 * t - 8 + max(f - 1, 0))
                if f == 0:
                    act.wait_ge(b1_in, (lf + 1) * 16)
                act.activation(hid[f % 2][:, :], ps_hid[f % 2][:, :], ACT.Relu, bias=b1[:, f:f + 1]).then_inc(hid_ready, 1)
                if f == 0:
                    wait(act, ff_ps, t - 4)
                act.wait_ge(hid_ready, 2 * t - 8 + f + 1)
                act.activation(hid_hi[:, f, :], hid[f % 2][:, :], ACT.Copy).then_inc(hid_hi_ready, 1)

            def exp(t, i):
                act.wait_ge(negmax_ready, t + i + 1)
                wait(act, pT_ps, t + i - 1)
                act.activation(probs[i % 2][:, :], ps_s[i % 2][:, :], ACT.Exp, bias=negmax[:, i:i + 1],
                               accum_out=rowsum[:, i:i + 1]).then_inc(probs_ready, 1)

            def pT_high(t, i):
                act.wait_ge(pT_ps, t + i + 1)
                wait(act, mha_ps, t + i - 1)
                act.activation(pT_hi[i % 2][:, :, :], ps_pT[:, :, :], ACT.Copy).then_inc(pT_hi_ready, 1)

            def h1T_high(u, j):
                act.wait_ge(h1T_ps, 2 * u + j + 1)
                wait(act, hid_ps, 8 * u)
                act.activation(h1T_hi[:, :, 2 * j * P:(2 * j + 2) * P], ps_h1T[:, :, :, :].rearrange("p k i t -> p k (i t)"), ACT.Copy).then_inc(h1T_hi_ready, 1)

            def hT_high(u, t, j):
                act.wait_ge(hT_ps, 2 * u + 2 + j + 1)
                wait(act, scores, t + 4)
                act.activation(hT_hi[:, :, 2 * j * P:(2 * j + 2) * P], ps_hT[j].rearrange("p k i t -> p k (i t)"), ACT.Copy, scale=0.25).then_inc(hT_hi_ready, 1)

            def v_high(u, t, par, n):
                act.wait_ge(h_in[1 - par], 16 * n)
                wait(act, mha_ps, t + 4)
                act.activation(v_hi[:, :, :], hraw[1 - par][:, :, :], ACT.Copy).then_inc(v_hi_ready, 1)

            def split_w1(l):
                act.wait_ge(w1_in, 16 * l + 16)
                act.activation(w1_hi[:, :, :], w1_raw[:, :, :], ACT.Copy).then_inc(w1_hi_ready, 1)

            def split_w2(l):
                act.wait_ge(w2_in, 16 * l + 16)
                act.activation(w2_hi[:, :, :], w2_raw[:, :, :], ACT.Copy).then_inc(w2_hi_ready, 1)

            def step(u, t, par, b, la, lf, n, attn=True, ffn=True, prep=True, layer_end=False):
                for i in range(TT):
                    if attn:
                        if i >= 1:
                            pT_high(t, i - 1)
                        exp(t, i)
                    if ffn:
                        relu(t, 2 * i, lf)
                        relu(t, 2 * i + 1, lf)
                if attn:
                    pT_high(t, 3)
                if not ffn:
                    split_w1(0)
                    split_w2(0)
                if layer_end:
                    act.wait_ge(hid_ps, 2 * t)
                    split_w1(lf + 1)
                if attn:
                    h1T_high(u, 0)
                if prep:
                    v_high(u, t, par, n)
                    hT_high(u, t, 0)
                    hT_high(u, t, 1)
                if attn:
                    h1T_high(u, 1)

            def start():
                v_high(-1, -4, 1, 1)
                for j in range(2):
                    hT_high(-1, -4, j)

            def split(u, t, l):
                act.wait_ge(ff_ps, t)
                split_w2(l)

            schedule(act, start, step, split)

        @block.vector
        def _(dve):
            def neg_max(t, i):
                dve.wait_ge(scores, t + i + 1)
                wait(dve, probs_ready, t + i - 3)
                dve.tensor_reduce(negmax[:, i:i + 1], ps_s[i % 2][:, :], AX_X, ALU.max, negate=True).then_inc(negmax_ready, 1)

            def pT_low(t, i):
                dve.wait_ge(pT_hi_ready, t + i + 1)
                wait(dve, mha_ps, t + i - 1)
                dve.tensor_tensor(pT_lo[i % 2][:, :, :], ps_pT[:, :, :], pT_hi[i % 2][:, :, :].bitcast(F32), ALU.subtract).then_inc(pT_lo_ready, 1)

            def residual1(t, par, i):
                dve.wait_ge(probs_ready, t + i + 1)
                dve.reciprocal(rinv[:, i:i + 1], rowsum[:, i:i + 1]).then_inc(rinv_ready, 1)
                dve.wait_ge(mha_ps, t + i + 1)
                dve.wait_ge(rinv_ready, t + i + 1)
                dve.scalar_tensor_tensor(out=x1[:, i % 2, :], in0=ps_mha[:, :], scalar=rinv[:, i:i + 1],
                                         in1=hraw[par][:, i, :], op0=ALU.mult, op1=ALU.add).then_inc(x1_ready, 1)
                dve.wait_ge(x1_ready, t + i + 1)
                dve.bn_stats(st1[:, i, :], x1[:, i % 2, :]).then_inc(st1_ready, 1)
                dve.wait_ge(st1_ready, t + i + 1)
                dve.memset(ve1[:, i:i + 1], EPS)
                dve.bn_aggr(mv1[:, i, :], st1[:, i, :]).then_inc(mv1_ready, 1)
                dve.wait_ge(mv1_ready, t + i + 1)
                dve.tensor_tensor(ve1[:, i:i + 1], mv1[:, i, 1:2], ve1[:, i:i + 1], ALU.add).then_inc(ve1_ready, 1)

            def norm1(t, par, i, la):
                if i == 0:
                    dve.wait_ge(ln1_in, (la + 1) * 32)
                dve.scalar_tensor_tensor(out=x1[:, i % 2, :], in0=x1[:, i % 2, :], scalar=mv1[:, i, 0:1],
                                         in1=g1[:, :], op0=ALU.subtract, op1=ALU.mult).then_inc(n1_ready, 1)
                dve.wait_ge(n1_ready, t + i + 1)
                dve.wait_ge(rs1_ready, t + i + 1)
                dve.scalar_tensor_tensor(out=h1[par][:, i, :], in0=x1[:, i % 2, :], scalar=rs1[:, i:i + 1],
                                         in1=be1[:, :], op0=ALU.mult, op1=ALU.add).then_inc(h1_ready, 1)

            def h1T_low(u, j):
                dve.wait_ge(h1T_hi_ready, 2 * u + j + 1)
                sl = slice(2 * j * P, (2 * j + 2) * P)
                dve.tensor_tensor(h1T_lo[:, :, sl], ps_h1T[:, :, :, :].rearrange("p k i t -> p k (i t)"), h1T_hi[:, :, sl].bitcast(F32), ALU.subtract).then_inc(h1T_lo_ready, 1)

            def hT_low(u, j):
                dve.wait_ge(hT_hi_ready, 2 * u + 2 + j + 1)
                sl = slice(2 * j * P, (2 * j + 2) * P)
                dve.scalar_tensor_tensor(out=hT_lo[:, :, sl], in0=ps_hT[j].rearrange("p k i t -> p k (i t)"), scalar=0.25,
                                         in1=hT_hi[:, :, sl].bitcast(F32), op0=ALU.mult, op1=ALU.subtract).then_inc(hT_lo_ready, 1)

            def residual2(u, t, i):
                n = t - 4 + i + 1
                dve.wait_ge(ff_ps, n)
                if i == 0:
                    dve.wait_ge(h1b_ready, u)
                dve.tensor_tensor(x2[:, i % 2, :], ps_ff[i % 2], h1b[:, i, :], ALU.add).then_inc(x2_ready, 1)
                dve.wait_ge(x2_ready, n)
                dve.bn_stats(st2[:, i, :], x2[:, i % 2, :]).then_inc(st2_ready, 1)
                dve.wait_ge(st2_ready, n)
                dve.memset(ve2[:, i:i + 1], EPS)
                dve.bn_aggr(mv2[:, i, :], st2[:, i, :]).then_inc(mv2_ready, 1)
                dve.wait_ge(mv2_ready, n)
                dve.tensor_tensor(ve2[:, i:i + 1], mv2[:, i, 1:2], ve2[:, i:i + 1], ALU.add).then_inc(ve2_ready, 1)

            def norm2(t, b, i, lf):
                n = t - 4 + i + 1
                if i == 0:
                    dve.wait_ge(ln2_in, (lf + 1) * 48)
                dve.scalar_tensor_tensor(out=x2[:, i % 2, :], in0=x2[:, i % 2, :], scalar=mv2[:, i, 0:1],
                                         in1=g2[:, :], op0=ALU.subtract, op1=ALU.mult).then_inc(n2_ready, 1)
                dve.wait_ge(n2_ready, n)
                dve.wait_ge(rs2_ready, n)
                at = (b + 6) % 8 if isinstance(b, int) else b - 2
                dve.scalar_tensor_tensor(out=state[:, bass.ds(at, 1), i, :].rearrange("p b d -> p (b d)"), in0=x2[:, i % 2, :],
                                         scalar=rs2[:, i:i + 1], in1=be2[:, :], op0=ALU.mult, op1=ALU.add).then_inc(state_ready, 1)

            def hid_low(t, f):
                dve.wait_ge(hid_hi_ready, 2 * t - 8 + f + 1)
                dve.tensor_tensor(hid_lo[:, f, :], hid[f % 2][:, :], hid_hi[:, f, :].bitcast(F32), ALU.subtract).then_inc(hid_lo_ready, 1)

            def add_positions(b):
                dve.wait_ge(gathered[b], 16 * TT)
                dve.tensor_tensor(state[:, b, :, :], state[:, b, :, :], pos[:, :, :], ALU.add).then_inc(first_ready if b < 2 else state_ready, TT)

            def split_w1(l):
                dve.wait_ge(w1_hi_ready, l + 1)
                dve.tensor_tensor(w1_lo[:, :, :], w1_raw[:, :, :], w1_hi[:, :, :].bitcast(F32), ALU.subtract).then_inc(w1_lo_ready, 1)

            def split_w2(l):
                dve.wait_ge(w2_hi_ready, l + 1)
                dve.tensor_tensor(w2_lo[:, :, :], w2_raw[:, :, :], w2_hi[:, :, :].bitcast(F32), ALU.subtract).then_inc(w2_lo_ready, 1)

            def start():
                dve.wait_ge(ids_in, 16)
                dve.tensor_scalar(neg[:, :], ids[:, :], 0, V, ALU.is_lt, ALU.mult).then_inc(rows_step, 1)
                dve.wait_ge(rows_step, 1)
                dve.tensor_tensor(ids[:, :], ids[:, :], neg[:, :], ALU.add).then_inc(rows_step, 1)
                dve.wait_ge(rows_step, 2)
                dve.tensor_scalar(rows[:, :], ids[:, :], 0, V - 1, ALU.max, ALU.min).then_inc(rows_ready, 1)
                dve.wait_ge(consts_in, 32)
                add_positions(0)
                add_positions(1)
                for j in range(2):
                    hT_low(-1, j)

            def step(u, t, par, b, la, lf, n, attn=True, ffn=True, prep=True, layer_end=False):
                if attn:
                    neg_max(t, 0)
                    neg_max(t, 1)
                    pT_low(t, 0)
                    residual1(t, par, 0)
                    neg_max(t, 2)
                    pT_low(t, 1)
                    residual1(t, par, 1)
                    neg_max(t, 3)
                    norm1(t, par, 0, la)
                    if not ffn:
                        add_positions(2)
                    pT_low(t, 2)
                    norm1(t, par, 1, la)
                    if not ffn:
                        add_positions(3)
                if ffn:
                    hid_low(t, KF - 1)
                if attn:
                    residual1(t, par, 2)
                    pT_low(t, 3)
                    norm1(t, par, 2, la)
                    h1T_low(u, 0)
                    if not ffn:
                        add_positions(4)
                if ffn:
                    residual2(u, t, 0)
                if attn:
                    residual1(t, par, 3)
                    if not ffn:
                        add_positions(5)
                if ffn:
                    norm2(t, b, 0, lf)
                if attn:
                    norm1(t, par, 3, la)
                if layer_end:
                    split_w1(lf + 1)
                if prep:
                    hT_low(u, 0)
                if ffn:
                    residual2(u, t, 1)
                if prep:
                    hT_low(u, 1)
                if ffn:
                    norm2(t, b, 1, lf)
                    residual2(u, t, 2)
                if attn:
                    h1T_low(u, 1)
                if ffn:
                    norm2(t, b, 2, lf)
                    residual2(u, t, 3)
                    norm2(t, b, 3, lf)
                else:
                    split_w1(0)
                    split_w2(0)
                    add_positions(6)
                    add_positions(7)

            schedule(dve, start, step, lambda u, t, l: None)

        @block.tensor
        def _(pe):
            def tile_of(i):
                return slice(i * P, (i + 1) * P)

            def score(u, t, i):
                if i == 0:
                    pe.wait_ge(hT_lo_ready, 2 * u + 2)
                    pe.wait_ge(hT_hi_ready, 2 * u + 2)
                wait(pe, probs_ready, t + i - 1)
                for k in range(KD):
                    m = passes(pe, ps_s[i % 2][:, :], (hT_hi[:, k, tile_of(i)], hT_lo[:, k, tile_of(i)]),
                               (hT_hi[:, k, :], hT_lo[:, k, :]), k == 0, k == KD - 1)
                m.then_inc(scores, 1)

            def turn_probs(t, i):
                pe.wait_ge(probs_ready, t + i + 1)
                wait(pe, pT_lo_ready, t + i)
                for c in range(TT):
                    m = pe.transpose(ps_pT[:, c, :], probs[i % 2][:, tile_of(c)], ident[:, :])
                m.then_inc(pT_ps, 1)

            def mix(u, t, i):
                if i == 0:
                    pe.wait_ge(v_lo_ready, u + 1)
                    pe.wait_ge(v_hi_ready, u + 1)
                pe.wait_ge(pT_lo_ready, t + i + 1)
                wait(pe, x1_ready, t + i)
                for c in range(TT):
                    m = passes(pe, ps_mha[:, :], (pT_hi[i % 2][:, c, :], pT_lo[i % 2][:, c, :]),
                               (v_hi[:, c, :], v_lo[:, c, :]), c == 0, c == TT - 1)
                m.then_inc(mha_ps, 1)

            def turn(src, j, bank):
                for k in range(KD):
                    for i in range(2):
                        m = pe.transpose(bank[:, k, i, :], src[:, 2 * j + i, k * P:(k + 1) * P], ident[:, :])
                return m

            def turn_h1(u, t, par, j):
                pe.wait_ge(h1_ready, t + 2 * j + 2)
                wait(pe, h1T_lo_ready, 2 * u + j)
                turn(h1[par], j, ps_h1T).then_inc(h1T_ps, 1)

            def turn_h(u, t, par, j, n):
                pe.wait_ge(h_in[1 - par], 16 * n)
                wait(pe, probs_ready, t + 4)
                turn(hraw[1 - par], j, ps_hT[j]).then_inc(hT_ps, 1)

            def up(u, t, f, lf):
                if f == 0:
                    pe.wait_ge(h1T_lo_ready, 2 * u)
                    pe.wait_ge(w1_lo_ready, lf + 1)
                if f == 1:
                    wait(pe, x2_ready, t - 4)
                wait(pe, hid_ready, 2 * t - 8 + max(f - 1, 0))
                for k in range(KD):
                    m = passes(pe, ps_hid[f % 2][:, :], (w1_hi[:, k, tile_of(f)], w1_lo[:, k, tile_of(f)]),
                               (h1T_hi[:, k, :], h1T_lo[:, k, :]), k == 0, k == KD - 1)
                m.then_inc(hid_ps, 1)

            def down(t, i, lf):
                if i == 0:
                    pe.wait_ge(hid_lo_ready, 2 * t)
                    pe.wait_ge(w2_lo_ready, lf + 1)
                wait(pe, x2_ready, t - 4 + max(i - 1, 0))
                for f in range(KF):
                    m = passes(pe, ps_ff[i % 2], (hid_hi[:, f, tile_of(i)], hid_lo[:, f, tile_of(i)]),
                               (w2_hi[:, f, :], w2_lo[:, f, :]), f == 0, f == KF - 1)
                m.then_inc(ff_ps, 1)

            def step(u, t, par, b, la, lf, n, attn=True, ffn=True, prep=True, layer_end=False):
                if attn:
                    score(u, t, 0)
                if ffn:
                    up(u, t, 0, lf)
                if attn:
                    score(u, t, 1)
                if ffn:
                    up(u, t, 1, lf)
                if attn:
                    turn_probs(t, 0)
                if ffn:
                    up(u, t, 2, lf)
                    up(u, t, 3, lf)
                if attn:
                    mix(u, t, 0)
                    score(u, t, 2)
                    turn_probs(t, 1)
                if ffn:
                    up(u, t, 4, lf)
                    up(u, t, 5, lf)
                if attn:
                    mix(u, t, 1)
                    score(u, t, 3)
                    turn_probs(t, 2)
                if ffn:
                    up(u, t, 6, lf)
                    up(u, t, 7, lf)
                if attn:
                    mix(u, t, 2)
                    turn_probs(t, 3)
                    turn_h1(u, t, par, 0)
                if ffn:
                    down(t, 0, lf)
                if attn:
                    mix(u, t, 3)
                if prep:
                    turn_h(u, t, par, 0, n)
                if ffn:
                    down(t, 1, lf)
                if prep:
                    turn_h(u, t, par, 1, n)
                if ffn:
                    down(t, 2, lf)
                if attn:
                    turn_h1(u, t, par, 1)
                if ffn:
                    down(t, 3, lf)

            def start():
                pe.wait_ge(consts_in, 32)
                for j in range(2):
                    turn_h(-1, -4, 1, j, 1)

            schedule(pe, start, step, lambda u, t, l: None)


HEADS, HD, HALF = 16, 16, 32
HC = HEADS // KD
QB = 64
WIN = 2 * QB
NWIN = T // QB
UNITS = TT * KD
EXPERTS, GROUPS, TOP_GROUPS, TOP = 16, 4, 2, 4
SHARED = 2
SLOTS = SHARED + EXPERTS
HPC = 4
OC = HEADS // HPC
GATE_OPS = 25
GATE_PARTS = 15, 17, 19, GATE_OPS
LOW_BY_POOL = 0, 1, 13, 14, 15, 16, 17
APART = 12


def window(b):
    return min(max(QB * b - HALF, 0), T - WIN)


def experts(nc, ins, hidden, out):
    ctx = ExitStack()
    with ctx:
        def sb(name, shape, dt=F32):
            return ctx.enter_context(nc.sbuf_tensor("e_" + name, shape, dt))

        def sem(name):
            return ctx.enter_context(nc.semaphore("e_" + name))

        def pair(name, shape):
            return sb(name + "_hi", shape, F32R), sb(name + "_lo", shape, F32R)

        ident = sb("ident", [P, P])
        band = sb("band", [P, 3, P])
        hmask = sb("hmask", [P, HC])
        before4, before16 = sb("before4", [P, 4, 4]), sb("before16", [P, 16, 16])
        bq, bk = sb("bq", [P, KD]), sb("bk", [P, KD])
        bv, bo = sb("bv", [P, D]), sb("bo", [P, D])
        minus_half = sb("minus_half", [P, 1])
        wq, wk, wv = pair("wq", [P, KD, D]), pair("wk", [P, KD, D]), pair("wv", [P, KD, D])
        wo = pair("wo", [P, OC, D])
        wg = pair("wg", [P, KD, EXPERTS])
        w_raw = sb("w_raw", [P, SLOTS, 3 * D])
        w13 = [pair(f"w13_{i}", [P, 2 * D]) for i in range(2)]
        w2 = [pair(f"w2_{i}", [P, D]) for i in range(3)]
        x = sb("x", [P, TT, D])
        xT = pair("xT", [P, KD, T])
        qf, kf = sb("qf", [P, KD, T]), sb("kf", [P, KD, T])
        qm = [sb(f"qm{i}", [P, HC, P]) for i in range(2)]
        vw = sb("vw", [P, NWIN, D + HD])
        s = [sb(f"s{i}", [P, HC, P]) for i in range(2)]
        pT = sb("pT", [P, HC, P])
        oT = pair("oT", [P, OC, P])
        h2, y = sb("h2", [P, TT, D]), sb("y", [P, TT, D])
        yT = pair("yT", [P, KD, T])
        yT_next = pair("yT_next", [P, KD, T])
        acc = sb("acc", [P, TT, D])
        th, act_f = sb("th", [P, T]), sb("act_f", [P, T])
        act = [pair(f"act{i}", [P, T]) for i in range(2)]
        negmax, rowsum, rinv = sb("negmax", [P, 2, HC]), sb("rowsum", [P, 2, HC]), sb("rinv", [P, 2, HC])
        st, mv, ve, rs = sb("st", [P, TT, 6]), sb("mv", [P, TT, 2]), sb("ve", [P, TT]), sb("rs", [P, TT])
        sty, mvy, vey, rsy = sb("sty", [P, TT, 6]), sb("mvy", [P, TT, 2]), sb("vey", [P, TT]), sb("rsy", [P, TT])
        g_e, g_s, g_w = sb("g_e", [P, TT, EXPERTS]), sb("g_s", [P, TT, EXPERTS]), sb("g_w", [P, TT, EXPERTS])
        g_two, g_top = sb("g_two", [P, TT * GROUPS, 6]), sb("g_top", [P, TT, GROUPS])
        g_a, g_b = sb("g_a", [P, TT, 16, 16]), sb("g_b", [P, TT, 16, 16])
        g_ok, g_okm, g_m = sb("g_ok", [P, TT * GROUPS]), sb("g_okm", [P, TT * GROUPS]), sb("g_m", [P, TT, EXPERTS])
        g_rank, g_sum = sb("g_rank", [P, TT, EXPERTS]), sb("g_sum", [P, TT])
        weight = sb("weight", [P, TT, SLOTS])

        ps_s = ctx.enter_context(nc.psum_tensor("e_ps_s", [P, HC, P], F32))
        ps_p = ctx.enter_context(nc.psum_tensor("e_ps_p", [P, HC, P], F32))
        ps_g = ctx.enter_context(nc.psum_tensor("e_ps_g", [P, T], F32))
        ps_u = ctx.enter_context(nc.psum_tensor("e_ps_u", [P, T], F32))
        ps_y = ctx.enter_context(nc.psum_tensor("e_ps_y", [P, 2, D], F32))
        ps_x = ctx.enter_context(nc.psum_tensor("e_ps_x", [P, T], F32))
        ps_y1 = [ps_y[:, :, :], ps_s[:, 4:8, :].rearrange("p (i a) t -> p i (a t)", i=2)]
        ps_q, ps_k = (ps_s[:, 4 * n:4 * n + 4, :].rearrange("p a t -> p (a t)") for n in range(2))
        ps_xT = [ps_p[:, 4 * j:4 * j + 4, :].rearrange("p (k i) t -> p k (i t)", k=KD) for j in range(2)]
        ps_v = [ps_p[:, 4 * j:4 * j + 4, :].rearrange("p (w a) t -> p w (a t)", w=2) for j in range(2)]
        ps_o = ps_x[:, 0:2 * P].rearrange("p (c t) -> p c t", c=2)
        ps_yT = ps_x[:, :].rearrange("p (k t) -> p k t", k=KD)
        ps_gate = ps_x[:, 0:TT * EXPERTS].rearrange("p (i e) -> p i e", i=TT)

        consts_in, attn_in, x_in, out_done = sem("consts_in"), sem("attn_in"), sem("x_in"), sem("out_done")
        w_in = [sem(f"w_in{g}") for g in range(3)]
        half_ready, zeros_ready, ones_ready = sem("half_ready"), sem("zeros_ready"), sem("ones_ready")
        attn_hi, attn_lo = sem("attn_hi"), sem("attn_lo")
        st_ready, mv_ready, ve_ready, rs_ready, x_ready = sem("st_ready"), sem("mv_ready"), sem("ve_ready"), sem("rs_ready"), sem("x_ready")
        hb_ready = sem("hb_ready")
        xT_ps, xT_hi, xT_lo = sem("xT_ps"), sem("xT_hi"), sem("xT_lo")
        q_ps, k_ps, q_ready, k_ready = sem("q_ps"), sem("k_ps"), sem("q_ready"), sem("k_ready")
        v_ps, v_ready = sem("v_ps"), sem("v_ready")
        qm_ready, scores, masked, negmax_ready = sem("qm_ready"), sem("scores"), sem("masked"), sem("negmax_ready")
        probs, rinv_ready, probs_ready = sem("probs"), sem("rinv_ready"), sem("probs_ready")
        pT_ps, pT_ready = sem("pT_ps"), sem("pT_ready")
        oT_ps, oT_hi, oT_lo = sem("oT_ps"), sem("oT_hi"), sem("oT_lo")
        wo_ps, h2_ready = sem("wo_ps"), sem("h2_ready")
        sty_ready, mvy_ready, vey_ready, rsy_ready, y_ready = sem("sty_ready"), sem("mvy_ready"), sem("vey_ready"), sem("rsy_ready"), sem("y_ready")
        yT_ps, yT_hi, yT_lo = sem("yT_ps"), sem("yT_hi"), sem("yT_lo")
        moved_hi, moved_lo = sem("moved_hi"), sem("moved_lo")
        gate_ps, gate_exp, gate_step = sem("gate_ps"), sem("gate_exp"), sem("gate_step")
        w13_hi, w13_lo, w2_hi, w2_lo = sem("w13_hi"), sem("w13_lo"), sem("w2_hi"), sem("w2_lo")
        g_ps, u_ps, tanh_ready, silu_ready, act_ready = sem("g_ps"), sem("u_ps"), sem("tanh_ready"), sem("silu_ready"), sem("act_ready")
        act_hi, act_lo, act_lo_pool = sem("act_hi"), sem("act_lo"), sem("act_lo_pool")
        y_ps, acc_ready = sem("y_ps"), sem("acc_ready")

        def wait(eng, sm, value):
            if not isinstance(value, int) or value > 0:
                eng.wait_ge(sm, value)

        def wait_act_low(eng, v, e):
            mine = [k for k in range(SLOTS) if (k in LOW_BY_POOL) == (e in LOW_BY_POOL)]
            eng.wait_ge(act_lo_pool if e in LOW_BY_POOL else act_lo, len(mine) * v + mine.index(e) + 1)

        def take_act_low(eng, v, e):
            eng.wait_ge(act_hi, 18 * v + e + 1)
            hi, lo = act[e % 2]
            eng.tensor_tensor(lo[:, :], act_f[:, :], hi[:, :].bitcast(F32), ALU.subtract).then_inc(act_lo_pool if e in LOW_BY_POOL else act_lo, 1)

        def schedule(eng, begin, slots, end):
            begin()
            slots(0, -1, True, False, True)
            end(0, -1, True, False, True)
            with eng.Fori(0, BATCH - 2) as v:
                slots(v + 1, v, True, True, True)
                end(v + 1, v, True, True, True)
            slots(BATCH - 1, BATCH - 2, True, True, False)
            end(BATCH - 1, BATCH - 2, True, True, False)
            slots(BATCH, BATCH - 1, False, True, False)
            end(BATCH, BATCH - 1, False, True, False)

        block = ctx.enter_context(nc.Block())

        @block.sync
        def _(sp):
            def load_x(w):
                sp.dma_start(x[:, :, :], hidden[bass.ds(w, 1), :, :, :].rearrange("b p t d -> p (b t) d")).then_inc(x_in, 16)

            load_x(0)
            for dst, name in ((ident[:, :], "ident"), (band[:, :, :], "band"), (hmask[:, :], "hmask"),
                              (before4[:, :, :], "before4"), (before16[:, :, :], "before16"),
                              (bq[:, :], "bq"), (bk[:, :], "bk"), (bv[:, :], "bv"), (bo[:, :], "bo")):
                src = ins[name] if name not in ("bv", "bo") else ins[name].broadcast_to([P, D])
                sp.dma_start(dst, src).then_inc(consts_in, 16)
            for dst, name in ((s[0][:, 0:4, :], "wq"), (s[0][:, 4:8, :], "wk"), (s[1][:, 0:4, :], "wv"),
                              (pT[:, :, :], "wo"), (s[1][:, 4, 0:2 * EXPERTS], "wg")):
                sp.dma_start(dst if name == "wg" else dst.rearrange("p a t -> p (a t)"), ins[name]).then_inc(attn_in, 16)
            for g in range(3):
                sp.dma_start(w_raw[:, 6 * g:6 * g + 6, :], ins["moe"][:, 6 * g:6 * g + 6, :]).then_inc(w_in[g], 16)
            sp.wait_ge(hb_ready, 1)
            sp.wait_ge(xT_ps, 2)
            load_x(1)
            with sp.Fori(0, BATCH - 2) as v:
                sp.wait_ge(hb_ready, v + 2)
                sp.wait_ge(xT_ps, 2 * v + 4)
                load_x(v + 2)
                sp.wait_ge(acc_ready, 72 * v + 72)
                sp.dma_start(out[bass.ds(v, 1), :, :].rearrange("b (t p) d -> p (b t) d", p=P), acc[:, :, :]).then_inc(out_done, 16)
            for v in (BATCH - 2, BATCH - 1):
                sp.wait_ge(acc_ready, 72 * v + 72)
                sp.dma_start(out[v, :, :].rearrange("(t p) d -> p t d", p=P), acc[:, :, :]).then_inc(out_done, 16)
            sp.wait_ge(out_done, 16 * BATCH)

        @block.gpsimd
        def _(pool):
            pool.memset(minus_half[:, :], -0.5).then_inc(half_ready, 1)
            pool.memset(vw[:, :, D:D + HD], 0.0).then_inc(zeros_ready, 1)
            pool.memset(weight[:, :, 0:SHARED], 1.0).then_inc(ones_ready, 1)
            pool.wait_ge(half_ready, 1)

            def rstd(w, i):
                pool.wait_ge(ve_ready, 4 * w + i + 1)
                pool.tensor_tensor(rs[:, i:i + 1], ve[:, i:i + 1], minus_half[:, :], ALU.pow).then_inc(rs_ready, 1)

            def rstd_y(w, i):
                pool.wait_ge(vey_ready, 4 * w + i + 1)
                pool.tensor_tensor(rsy[:, i:i + 1], vey[:, i:i + 1], minus_half[:, :], ALU.pow).then_inc(rsy_ready, 1)

            def add_bo(w):
                if isinstance(w, int) and w == 0:
                    pool.wait_ge(x_in, 16)
                    pool.wait_ge(consts_in, 16 * 9)
                else:
                    pool.wait_ge(x_in, 16 * w + 16)
                    pool.wait_ge(acc_ready, 72 * w - 68)
                pool.tensor_tensor(h2[:, :, :], x[:, :, :], bo[:, :].unsqueeze(1).broadcast_to([P, TT, D]), ALU.add).then_inc(hb_ready, 1)

            def mask_q(w, n):
                i, c = n // 2, n % 2
                pool.wait_ge(q_ready, 2 * w + 2)
                wait(pool, scores, 8 * w + n - 1)
                pool.tensor_tensor(qm[n % 2][:, :, :], qf[:, c, i * P:(i + 1) * P].unsqueeze(1).broadcast_to([P, HC, P]),
                                   hmask[:, :].unsqueeze(2).broadcast_to([P, HC, P]), ALU.mult).then_inc(qm_ready, 1)

            def normalize(w, n):
                pool.wait_ge(rinv_ready, 8 * w + n + 1)
                pool.tensor_tensor(s[n % 2][:, :, :], s[n % 2][:, :, :], rinv[:, n % 2, :].unsqueeze(2).broadcast_to([P, HC, P]),
                                   ALU.mult).then_inc(probs_ready, 1)

            def w_low(v, e):
                hi, lo = w13[e % 2]
                pool.wait_ge(w13_hi, 18 * v + e + 1)
                pool.tensor_tensor(lo[:, :], w_raw[:, e, 0:2 * D], hi[:, :].bitcast(F32), ALU.subtract).then_inc(w13_lo, 1)
                hi, lo = w2[e % 3]
                pool.wait_ge(w2_hi, 18 * v + e + 1)
                pool.tensor_tensor(lo[:, :], w_raw[:, e, 2 * D:3 * D], hi[:, :].bitcast(F32), ALU.subtract).then_inc(w2_lo, 1)

            def slots(w, v, attn, moe, more):
                for k in range(SLOTS):
                    if moe and k + 1 < SLOTS:
                        w_low(v, k + 1)
                    if moe and k in LOW_BY_POOL:
                        take_act_low(pool, v, k)
                    if attn:
                        if k == 2:
                            add_bo(w)
                        if 0 <= k - 2 < UNITS:
                            mask_q(w, k - 2)
                        if k in (8, 10, 12, 14):
                            rstd_y(w, (k - 8) // 2)
                        if more and 0 <= k - 11 < TT:
                            rstd(w + 1, k - 11)
                        if 0 <= k - 4 < UNITS:
                            normalize(w, k - 4)

            def begin():
                for i in range(TT):
                    rstd(0, i)

            def end(w, v, attn, moe, more):
                if attn:
                    w_low(w, 0)

            schedule(pool, begin, slots, end)

        @block.scalar
        def _(act_e):
            def split_attention():
                act_e.wait_ge(attn_in, 16 * 5)
                for (hi, _), src in ((wq, s[0][:, 0:4, :]), (wk, s[0][:, 4:8, :]), (wv, s[1][:, 0:4, :]), (wo, pT[:, :, :])):
                    act_e.activation(hi[:, :, :].rearrange("p a b -> p (a b)"), src.rearrange("p a b -> p (a b)"), ACT.Copy).then_inc(attn_hi, 1)
                act_e.activation(wg[0][:, :, :].rearrange("p a b -> p (a b)"), s[1][:, 4, 0:2 * EXPERTS], ACT.Copy).then_inc(attn_hi, 1)

            def w_high(v, e):
                act_e.wait_ge(w_in[e // 6], 16)
                wait(act_e, u_ps, 18 * v + e - 1)
                act_e.activation(w13[e % 2][0][:, :], w_raw[:, e, 0:2 * D], ACT.Copy).then_inc(w13_hi, 1)
                wait(act_e, y_ps, 36 * v + (2 * e - 4 if e == 0 else max(2 * e - 4, 0)))
                act_e.activation(w2[e % 3][0][:, :], w_raw[:, e, 2 * D:3 * D], ACT.Copy).then_inc(w2_hi, 1)

            def tanh(v, e):
                act_e.wait_ge(g_ps, 18 * v + e + 1)
                wait(act_e, act_ready, 18 * v + e)
                act_e.activation(th[:, :], ps_g[:, :], ACT.Tanh, scale=0.5).then_inc(tanh_ready, 1)

            def act_high(v, e):
                act_e.wait_ge(act_ready, 18 * v + e + 1)
                wait(act_e, y_ps, 36 * v + max(2 * e - 2, 0))
                act_e.activation(act[e % 2][0][:, :], act_f[:, :], ACT.Copy).then_inc(act_hi, 1)

            def xT_high(w, j):
                act_e.wait_ge(xT_ps, 2 * w + j + 1)
                wait(act_e, v_ps, 4 * w)
                act_e.activation(xT[0][:, :, 2 * j * P:(2 * j + 2) * P], ps_xT[j], ACT.Copy).then_inc(xT_hi, 1)

            def qk(w, c):
                act_e.wait_ge(q_ps, 2 * w + c + 1)
                act_e.activation(qf[:, c, :], ps_q, ACT.Identity, bias=bq[:, c:c + 1]).then_inc(q_ready, 1)
                act_e.wait_ge(k_ps, 2 * w + c + 1)
                act_e.activation(kf[:, c, :], ps_k, ACT.Identity, bias=bk[:, c:c + 1]).then_inc(k_ready, 1)

            def exp(w, n, half):
                if half == 0:
                    act_e.wait_ge(negmax_ready, 8 * w + n + 1)
                for h in range(4 * half, 4 * half + 4):
                    m = act_e.activation(s[n % 2][:, h, :], s[n % 2][:, h, :], ACT.Exp, bias=negmax[:, n % 2, h:h + 1],
                                         accum_out=rowsum[:, n % 2, h:h + 1])
                if half == 1:
                    m.then_inc(probs, 1)

            def pT_copy(w, n):
                act_e.wait_ge(pT_ps, 8 * w + n + 1)
                wait(act_e, oT_ps, 8 * w + n)
                act_e.activation(pT[:, :, :], ps_p[:, :, :], ACT.Copy).then_inc(pT_ready, 1)

            def oT_high(w, n):
                act_e.wait_ge(oT_ps, 8 * w + n + 1)
                wait(act_e, wo_ps, 4 * w + n // 2)
                c = n % 2
                act_e.activation(oT[0][:, 2 * c:2 * c + 2, :], ps_o, ACT.Copy).then_inc(oT_hi, 1)

            def yT_high(w, j):
                act_e.wait_ge(yT_ps, 2 * w + j + 1)
                act_e.activation(yT_next[0][:, :, 2 * j * P:(2 * j + 2) * P], ps_yT, ACT.Copy).then_inc(yT_hi, 1)

            def move(w):
                wait(act_e, u_ps, 18 * w)
                act_e.activation(yT[0][:, :, :], yT_next[0][:, :, :].bitcast(F32), ACT.Copy).then_inc(moved_hi, 1)

            def gate_exp_of(w):
                act_e.wait_ge(gate_ps, w + 1)
                wait(act_e, gate_step, GATE_OPS * w)
                act_e.activation(g_e[:, :, :], ps_gate, ACT.Exp, scale=-1.0).then_inc(gate_exp, 1)

            def slots(w, v, attn, moe, more):
                for k in range(SLOTS):
                    if attn:
                        if 0 <= k - 7 < UNITS:
                            oT_high(w, k - 7)
                        if 0 <= k - 6 < UNITS:
                            pT_copy(w, k - 6)
                    if moe:
                        if k + 1 < SLOTS:
                            w_high(v, k + 1)
                        tanh(v, k)
                    if attn and k in (12, 15):
                        yT_high(w, (k - 12) // 3)
                    if attn and 0 <= k - 4 < UNITS:
                        exp(w, k - 4, 0)
                    if moe:
                        act_high(v, k)
                    if attn:
                        if 0 <= k - 4 < UNITS:
                            exp(w, k - 4, 1)
                        if k in (0, 1):
                            qk(w, k)
                        if k == 15:
                            gate_exp_of(w)
                        if k == 17 and more:
                            xT_high(w + 1, 0)
                            xT_high(w + 1, 1)

            def end(w, v, attn, moe, more):
                if attn:
                    w_high(w, 0)
                    move(w)

            def begin():
                xT_high(0, 0)
                xT_high(0, 1)

            split_attention()
            schedule(act_e, begin, slots, end)

        @block.vector
        def _(dve):
            def split_attention():
                for n, ((hi, lo), src) in enumerate(((wq, s[0][:, 0:4, :]), (wk, s[0][:, 4:8, :]), (wv, s[1][:, 0:4, :]), (wo, pT[:, :, :]))):
                    dve.wait_ge(attn_hi, n + 1)
                    dve.tensor_tensor(lo[:, :, :].rearrange("p a b -> p (a b)"), src.rearrange("p a b -> p (a b)"),
                                      hi[:, :, :].rearrange("p a b -> p (a b)").bitcast(F32), ALU.subtract).then_inc(attn_lo, 1)
                dve.wait_ge(attn_hi, 5)
                dve.tensor_tensor(wg[1][:, :, :].rearrange("p a b -> p (a b)"), s[1][:, 4, 0:2 * EXPERTS],
                                  wg[0][:, :, :].rearrange("p a b -> p (a b)").bitcast(F32), ALU.subtract).then_inc(attn_lo, 1)

            def x_stats(w, i):
                n = 4 * w + i + 1
                dve.wait_ge(x_in, 16 * w + 16)
                dve.bn_stats(st[:, i, :], x[:, i, :]).then_inc(st_ready, 1)
                dve.wait_ge(st_ready, n)
                dve.memset(ve[:, i:i + 1], EPS)
                dve.bn_aggr(mv[:, i, :], st[:, i, :]).then_inc(mv_ready, 1)
                dve.wait_ge(mv_ready, n)
                dve.tensor_tensor(ve[:, i:i + 1], mv[:, i, 1:2], ve[:, i:i + 1], ALU.add).then_inc(ve_ready, 1)

            def x_norm(w, i):
                dve.wait_ge(rs_ready, 4 * w + i + 1)
                wait(dve, yT_ps, 2 * w)
                dve.tensor_scalar(y[:, i, :], x[:, i, :], mv[:, i, 0:1], rs[:, i:i + 1], ALU.subtract, ALU.mult).then_inc(x_ready, 1)

            def xT_low(w, j):
                dve.wait_ge(xT_hi, 2 * w + j + 1)
                sl = slice(2 * j * P, (2 * j + 2) * P)
                dve.tensor_tensor(xT[1][:, :, sl], ps_xT[j], xT[0][:, :, sl].bitcast(F32), ALU.subtract).then_inc(xT_lo, 1)

            def values(w, m):
                if m == 0:
                    wait(dve, oT_ps, 8 * w)
                    dve.wait_ge(zeros_ready, 1)
                dve.wait_ge(v_ps, 4 * w + m + 1)
                dve.tensor_tensor(vw[:, 2 * m:2 * m + 2, 0:D], ps_v[m % 2], bv[:, :].unsqueeze(1).broadcast_to([P, 2, D]), ALU.add).then_inc(v_ready, 1)

            def mask_scores(w, n):
                i = n // 2
                dve.wait_ge(scores, 8 * w + n + 1)
                wait(dve, pT_ps, 8 * w + n - 1)
                kind = 0 if i == 0 else 2 if i == TT - 1 else 1
                dve.tensor_tensor(s[n % 2][:, :, :], ps_s[:, :, :], band[:, kind, :].unsqueeze(1).broadcast_to([P, HC, P]), ALU.add).then_inc(masked, 1)

            def neg_max(w, n):
                dve.wait_ge(masked, 8 * w + n + 1)
                dve.tensor_reduce(negmax[:, n % 2, :], s[n % 2][:, :, :], AX_X, ALU.max, negate=True).then_inc(negmax_ready, 1)

            def inverse(w, n):
                dve.wait_ge(probs, 8 * w + n + 1)
                wait(dve, probs_ready, 8 * w + n - 1)
                dve.reciprocal(rinv[:, n % 2, :], rowsum[:, n % 2, :]).then_inc(rinv_ready, 1)

            def oT_low(w, n):
                dve.wait_ge(oT_hi, 8 * w + n + 1)
                c = n % 2
                dve.tensor_tensor(oT[1][:, 2 * c:2 * c + 2, :], ps_o, oT[0][:, 2 * c:2 * c + 2, :].bitcast(F32), ALU.subtract).then_inc(oT_lo, 1)

            def residual(w, i):
                dve.wait_ge(wo_ps, 4 * w + i + 1)
                dve.wait_ge(hb_ready, w + 1)
                dve.tensor_tensor(h2[:, i, :], ps_x[:, 0:D], h2[:, i, :], ALU.add).then_inc(h2_ready, 1)

            def y_stats(w, i):
                n = 4 * w + i + 1
                dve.wait_ge(h2_ready, n)
                dve.bn_stats(sty[:, i, :], h2[:, i, :]).then_inc(sty_ready, 1)
                dve.wait_ge(sty_ready, n)
                dve.memset(vey[:, i:i + 1], EPS)
                dve.bn_aggr(mvy[:, i, :], sty[:, i, :]).then_inc(mvy_ready, 1)
                dve.wait_ge(mvy_ready, n)
                dve.tensor_tensor(vey[:, i:i + 1], mvy[:, i, 1:2], vey[:, i:i + 1], ALU.add).then_inc(vey_ready, 1)

            def y_norm(w, i):
                dve.wait_ge(rsy_ready, 4 * w + i + 1)
                dve.tensor_scalar(y[:, i, :], h2[:, i, :], mvy[:, i, 0:1], rsy[:, i:i + 1], ALU.subtract, ALU.mult).then_inc(y_ready, 1)

            def yT_low(w, j):
                dve.wait_ge(yT_hi, 2 * w + j + 1)
                hi, lo = (yT_next[n][:, :, 2 * j * P:(2 * j + 2) * P] for n in range(2))
                dve.tensor_tensor(lo, ps_yT, hi.bitcast(F32), ALU.subtract).then_inc(yT_lo, 1)

            def move(w):
                wait(dve, u_ps, 18 * w)
                dve.tensor_copy(yT[1][:, :, :], yT_next[1][:, :, :].bitcast(F32)).then_inc(moved_lo, 1)

            def silu(v, e):
                n = 18 * v + e + 1
                dve.wait_ge(tanh_ready, n)
                dve.scalar_tensor_tensor(out=th[:, :], in0=th[:, :], scalar=1.0, in1=ps_g[:, :], op0=ALU.add, op1=ALU.mult).then_inc(silu_ready, 1)

            def times_u(v, e):
                n = 18 * v + e + 1
                if e - 1 in LOW_BY_POOL:
                    wait_act_low(dve, v, e - 1)
                elif e == 0:
                    dve.wait_ge(act_lo_pool, len(LOW_BY_POOL) * v)
                dve.wait_ge(silu_ready, n)
                dve.wait_ge(u_ps, n)
                dve.scalar_tensor_tensor(out=act_f[:, :], in0=th[:, :], scalar=0.5, in1=ps_u[:, :], op0=ALU.mult, op1=ALU.mult).then_inc(act_ready, 1)

            def add_expert(v, e, j):
                dve.wait_ge(y_ps, 36 * v + 2 * e + j + 1)
                if e == 0 and j == 0:
                    dve.wait_ge(ones_ready, 1)
                    wait(dve, out_done, 16 * v)
                if e == SHARED and j == 0:
                    dve.wait_ge(gate_step, GATE_OPS * v + GATE_OPS)
                for i in (2 * j, 2 * j + 1):
                    if e > 0:
                        dve.wait_ge(acc_ready, 72 * v + 4 * e - 4 + i + 1)
                    bank = ps_y1[e + 1 >= APART] if j == 1 else ps_y
                    dve.scalar_tensor_tensor(out=acc[:, i, :], in0=bank[:, i % 2, :], scalar=weight[:, i, e:e + 1],
                                             in1=h2[:, i, :] if e == 0 else acc[:, i, :], op0=ALU.mult, op1=ALU.add).then_inc(acc_ready, 1)

            def gate(w, part):
                done = [0 if part == 0 else GATE_PARTS[part - 1]]

                def then(ins, last=False):
                    done[0] += 1
                    ins.then_inc(gate_step, 1)
                    if not last:
                        dve.wait_ge(gate_step, GATE_OPS * w + done[0])

                def ranks(out_, scores_, before, size, which=(0, 1, 2)):
                    g = g_a[:, :, 0:size, 0:size]
                    e = g_b[:, :, 0:size, 0:size]
                    other = scores_.unsqueeze(2).broadcast_to([P, TT, size, size])
                    own = scores_.unsqueeze(3).broadcast_to([P, TT, size, size])
                    if 0 in which:
                        then(dve.tensor_tensor(g, other, own, ALU.is_gt))
                        then(dve.tensor_tensor(e, other, own, ALU.is_ge))
                    if 1 in which:
                        then(dve.tensor_tensor(e, e, before.unsqueeze(1).broadcast_to([P, TT, size, size]), ALU.mult))
                        then(dve.tensor_tensor(g, g, e, ALU.max))
                    if 2 in which:
                        then(dve.tensor_reduce(out_, g, AX_X, ALU.add))

                if part == 0:
                    dve.wait_ge(gate_exp, w + 1)
                    then(dve.tensor_scalar(g_e[:, :, :], g_e[:, :, :], 1.0, None, ALU.add))
                    then(dve.reciprocal(g_s[:, :, :], g_e[:, :, :]))
                    four = g_s[:, :, :].rearrange("p i (g e) -> p (i g) e", e=4)
                    then(dve.tensor_tensor(g_two[:, :, 0:3], four[:, :, 0:3], four[:, :, 1:4], ALU.add))
                    then(dve.tensor_tensor(g_two[:, :, 3:5], four[:, :, 0:2], four[:, :, 2:4], ALU.add))
                    then(dve.tensor_tensor(g_two[:, :, 5:6], four[:, :, 0:1], four[:, :, 3:4], ALU.add))
                    then(dve.tensor_reduce(g_top[:, :, :].rearrange("p i g -> p (i g)"), g_two[:, :, :], AX_X, ALU.max))
                    ranks(g_rank[:, :, 0:GROUPS], g_top[:, :, :], before4[:, :, :], GROUPS)
                    ok3 = g_ok[:, :].rearrange("p (i g) -> p i g", i=TT)
                    then(dve.tensor_scalar(ok3, g_rank[:, :, 0:GROUPS], float(TOP_GROUPS), None, ALU.is_lt))
                    then(dve.tensor_scalar(g_okm[:, :], g_ok[:, :], 1.0, None, ALU.subtract))
                    m4 = g_m[:, :, :].rearrange("p i (g e) -> p (i g) e", e=4)
                    then(dve.tensor_tensor(m4, four, g_ok[:, :].unsqueeze(2).broadcast_to([P, TT * GROUPS, 4]), ALU.mult))
                    then(dve.tensor_tensor(m4, m4, g_okm[:, :].unsqueeze(2).broadcast_to([P, TT * GROUPS, 4]), ALU.add))
                else:
                    ranks(g_rank[:, :, :], g_m[:, :, :], before16[:, :, :], EXPERTS, (part - 1,))
                if part == 3:
                    then(dve.scalar_tensor_tensor(out=g_w[:, :, :], in0=g_rank[:, :, :], scalar=float(TOP), in1=g_s[:, :, :],
                                                  op0=ALU.is_lt, op1=ALU.mult))
                    then(dve.tensor_reduce(g_sum[:, :], g_w[:, :, :], AX_X, ALU.add))
                    then(dve.tensor_scalar(g_sum[:, :], g_sum[:, :], 1e-6, None, ALU.add))
                    then(dve.reciprocal(g_sum[:, :], g_sum[:, :]))
                    ins = dve.tensor_tensor(weight[:, :, SHARED:SLOTS], g_w[:, :, :],
                                            g_sum[:, :].unsqueeze(2).broadcast_to([P, TT, EXPERTS]), ALU.mult)
                    then(ins, last=True)
                assert done[0] == GATE_PARTS[part], done[0]

            def slots(w, v, attn, moe, more):
                for k in range(SLOTS):
                    if moe and k == 0:
                        gate(v, 1)
                        gate(v, 2)
                    if moe and 2 <= k <= APART:
                        add_expert(v, k - 2, 1)
                    if attn:
                        if 0 <= k - 7 < UNITS:
                            oT_low(w, k - 7)
                        if k in (9, 11, 13, 15):
                            y_norm(w, (k - 9) // 2)
                    if moe:
                        silu(v, k)
                    if attn and k in (12, 15):
                        yT_low(w, (k - 12) // 3)
                    if moe:
                        if k > APART:
                            add_expert(v, k - 2, 1)
                        times_u(v, k)
                        if k >= 1:
                            add_expert(v, k - 1, 0)
                        if k not in LOW_BY_POOL:
                            take_act_low(dve, v, k)
                    if attn:
                        if k in (8, 10, 12, 14):
                            residual(w, (k - 8) // 2)
                        if not moe and 0 <= k - 4 < UNITS:
                            inverse(w, k - 4)
                        if 0 <= k - 3 < UNITS:
                            mask_scores(w, k - 3)
                        if k in (8, 10, 12, 14):
                            y_stats(w, (k - 8) // 2)
                        if 0 <= k - 3 < UNITS:
                            neg_max(w, k - 3)
                        if moe and 0 <= k - 4 < UNITS:
                            inverse(w, k - 4)
                        if k in (1, 2):
                            values(w, 2 * k - 2)
                            values(w, 2 * k - 1)
                        if more and 0 <= k - 11 < TT:
                            x_stats(w + 1, k - 11)
                        if k == 16 and more:
                            for i in range(TT):
                                x_norm(w + 1, i)
                        if k == 15:
                            gate(w, 0)
                        if k == 17 and more:
                            xT_low(w + 1, 0)
                            xT_low(w + 1, 1)
                    if moe and k == 0:
                        gate(v, 3)

            def end(w, v, attn, moe, more):
                if moe:
                    add_expert(v, SLOTS - 2, 1)
                if attn:
                    move(w)
                if moe:
                    add_expert(v, SLOTS - 1, 0)
                if moe:
                    add_expert(v, SLOTS - 1, 1)

            def begin():
                for i in range(TT):
                    x_stats(0, i)
                for i in range(TT):
                    x_norm(0, i)
                xT_low(0, 0)
                xT_low(0, 1)

            split_attention()
            schedule(dve, begin, slots, end)

        @block.tensor
        def _(pe):
            def up(v, e, which):
                hi, lo = w13[e % 2]
                if which == 0:
                    if e == 0:
                        pe.wait_ge(moved_hi, v + 1)
                        pe.wait_ge(moved_lo, v + 1)
                    pe.wait_ge(w13_lo, 18 * v + e + 1)
                    wait(pe, silu_ready, 18 * v + e)
                else:
                    wait(pe, act_ready, 18 * v + e)
                bank, done = ((ps_g, g_ps), (ps_u, u_ps))[which]
                for k in range(KD):
                    c = (2 * which + k) * P
                    m = passes(pe, bank[:, :], (hi[:, c:c + P], lo[:, c:c + P]), (yT[0][:, k, :], yT[1][:, k, :]), k == 0, k == KD - 1)
                m.then_inc(done, 1)

            def down(v, e, j, attn=False):
                hi, lo = w2[e % 3]
                if j == 0:
                    wait_act_low(pe, v, e)
                    pe.wait_ge(w2_lo, 18 * v + e + 1)
                if j == 0:
                    pe.wait_ge(acc_ready, 72 * v + (4 * e - 2 if e >= APART else 4 * e))
                elif e + 1 > APART:
                    pe.wait_ge(acc_ready, 72 * v + 4 * e)
                elif e + 1 < APART:
                    pe.wait_ge(acc_ready, 72 * v + 4 * e + 2)
                elif attn:
                    pe.wait_ge(masked, 8 * v + 16)
                bank = ps_y1[e + 1 >= APART] if j == 1 else ps_y
                for i in (2 * j, 2 * j + 1):
                    sl = slice(i * P, (i + 1) * P)
                    m = passes(pe, bank[:, i % 2, :], (act[e % 2][0][:, sl], act[e % 2][1][:, sl]), (hi[:, :], lo[:, :]))
                m.then_inc(y_ps, 1)

            def turn(src, j, bank):
                for k in range(KD):
                    for i in range(2):
                        m = pe.transpose(bank[:, k, i * P:(i + 1) * P], src[:, 2 * j + i, k * P:(k + 1) * P], ident[:, :])
                return m

            def turn_x(w, j):
                pe.wait_ge(x_ready, 4 * w + 2 * j + 2)
                wait(pe, pT_ready, 8 * w)
                turn(y, j, ps_xT[j]).then_inc(xT_ps, 1)

            def project(w, c):
                if c == 0:
                    pe.wait_ge(xT_lo, 2 * w + 2)
                    pe.wait_ge(attn_lo, 5)
                    wait(pe, masked, 8 * w)
                wait(pe, q_ready, 2 * w + c)
                wait(pe, k_ready, 2 * w + c)
                for (hi, lo), bank, done in ((wq, ps_q, q_ps), (wk, ps_k, k_ps)):
                    if c == 0 and bank is ps_k:
                        wait(pe, acc_ready, 72 * w - 72)
                    for k in range(KD):
                        m = passes(pe, bank, (hi[:, k, c * P:(c + 1) * P], lo[:, k, c * P:(c + 1) * P]), (xT[0][:, k, :], xT[1][:, k, :]), k == 0, k == KD - 1)
                    m.then_inc(done, 1)

            def values(w, n):
                wait(pe, v_ready, 4 * w + n - 1)
                for b in (2 * n, 2 * n + 1):
                    sl = slice(window(b), window(b) + WIN)
                    for k in range(KD):
                        m = passes(pe, ps_v[n % 2][:, b % 2, :], (xT[0][:, k, sl], xT[1][:, k, sl]), (wv[0][:, k, :], wv[1][:, k, :]), k == 0, k == KD - 1)
                m.then_inc(v_ps, 1)

            def score(w, n):
                i, c = n // 2, n % 2
                pe.wait_ge(qm_ready, 8 * w + n + 1)
                if n == 0:
                    pe.wait_ge(k_ready, 2 * w + 2)
                wait(pe, masked, 8 * w + n)
                for h in range(HC):
                    for b in range(2):
                        first = window(2 * i + b)
                        m = pe.matmul(ps_s[QB * b:QB * b + QB, h, :], qm[n % 2][:, h, QB * b:QB * b + QB], kf[:, c, first:first + WIN], start=True, stop=True)
                m.then_inc(scores, 1)

            def turn_probs(w, n):
                pe.wait_ge(probs_ready, 8 * w + n + 1)
                if n == 0:
                    pe.wait_ge(v_ready, 4 * w + 4)
                wait(pe, pT_ready, 8 * w + n)
                for h in range(HC):
                    m = pe.transpose(ps_p[:, h, :], s[n % 2][:, h, :], ident[:, :])
                m.then_inc(pT_ps, 1)

            def mix(w, n):
                i, c = n // 2, n % 2
                pe.wait_ge(pT_ready, 8 * w + n + 1)
                bank_x_free(w, n)
                for h in range(HC):
                    head = HC * c + h
                    for b in range(2):
                        m = pe.matmul(ps_o[32 * (h % HPC):32 * (h % HPC) + 32, h // HPC, QB * b:QB * b + QB],
                                      vw[:, 2 * i + b, HD * head:HD * head + 32], pT[:, h, QB * b:QB * b + QB], start=True, stop=True,
                                      skip_group_check=True)
                m.then_inc(oT_ps, 1)

            def bank_x_free(w, n):
                wait(pe, oT_lo, 8 * w + n)
                if n >= 2 and n % 2 == 0:
                    pe.wait_ge(h2_ready, 4 * w + n // 2)
                if n == 0:
                    wait(pe, gate_exp, w)

            def project_out(w, i):
                pe.wait_ge(oT_lo, 8 * w + 2 * i + 2)
                if i == 2:
                    pe.wait_ge(yT_lo, 2 * w + 1)
                for c in range(OC):
                    m = passes(pe, ps_x[:, 0:D], (oT[0][:, c, :], oT[1][:, c, :]), (wo[0][:, c, :], wo[1][:, c, :]), c == 0, c == OC - 1)
                m.then_inc(wo_ps, 1)

            def turn_y(w, j):
                pe.wait_ge(y_ready, 4 * w + 2 * j + 2)
                if j == 0:
                    pe.wait_ge(oT_lo, 8 * w + 6)
                turn(y, j, ps_yT).then_inc(yT_ps, 1)

            def logits(w):
                pe.wait_ge(yT_lo, 2 * w + 2)
                for i in range(TT):
                    sl = slice(i * P, (i + 1) * P)
                    for k in range(KD):
                        m = passes(pe, ps_gate[:, i, :], (yT_next[0][:, k, sl], yT_next[1][:, k, sl]), (wg[0][:, k, :], wg[1][:, k, :]), k == 0, k == KD - 1)
                m.then_inc(gate_ps, 1)

            def slots(w, v, attn, moe, more):
                for k in range(SLOTS):
                    if attn and k == 0:
                        project(w, 0)
                    if moe:
                        up(v, k, 0)
                    if attn and k in (12, 15):
                        turn_y(w, (k - 12) // 3)
                    if moe:
                        up(v, k, 1)
                        if k >= 1:
                            down(v, k - 1, 0)
                    if attn:
                        if k == 1:
                            project(w, 1)
                        if k in (1, 2):
                            values(w, 2 * k - 2)
                            values(w, 2 * k - 1)
                        if 0 <= k - 5 < UNITS:
                            turn_probs(w, k - 5)
                        if k in (8, 10, 12, 14):
                            project_out(w, (k - 8) // 2)
                        if 0 <= k - 3 < UNITS:
                            score(w, k - 3)
                        if 0 <= k - 6 < UNITS:
                            mix(w, k - 6)
                        if k == 15:
                            logits(w)
                        if k == 17 and more:
                            turn_x(w + 1, 0)
                            turn_x(w + 1, 1)
                    if moe and k >= 1:
                        down(v, k - 1, 1, attn)

            def end(w, v, attn, moe, more):
                if moe:
                    down(v, SLOTS - 1, 0)
                    down(v, SLOTS - 1, 1)

            def begin():
                turn_x(0, 0)
                turn_x(0, 1)

            pe.wait_ge(consts_in, 16 * 9)
            schedule(pe, begin, slots, end)


def mixed_lm_kernel(nc, ins, out):
    hidden = nc.dram_tensor("hidden", [BATCH, P, TT, D], F32)
    with nc.sbuf_tensor("state", [P, BATCH, TT, D], F32) as state:
        encoder(nc, ins, state, hidden)
    experts(nc, ins, hidden, out)


def layout(x, _lenS, L0_tok_embed, L0_tok_ln1_g, L0_tok_ln1_b, L0_tok_ln2_g, L0_tok_ln2_b, L0_tok_W1, L0_tok_b1,
           L0_tok_W2, L0_tok_b2, L0_attn_Wq, L0_attn_bq, L0_attn_Wk, L0_attn_bk, L0_attn_Wv, L0_attn_bv, L0_attn_Wo,
           L0_attn_bo, L0_ffn_w_gate, L0_ffn_w1_e, L0_ffn_w3_e, L0_ffn_w2_e, L0_ffn_w1_s, L0_ffn_w3_s, L0_ffn_w2_s):
    def by_rows(w):
        return w.reshape(-1, P, w.shape[1]).transpose(1, 0, 2).reshape(P, -1)

    def up(w):
        return w.reshape(-1, P, KD, P).transpose(3, 0, 2, 1).reshape(P, -1, D)

    wo = np.zeros((OC, HPC, 32, D), np.float32)
    wo[:, :, :HD] = L0_attn_Wo.reshape(OC, HPC, HD, D)
    w1 = np.concatenate([L0_ffn_w1_s.reshape(2, P, D), L0_ffn_w1_e])
    w3 = np.concatenate([L0_ffn_w3_s.reshape(2, P, D), L0_ffn_w3_e])
    w2 = np.concatenate([L0_ffn_w2_s.reshape(D, 2, P).transpose(1, 0, 2), L0_ffn_w2_e])
    arrays = {
        "x": x.reshape(BATCH * TT, P).T, "embed": L0_tok_embed,
        "ln1_g": L0_tok_ln1_g, "ln1_b": L0_tok_ln1_b, "ln2_g": L0_tok_ln2_g, "ln2_b": L0_tok_ln2_b,
        "w1": L0_tok_W1, "w2": L0_tok_W2, "b1": L0_tok_b1.reshape(LAYERS, KF, P).transpose(0, 2, 1), "b2": L0_tok_b2,
        "wq": by_rows(L0_attn_Wq), "wk": by_rows(L0_attn_Wk), "wv": by_rows(L0_attn_Wv),
        "wo": by_rows(wo.reshape(OC * P, D)), "wg": by_rows(L0_ffn_w_gate.T),
        "bq": L0_attn_bq.reshape(KD, P).T, "bk": L0_attn_bk.reshape(KD, P).T, "bv": L0_attn_bv[None], "bo": L0_attn_bo[None],
        "moe": np.concatenate([up(w1), up(w3), w2.transpose(2, 0, 1)], axis=2),
    }

    i = np.arange(D, dtype=np.float32)
    t = np.arange(T, dtype=np.float32)[:, None]
    f = np.float32
    sin = np.sin(t / f(10) ** (f(4) * i / f(D)))
    cos = np.cos(t / f(10) ** (f(4) * (i - f(1)) / f(D)))
    arrays["pos"] = np.where(np.arange(D) % 2 == 0, sin, cos).astype(np.float32)
    arrays["ident"] = np.eye(P, dtype=np.float32)
    band = np.zeros((P, 3, P), np.float32)
    for kind, tile in enumerate((0, 1, TT - 1)):
        for b in range(2):
            q = QB * (2 * tile + b) + np.arange(QB)[:, None]
            k = window(2 * tile + b) + np.arange(WIN)[None, :]
            band[QB * b:QB * b + QB, kind] = np.where(np.abs(q - k) <= HALF, 0.0, -1e30)
    arrays["band"] = band
    arrays["hmask"] = np.where(np.arange(P)[:, None] // HD == np.arange(HC), np.float32(HD ** -0.5), np.float32(0)).astype(np.float32)
    for n in (4, 16):
        arrays[f"before{n}"] = np.broadcast_to(np.tril(np.ones((n, n), np.float32), -1), (P, n, n))
    return {name: np.ascontiguousarray(a) for name, a in arrays.items()}


def kernel(**inputs):
    import concourse.bacc as bacc
    from concourse.bass_utils import run_bass_kernel_spmd

    nc = bacc.Bacc("TRN2", target_bir_lowering=False, num_devices=1)
    arrays = layout(**{name: np.asarray(a) for name, a in inputs.items()})
    ins = {name: nc.dram_tensor(f"in_{name}", a.shape, mybir.dt.from_np(a.dtype), kind="ExternalInput").ap() for name, a in arrays.items()}
    out = nc.dram_tensor("out", (BATCH, T, D), F32, kind="ExternalOutput").ap()
    mixed_lm_kernel(nc, ins, out)
    r = run_bass_kernel_spmd(nc, [{f"in_{name}": a for name, a in arrays.items()}], core_ids=[0])
    return r.results[0]["out"]
```

```python
from contextlib import ExitStack

import numpy as np
import concourse.bass as bass
from concourse import mybir

F32 = mybir.dt.float32
F32R = mybir.dt.float32r
I32 = mybir.dt.int32
U32 = mybir.dt.uint32
ALU = mybir.AluOpType
ACT = mybir.ActivationFunctionType
AX_X = mybir.AxisListType.X

P = 128
LAYERS, D, DF, V = 6, 256, 1024, 8000
BATCH, T = 8, 512
TT = T // P
KD = D // P
KF = DF // P
EPS = 1e-5


def passes(pe, out, a, b, first=True, last=True):
    pe.matmul(out, a[1], b[0], start=first, stop=False)
    pe.matmul(out, a[0], b[1], start=False, stop=False)
    return pe.matmul(out, a[0], b[0], start=False, stop=last)


def encoder(nc, ins, state, hidden):
    ctx = ExitStack()
    with ctx:
        def sb(name, shape, dt=F32):
            return ctx.enter_context(nc.sbuf_tensor(name, shape, dt))

        def sem(name):
            return ctx.enter_context(nc.semaphore(name))

        ident = sb("ident", [P, P])
        pos = sb("pos", [P, TT, D])
        ids = sb("ids", [P, BATCH * TT], I32)
        neg = sb("neg", [P, BATCH * TT], I32)
        rows = sb("rows", [P, BATCH * TT], U32)
        hraw = [sb(f"hraw{i}", [P, TT, D]) for i in range(2)]
        v_hi, v_lo = sb("v_hi", [P, TT, D], F32R), sb("v_lo", [P, TT, D], F32R)
        hT_hi, hT_lo = sb("hT_hi", [P, KD, T], F32R), sb("hT_lo", [P, KD, T], F32R)
        probs = [sb(f"probs{i}", [P, T]) for i in range(2)]
        pT_hi = [sb(f"pT_hi{i}", [P, TT, P], F32R) for i in range(2)]
        pT_lo = [sb(f"pT_lo{i}", [P, TT, P], F32R) for i in range(2)]
        h1 = [sb(f"h1_{i}", [P, TT, D]) for i in range(2)]
        h1b = sb("h1b", [P, TT, D])
        h1T_hi, h1T_lo = sb("h1T_hi", [P, KD, T], F32R), sb("h1T_lo", [P, KD, T], F32R)
        x1, x2 = sb("x1", [P, 2, D]), sb("x2", [P, 2, D])
        hid = [sb(f"hid{i}", [P, T]) for i in range(2)]
        hid_hi, hid_lo = sb("hid_hi", [P, KF, T], F32R), sb("hid_lo", [P, KF, T], F32R)
        w1_raw, w2_raw = sb("w1_raw", [P, KD, DF]), sb("w2_raw", [P, KF, D])
        w1_hi, w1_lo = sb("w1_hi", [P, KD, DF], F32R), sb("w1_lo", [P, KD, DF], F32R)
        w2_hi, w2_lo = sb("w2_hi", [P, KF, D], F32R), sb("w2_lo", [P, KF, D], F32R)
        g1, be1 = sb("g1", [P, D]), sb("be1", [P, D])
        g2, be2, b2 = sb("g2", [P, D]), sb("be2", [P, D]), sb("b2", [P, D])
        b1 = sb("b1", [P, KF])
        negmax, rowsum, rinv = sb("negmax", [P, TT]), sb("rowsum", [P, TT]), sb("rinv", [P, TT])
        st1, mv1, ve1, rs1 = sb("st1", [P, TT, 6]), sb("mv1", [P, TT, 2]), sb("ve1", [P, TT]), sb("rs1", [P, TT])
        st2, mv2, ve2, rs2 = sb("st2", [P, TT, 6]), sb("mv2", [P, TT, 2]), sb("ve2", [P, TT]), sb("rs2", [P, TT])
        minus_half = sb("minus_half", [P, 1])

        ps_s = [ctx.enter_context(nc.psum_tensor(f"ps_s{i}", [P, T], F32)) for i in range(2)]
        ps_pT = ctx.enter_context(nc.psum_tensor("ps_pT", [P, TT, P], F32))
        ps_mha = ctx.enter_context(nc.psum_tensor("ps_mha", [P, D], F32))
        ps_hid = [ctx.enter_context(nc.psum_tensor(f"ps_hid{i}", [P, T], F32)) for i in range(2)]
        ps_ff0 = ctx.enter_context(nc.psum_tensor("ps_ff0", [P, D], F32))
        ps_h1T = ctx.enter_context(nc.psum_tensor("ps_h1T", [P, KD, 2, P], F32))
        ps_hT = [ps_s[j][:, :].rearrange("p (k i t) -> p k i t", k=KD, i=2) for j in range(2)]
        ps_ff = [ps_ff0[:, :], ps_hid[1][:, 0:D]]

        consts_in, ids_in = sem("consts_in"), sem("ids_in")
        h_stored = sem("h_stored")
        h_in = [sem("h_in0"), sem("h_in1")]
        w1_in, w2_in = sem("w1_in"), sem("w2_in")
        ln1_in, ln2_in, b1_in = sem("ln1_in"), sem("ln2_in"), sem("b1_in")
        gathered = [sem(f"gathered{b}") for b in range(BATCH)]
        rows_step, rows_ready, half_ready = sem("rows_step"), sem("rows_ready"), sem("half_ready")
        first_ready, state_ready = sem("first_ready"), sem("state_ready")
        hT_ps, hT_hi_ready, hT_lo_ready = sem("hT_ps"), sem("hT_hi_ready"), sem("hT_lo_ready")
        v_hi_ready, v_lo_ready = sem("v_hi_ready"), sem("v_lo_ready")
        scores, negmax_ready, probs_ready = sem("scores"), sem("negmax_ready"), sem("probs_ready")
        pT_ps, pT_hi_ready, pT_lo_ready = sem("pT_ps"), sem("pT_hi_ready"), sem("pT_lo_ready")
        mha_ps, rinv_ready, x1_ready, st1_ready = sem("mha_ps"), sem("rinv_ready"), sem("x1_ready"), sem("st1_ready")
        mv1_ready, ve1_ready, rs1_ready = sem("mv1_ready"), sem("ve1_ready"), sem("rs1_ready")
        n1_ready, h1_ready = sem("n1_ready"), sem("h1_ready")
        h1T_ps, h1T_hi_ready, h1T_lo_ready = sem("h1T_ps"), sem("h1T_hi_ready"), sem("h1T_lo_ready")
        h1b_ready = sem("h1b_ready")
        hid_ps, hid_ready = sem("hid_ps"), sem("hid_ready")
        hid_hi_ready, hid_lo_ready = sem("hid_hi_ready"), sem("hid_lo_ready")
        ff_ps, x2_ready, st2_ready = sem("ff_ps"), sem("x2_ready"), sem("st2_ready")
        mv2_ready, ve2_ready, rs2_ready, n2_ready = sem("mv2_ready"), sem("ve2_ready"), sem("rs2_ready"), sem("n2_ready")
        w1_hi_ready, w1_lo_ready = sem("w1_hi_ready"), sem("w1_lo_ready")
        w2_hi_ready, w2_lo_ready = sem("w2_hi_ready"), sem("w2_lo_ready")

        def schedule(eng, start, step, split):
            start()
            step(0, 0, 0, 1, 0, 0, 1, ffn=False)

            def six_steps(l):
                with eng.Fori(0, 3) as p:
                    step(8 * l + 2 * p + 1, 32 * l + 8 * p + 4, 1, 2 * p + 2, l, l, 4 * l + p + 2)
                    step(8 * l + 2 * p + 2, 32 * l + 8 * p + 8, 0, 2 * p + 3, l, l, 4 * l + p + 2)

            with eng.Fori(0, LAYERS - 1) as l:
                six_steps(l)
                step(8 * l + 7, 32 * l + 28, 1, 0, l, l, 4 * l + 5)
                step(8 * l + 8, 32 * l + 32, 0, 1, l + 1, l, 4 * l + 5, layer_end=True)
                split(8 * l + 8, 32 * l + 32, l + 1)
            l = LAYERS - 1
            six_steps(l)
            step(8 * l + 7, 32 * l + 28, 1, 0, l, l, None, prep=False)
            step(8 * l + 8, 32 * l + 32, 0, 1, l, l, None, attn=False, prep=False)

        def wait(eng, s, value):
            if not isinstance(value, int) or value > 0:
                eng.wait_ge(s, value)

        block = ctx.enter_context(nc.Block())

        @block.sync
        def _(sp):
            def vectors(l, which):
                if which == 1:
                    pairs, s = ((g1, "ln1_g"), (be1, "ln1_b")), ln1_in
                else:
                    pairs, s = ((g2, "ln2_g"), (be2, "ln2_b"), (b2, "b2")), ln2_in
                for dst, name in pairs:
                    sp.dma_start(dst[:, :], ins[name][bass.ds(l, 1), :].broadcast_to([P, D])).then_inc(s, 16)

            def bias1(l):
                sp.dma_start(b1[:, :], ins["b1"][bass.ds(l, 1), :, :].rearrange("l p f -> (l p) f")).then_inc(b1_in,
                                                                                                              16)

            def weights(l):
                sp.dma_start(w1_raw[:, :, :], ins["w1"][bass.ds(l, 1), :, :].rearrange("l (k p) f -> p (l k) f",
                                                                                       p=P)).then_inc(w1_in, 16)
                sp.dma_start(w2_raw[:, :, :], ins["w2"][bass.ds(l, 1), :, :].rearrange("l (k p) f -> p (l k) f",
                                                                                       p=P)).then_inc(w2_in, 16)

            def load_h(t, par, b):
                if isinstance(t, int) and t <= 0:
                    sp.wait_ge(first_ready, t + 8)
                else:
                    sp.wait_ge(state_ready, t)
                wait(sp, x1_ready, t)
                sp.dma_start(hraw[1 - par][:, :, :], state[:, bass.ds(b, 1), :,
                                                           :].rearrange("p b t d -> p (b t) d")).then_inc(h_in[1 - par], 16)

            sp.dma_start(ids[:, :], ins["x"]).then_inc(ids_in, 16)
            sp.dma_start(pos[:, :, :], ins["pos"].rearrange("(t p) d -> p t d", p=P)).then_inc(consts_in, 16)
            sp.dma_start(ident[:, :], ins["ident"]).then_inc(consts_in, 16)
            vectors(0, 1)
            load_h(-4, 1, 0)
            load_h(0, 0, 1)
            weights(0)
            vectors(0, 2)
            bias1(0)
            with sp.Fori(1, LAYERS) as l:
                t0 = (l - 1) * 32
                sp.wait_ge(w1_hi_ready, l)
                sp.wait_ge(w1_lo_ready, l)
                sp.wait_ge(w2_hi_ready, l)
                sp.wait_ge(w2_lo_ready, l)
                weights(l)
                with sp.Fori(0, 3) as p:
                    load_h(t0 + 8 * p + 4, 1, 2 * p + 2)
                    load_h(t0 + 8 * p + 8, 0, 2 * p + 3)
                load_h(t0 + 28, 1, 0)
                sp.wait_ge(h1_ready, t0 + 32)
                vectors(l, 1)
                load_h(t0 + 32, 0, 1)
                sp.wait_ge(hid_ready, t0 * 2 + 64)
                bias1(l)
                sp.wait_ge(state_ready, t0 + 56)
                vectors(l, 2)
            t0 = (LAYERS - 1) * 32
            with sp.Fori(0, 3) as p:
                load_h(t0 + 8 * p + 4, 1, 2 * p + 2)
                load_h(t0 + 8 * p + 8, 0, 2 * p + 3)
            with sp.Fori(0, BATCH) as b:
                sp.wait_ge(state_ready, t0 + 28 + 4 * b)
                sp.dma_start(hidden[bass.ds(b, 1), :, :, :].rearrange("b p t d -> p (b t) d"),
                             state[:, bass.ds(b, 1), :, :].rearrange("p b t d -> p (b t) d")).then_inc(h_stored, 16)
            sp.wait_ge(h_stored, 16 * BATCH)

        @block.gpsimd
        def _(pool):
            def gather(b):
                for i in range(TT):
                    pool.indirect_dma_start(
                        out=state[:, b, i, :], out_offset=None, in_=ins["embed"],
                        in_offset=bass.IndirectOffsetOnAxis(ap=rows[:, b * TT + i:b * TT + i + 1],
                                                            axis=0)).then_inc(gathered[b], 16)

            def v_low(u, t, par, n):
                wait(pool, mha_ps, t + 4)
                pool.wait_ge(v_hi_ready, u + 2)
                pool.tensor_tensor(v_lo[:, :, :], hraw[1 - par][:, :, :], v_hi[:, :, :].bitcast(F32),
                                   ALU.subtract).then_inc(v_lo_ready, 1)

            def add_bias2(u, t, par, lf):
                pool.wait_ge(h1_ready, t)
                pool.wait_ge(ln2_in, (lf + 1) * 48)
                wait(pool, x2_ready, t - 4)
                pool.tensor_tensor(h1b[:, :, :], h1[1 - par][:, :, :], b2[:, :].unsqueeze(1).broadcast_to([P, TT, D]),
                                   ALU.add).then_inc(h1b_ready, 1)

            def hid_low(t, f):
                pool.wait_ge(hid_hi_ready, 2 * t - 8 + f + 1)
                if f == 0:
                    wait(pool, ff_ps, t - 4)
                pool.tensor_tensor(hid_lo[:, f, :], hid[f % 2][:, :], hid_hi[:, f, :].bitcast(F32),
                                   ALU.subtract).then_inc(hid_lo_ready, 1)

            def split_w2(l):
                pool.wait_ge(w2_hi_ready, l + 1)
                pool.tensor_tensor(w2_lo[:, :, :], w2_raw[:, :, :], w2_hi[:, :, :].bitcast(F32),
                                   ALU.subtract).then_inc(w2_lo_ready, 1)

            def rstd1(t, i):
                pool.wait_ge(ve1_ready, t + i + 1)
                pool.tensor_tensor(rs1[:, i:i + 1], ve1[:, i:i + 1], minus_half[:, :], ALU.pow).then_inc(rs1_ready, 1)

            def rstd2(t, i):
                pool.wait_ge(ve2_ready, t - 4 + i + 1)
                pool.tensor_tensor(rs2[:, i:i + 1], ve2[:, i:i + 1], minus_half[:, :], ALU.pow).then_inc(rs2_ready, 1)

            def step(u, t, par, b, la, lf, n, attn=True, ffn=True, prep=True, layer_end=False):
                for i in range(TT):
                    if ffn:
                        hid_low(t, 2 * i)
                        if i < TT - 1:
                            hid_low(t, 2 * i + 1)
                    elif i < 2:
                        gather(3 + i)
                    if ffn and i == 1:
                        add_bias2(u, t, par, lf)
                    if attn and i >= 1:
                        rstd1(t, i - 1)
                    if not ffn and i >= 2:
                        gather(3 + i)
                if ffn:
                    rstd2(t, 0)
                if attn:
                    rstd1(t, 3)
                if prep:
                    v_low(u, t, par, n)
                if not ffn:
                    gather(7)
                    split_w2(0)
                if ffn:
                    for i in range(1, TT):
                        rstd2(t, i)

            def start():
                pool.memset(minus_half[:, :], -0.5).then_inc(half_ready, 1)
                pool.wait_ge(rows_ready, 1)
                gather(0)
                gather(1)
                pool.wait_ge(half_ready, 1)
                gather(2)
                v_low(-1, -4, 1, 1)

            schedule(pool, start, step, lambda u, t, l: split_w2(l))

        @block.scalar
        def _(act):
            def relu(t, f, lf):
                act.wait_ge(hid_ps, 2 * t - 8 + f + 1)
                wait(act, hid_lo_ready, 2 * t - 8 + max(f - 1, 0))
                if f == 0:
                    act.wait_ge(b1_in, (lf + 1) * 16)
                act.activation(hid[f % 2][:, :], ps_hid[f % 2][:, :], ACT.Relu,
                               bias=b1[:, f:f + 1]).then_inc(hid_ready, 1)
                if f == 0:
                    wait(act, ff_ps, t - 4)
                act.wait_ge(hid_ready, 2 * t - 8 + f + 1)
                act.activation(hid_hi[:, f, :], hid[f % 2][:, :], ACT.Copy).then_inc(hid_hi_ready, 1)

            def exp(t, i):
                act.wait_ge(negmax_ready, t + i + 1)
                wait(act, pT_ps, t + i - 1)
                act.activation(probs[i % 2][:, :], ps_s[i % 2][:, :], ACT.Exp, bias=negmax[:, i:i + 1],
                               accum_out=rowsum[:, i:i + 1]).then_inc(probs_ready, 1)

            def pT_high(t, i):
                act.wait_ge(pT_ps, t + i + 1)
                wait(act, mha_ps, t + i - 1)
                act.activation(pT_hi[i % 2][:, :, :], ps_pT[:, :, :], ACT.Copy).then_inc(pT_hi_ready, 1)

            def h1T_high(u, j):
                act.wait_ge(h1T_ps, 2 * u + j + 1)
                wait(act, hid_ps, 8 * u)
                act.activation(h1T_hi[:, :, 2 * j * P:(2 * j + 2) * P],
                               ps_h1T[:, :, :, :].rearrange("p k i t -> p k (i t)"),
                               ACT.Copy).then_inc(h1T_hi_ready, 1)

            def hT_high(u, t, j):
                act.wait_ge(hT_ps, 2 * u + 2 + j + 1)
                wait(act, scores, t + 4)
                act.activation(hT_hi[:, :, 2 * j * P:(2 * j + 2) * P], ps_hT[j].rearrange("p k i t -> p k (i t)"),
                               ACT.Copy, scale=0.25).then_inc(hT_hi_ready, 1)

            def v_high(u, t, par, n):
                act.wait_ge(h_in[1 - par], 16 * n)
                wait(act, mha_ps, t + 4)
                act.activation(v_hi[:, :, :], hraw[1 - par][:, :, :], ACT.Copy).then_inc(v_hi_ready, 1)

            def split_w1(l):
                act.wait_ge(w1_in, 16 * l + 16)
                act.activation(w1_hi[:, :, :], w1_raw[:, :, :], ACT.Copy).then_inc(w1_hi_ready, 1)

            def split_w2(l):
                act.wait_ge(w2_in, 16 * l + 16)
                act.activation(w2_hi[:, :, :], w2_raw[:, :, :], ACT.Copy).then_inc(w2_hi_ready, 1)

            def step(u, t, par, b, la, lf, n, attn=True, ffn=True, prep=True, layer_end=False):
                if ffn:
                    relu(t, 0, lf)
                for i in range(TT):
                    if attn:
                        if i >= 1:
                            pT_high(t, i - 1)
                        exp(t, i)
                    if ffn:
                        if i >= 1:
                            relu(t, 2 * i, lf)
                        relu(t, 2 * i + 1, lf)
                if attn:
                    pT_high(t, 3)
                if layer_end:
                    act.wait_ge(hid_ps, 2 * t)
                    split_w1(lf + 1)
                if attn:
                    h1T_high(u, 0)
                if prep:
                    v_high(u, t, par, n)
                    hT_high(u, t, 0)
                    hT_high(u, t, 1)
                if attn:
                    h1T_high(u, 1)
                if not ffn:
                    split_w1(0)
                    split_w2(0)

            def start():
                v_high(-1, -4, 1, 1)
                for j in range(2):
                    hT_high(-1, -4, j)

            def split(u, t, l):
                act.wait_ge(ff_ps, t)
                split_w2(l)

            schedule(act, start, step, split)

        @block.vector
        def _(dve):
            def neg_max(t, i):
                dve.wait_ge(scores, t + i + 1)
                wait(dve, probs_ready, t + i - 3)
                dve.tensor_reduce(negmax[:, i:i + 1], ps_s[i % 2][:, :], AX_X, ALU.max,
                                  negate=True).then_inc(negmax_ready, 1)

            def pT_low(t, i):
                dve.wait_ge(pT_hi_ready, t + i + 1)
                wait(dve, mha_ps, t + i - 1)
                dve.tensor_tensor(pT_lo[i % 2][:, :, :], ps_pT[:, :, :], pT_hi[i % 2][:, :, :].bitcast(F32),
                                  ALU.subtract).then_inc(pT_lo_ready, 1)

            def residual1(t, par, i):
                dve.wait_ge(probs_ready, t + i + 1)
                dve.reciprocal(rinv[:, i:i + 1], rowsum[:, i:i + 1]).then_inc(rinv_ready, 1)
                dve.wait_ge(mha_ps, t + i + 1)
                dve.wait_ge(rinv_ready, t + i + 1)
                dve.scalar_tensor_tensor(out=x1[:, i % 2, :], in0=ps_mha[:, :], scalar=rinv[:, i:i + 1],
                                         in1=hraw[par][:, i, :], op0=ALU.mult, op1=ALU.add).then_inc(x1_ready, 1)
                dve.wait_ge(x1_ready, t + i + 1)
                dve.bn_stats(st1[:, i, :], x1[:, i % 2, :]).then_inc(st1_ready, 1)
                dve.wait_ge(st1_ready, t + i + 1)
                dve.memset(ve1[:, i:i + 1], EPS)
                dve.bn_aggr(mv1[:, i, :], st1[:, i, :]).then_inc(mv1_ready, 1)
                dve.wait_ge(mv1_ready, t + i + 1)
                dve.tensor_tensor(ve1[:, i:i + 1], mv1[:, i, 1:2], ve1[:, i:i + 1], ALU.add).then_inc(ve1_ready, 1)

            def norm1(t, par, i, la):
                if i == 0:
                    dve.wait_ge(ln1_in, (la + 1) * 32)
                dve.scalar_tensor_tensor(out=x1[:, i % 2, :], in0=x1[:, i % 2, :], scalar=mv1[:, i, 0:1],
                                         in1=g1[:, :], op0=ALU.subtract, op1=ALU.mult).then_inc(n1_ready, 1)
                dve.wait_ge(n1_ready, t + i + 1)
                dve.wait_ge(rs1_ready, t + i + 1)
                dve.scalar_tensor_tensor(out=h1[par][:, i, :], in0=x1[:, i % 2, :], scalar=rs1[:, i:i + 1],
                                         in1=be1[:, :], op0=ALU.mult, op1=ALU.add).then_inc(h1_ready, 1)

            def h1T_low(u, j):
                dve.wait_ge(h1T_hi_ready, 2 * u + j + 1)
                sl = slice(2 * j * P, (2 * j + 2) * P)
                dve.tensor_tensor(h1T_lo[:, :, sl], ps_h1T[:, :, :, :].rearrange("p k i t -> p k (i t)"),
                                  h1T_hi[:, :, sl].bitcast(F32), ALU.subtract).then_inc(h1T_lo_ready, 1)

            def hT_low(u, j):
                dve.wait_ge(hT_hi_ready, 2 * u + 2 + j + 1)
                sl = slice(2 * j * P, (2 * j + 2) * P)
                dve.scalar_tensor_tensor(out=hT_lo[:, :, sl], in0=ps_hT[j].rearrange("p k i t -> p k (i t)"),
                                         scalar=0.25,
                                         in1=hT_hi[:, :,
                                                   sl].bitcast(F32), op0=ALU.mult,
                                                   op1=ALU.subtract).then_inc(hT_lo_ready, 1)

            def residual2(u, t, i):
                n = t - 4 + i + 1
                dve.wait_ge(ff_ps, n)
                if i == 0:
                    dve.wait_ge(h1b_ready, u)
                dve.tensor_tensor(x2[:, i % 2, :], ps_ff[i % 2], h1b[:, i, :], ALU.add).then_inc(x2_ready, 1)
                dve.wait_ge(x2_ready, n)
                dve.bn_stats(st2[:, i, :], x2[:, i % 2, :]).then_inc(st2_ready, 1)
                dve.wait_ge(st2_ready, n)
                dve.memset(ve2[:, i:i + 1], EPS)
                dve.bn_aggr(mv2[:, i, :], st2[:, i, :]).then_inc(mv2_ready, 1)
                dve.wait_ge(mv2_ready, n)
                dve.tensor_tensor(ve2[:, i:i + 1], mv2[:, i, 1:2], ve2[:, i:i + 1], ALU.add).then_inc(ve2_ready, 1)

            def norm2(t, b, i, lf):
                n = t - 4 + i + 1
                if i == 0:
                    dve.wait_ge(ln2_in, (lf + 1) * 48)
                dve.scalar_tensor_tensor(out=x2[:, i % 2, :], in0=x2[:, i % 2, :], scalar=mv2[:, i, 0:1],
                                         in1=g2[:, :], op0=ALU.subtract, op1=ALU.mult).then_inc(n2_ready, 1)
                dve.wait_ge(n2_ready, n)
                dve.wait_ge(rs2_ready, n)
                at = (b + 6) % 8 if isinstance(b, int) else b - 2
                dve.scalar_tensor_tensor(out=state[:, bass.ds(at, 1), i, :].rearrange("p b d -> p (b d)"),
                                         in0=x2[:, i % 2, :],
                                         scalar=rs2[:, i:i + 1], in1=be2[:,
                                                                         :], op0=ALU.mult,
                                                                         op1=ALU.add).then_inc(state_ready, 1)

            def hid_low(t, f):
                dve.wait_ge(hid_hi_ready, 2 * t - 8 + f + 1)
                dve.tensor_tensor(hid_lo[:, f, :], hid[f % 2][:, :], hid_hi[:, f, :].bitcast(F32),
                                  ALU.subtract).then_inc(hid_lo_ready, 1)

            def add_positions(b):
                dve.wait_ge(gathered[b], 16 * TT)
                dve.tensor_tensor(state[:, b, :, :], state[:, b, :, :], pos[:, :, :],
                                  ALU.add).then_inc(first_ready if b < 2 else state_ready, TT)

            def split_w1(l):
                dve.wait_ge(w1_hi_ready, l + 1)
                dve.tensor_tensor(w1_lo[:, :, :], w1_raw[:, :, :], w1_hi[:, :, :].bitcast(F32),
                                  ALU.subtract).then_inc(w1_lo_ready, 1)

            def start():
                dve.wait_ge(ids_in, 16)
                dve.tensor_scalar(neg[:, :], ids[:, :], 0, V, ALU.is_lt, ALU.mult).then_inc(rows_step, 1)
                dve.wait_ge(rows_step, 1)
                dve.tensor_tensor(ids[:, :], ids[:, :], neg[:, :], ALU.add).then_inc(rows_step, 1)
                dve.wait_ge(rows_step, 2)
                dve.tensor_scalar(rows[:, :], ids[:, :], 0, V - 1, ALU.max, ALU.min).then_inc(rows_ready, 1)
                dve.wait_ge(consts_in, 32)
                add_positions(0)
                add_positions(1)
                for j in range(2):
                    hT_low(-1, j)

            def step(u, t, par, b, la, lf, n, attn=True, ffn=True, prep=True, layer_end=False):
                if attn:
                    neg_max(t, 0)
                    neg_max(t, 1)
                    pT_low(t, 0)
                    residual1(t, par, 0)
                    neg_max(t, 2)
                    pT_low(t, 1)
                    residual1(t, par, 1)
                    neg_max(t, 3)
                    norm1(t, par, 0, la)
                    pT_low(t, 2)
                    norm1(t, par, 1, la)
                if ffn:
                    hid_low(t, KF - 1)
                if attn:
                    residual1(t, par, 2)
                    pT_low(t, 3)
                    norm1(t, par, 2, la)
                    if not ffn:
                        add_positions(2)
                        add_positions(3)
                    h1T_low(u, 0)
                if ffn:
                    residual2(u, t, 0)
                if attn:
                    residual1(t, par, 3)
                if ffn:
                    norm2(t, b, 0, lf)
                if attn:
                    norm1(t, par, 3, la)
                if layer_end:
                    split_w1(lf + 1)
                if prep:
                    hT_low(u, 0)
                if ffn:
                    residual2(u, t, 1)
                if prep:
                    hT_low(u, 1)
                if ffn:
                    norm2(t, b, 1, lf)
                    residual2(u, t, 2)
                if attn:
                    h1T_low(u, 1)
                if ffn:
                    norm2(t, b, 2, lf)
                    residual2(u, t, 3)
                    norm2(t, b, 3, lf)
                else:
                    split_w1(0)
                    for later in range(4, BATCH):
                        add_positions(later)

            schedule(dve, start, step, lambda u, t, l: None)

        @block.tensor
        def _(pe):
            def tile_of(i):
                return slice(i * P, (i + 1) * P)

            def score(u, t, i):
                if i == 0:
                    pe.wait_ge(hT_lo_ready, 2 * u + 2)
                    pe.wait_ge(hT_hi_ready, 2 * u + 2)
                wait(pe, probs_ready, t + i - 1)
                for k in range(KD):
                    m = passes(pe, ps_s[i % 2][:, :], (hT_hi[:, k, tile_of(i)], hT_lo[:, k, tile_of(i)]),
                               (hT_hi[:, k, :], hT_lo[:, k, :]), k == 0, k == KD - 1)
                m.then_inc(scores, 1)

            def turn_probs(t, i):
                pe.wait_ge(probs_ready, t + i + 1)
                wait(pe, pT_lo_ready, t + i)
                for c in range(TT):
                    m = pe.transpose(ps_pT[:, c, :], probs[i % 2][:, tile_of(c)], ident[:, :])
                m.then_inc(pT_ps, 1)

            def mix(u, t, i):
                if i == 0:
                    pe.wait_ge(v_lo_ready, u + 1)
                    pe.wait_ge(v_hi_ready, u + 1)
                pe.wait_ge(pT_lo_ready, t + i + 1)
                wait(pe, x1_ready, t + i)
                for c in range(TT):
                    m = passes(pe, ps_mha[:, :], (pT_hi[i % 2][:, c, :], pT_lo[i % 2][:, c, :]),
                               (v_hi[:, c, :], v_lo[:, c, :]), c == 0, c == TT - 1)
                m.then_inc(mha_ps, 1)

            def turn(src, j, bank):
                for k in range(KD):
                    for i in range(2):
                        m = pe.transpose(bank[:, k, i, :], src[:, 2 * j + i, k * P:(k + 1) * P], ident[:, :])
                return m

            def turn_h1(u, t, par, j):
                pe.wait_ge(h1_ready, t + 2 * j + 2)
                wait(pe, h1T_lo_ready, 2 * u + j)
                turn(h1[par], j, ps_h1T).then_inc(h1T_ps, 1)

            def turn_h(u, t, par, j, n):
                pe.wait_ge(h_in[1 - par], 16 * n)
                wait(pe, probs_ready, t + 4)
                turn(hraw[1 - par], j, ps_hT[j]).then_inc(hT_ps, 1)

            def up(u, t, f, lf):
                if f == 0:
                    pe.wait_ge(h1T_lo_ready, 2 * u)
                    pe.wait_ge(w1_lo_ready, lf + 1)
                if f == 1:
                    wait(pe, x2_ready, t - 4)
                wait(pe, hid_ready, 2 * t - 8 + max(f - 1, 0))
                for k in range(KD):
                    m = passes(pe, ps_hid[f % 2][:, :], (w1_hi[:, k, tile_of(f)], w1_lo[:, k, tile_of(f)]),
                               (h1T_hi[:, k, :], h1T_lo[:, k, :]), k == 0, k == KD - 1)
                m.then_inc(hid_ps, 1)

            def down(t, i, lf):
                if i == 0:
                    pe.wait_ge(hid_lo_ready, 2 * t)
                    pe.wait_ge(w2_lo_ready, lf + 1)
                wait(pe, x2_ready, t - 4 + max(i - 1, 0))
                for f in range(KF):
                    m = passes(pe, ps_ff[i % 2], (hid_hi[:, f, tile_of(i)], hid_lo[:, f, tile_of(i)]),
                               (w2_hi[:, f, :], w2_lo[:, f, :]), f == 0, f == KF - 1)
                m.then_inc(ff_ps, 1)

            def step(u, t, par, b, la, lf, n, attn=True, ffn=True, prep=True, layer_end=False):
                if attn:
                    score(u, t, 0)
                if ffn:
                    up(u, t, 0, lf)
                if attn:
                    score(u, t, 1)
                if ffn:
                    up(u, t, 1, lf)
                    up(u, t, 2, lf)
                if attn:
                    turn_probs(t, 0)
                if ffn:
                    up(u, t, 3, lf)
                if attn:
                    score(u, t, 2)
                    mix(u, t, 0)
                    turn_probs(t, 1)
                if ffn:
                    up(u, t, 4, lf)
                    up(u, t, 5, lf)
                if attn:
                    mix(u, t, 1)
                    score(u, t, 3)
                    turn_probs(t, 2)
                if ffn:
                    up(u, t, 6, lf)
                    up(u, t, 7, lf)
                if attn:
                    mix(u, t, 2)
                    turn_probs(t, 3)
                    turn_h1(u, t, par, 0)
                if ffn:
                    down(t, 0, lf)
                if attn:
                    mix(u, t, 3)
                if prep:
                    turn_h(u, t, par, 0, n)
                if ffn:
                    down(t, 1, lf)
                if prep:
                    turn_h(u, t, par, 1, n)
                if ffn:
                    down(t, 2, lf)
                if attn:
                    turn_h1(u, t, par, 1)
                if ffn:
                    down(t, 3, lf)

            def start():
                pe.wait_ge(consts_in, 32)
                for j in range(2):
                    turn_h(-1, -4, 1, j, 1)

            schedule(pe, start, step, lambda u, t, l: None)


HEADS, HD, HALF = 16, 16, 32
HC = HEADS // KD
QB = 64
WIN = 2 * QB
NWIN = T // QB
UNITS = TT * KD
EXPERTS, GROUPS, TOP_GROUPS, TOP = 16, 4, 2, 4
SHARED = 2
SLOTS = SHARED + EXPERTS
HPC = 4
OC = HEADS // HPC
GATE_OPS = 25
GATE_PARTS = 6, 15, 17, 19, GATE_OPS
LOW_BY_POOL = 0, 1, 13, 14, 15, 16
APART = 12


def window(b):
    return min(max(QB * b - HALF, 0), T - WIN)


def experts(nc, ins, hidden, out):
    ctx = ExitStack()
    with ctx:
        def sb(name, shape, dt=F32):
            return ctx.enter_context(nc.sbuf_tensor("e_" + name, shape, dt))

        def sem(name):
            return ctx.enter_context(nc.semaphore("e_" + name))

        def pair(name, shape):
            return sb(name + "_hi", shape, F32R), sb(name + "_lo", shape, F32R)

        ident = sb("ident", [P, P])
        band = sb("band", [P, 3, P])
        hmask = sb("hmask", [P, HC])
        before4, before16 = sb("before4", [P, 4, 4]), sb("before16", [P, 16, 16])
        bq, bk = sb("bq", [P, KD]), sb("bk", [P, KD])
        bv, bo = sb("bv", [P, D]), sb("bo", [P, D])
        minus_half = sb("minus_half", [P, 1])
        wq, wk, wv = pair("wq", [P, KD, D]), pair("wk", [P, KD, D]), pair("wv", [P, KD, D])
        wo = pair("wo", [P, OC, D])
        wg = pair("wg", [P, KD, EXPERTS])
        w_raw = sb("w_raw", [P, SLOTS, 3 * D])
        w13 = [pair(f"w13_{i}", [P, 2 * D]) for i in range(2)]
        w2 = [pair(f"w2_{i}", [P, D]) for i in range(3)]
        x = sb("x", [P, TT, D])
        xT = pair("xT", [P, KD, T])
        qf, kf = sb("qf", [P, KD, T]), sb("kf", [P, KD, T])
        qm = [sb(f"qm{i}", [P, HC, P]) for i in range(2)]
        vw = sb("vw", [P, NWIN, D + HD])
        s = [sb(f"s{i}", [P, HC, P]) for i in range(2)]
        pT = sb("pT", [P, HC, P])
        oT = pair("oT", [P, OC, P])
        h2, y = sb("h2", [P, TT, D]), sb("y", [P, TT, D])
        yT = pair("yT", [P, KD, T])
        yT_next = pair("yT_next", [P, KD, T])
        acc = sb("acc", [P, TT, D])
        th, act_f = sb("th", [P, T]), sb("act_f", [P, T])
        act = [pair(f"act{i}", [P, T]) for i in range(2)]
        negmax, rowsum, rinv = sb("negmax", [P, 2, HC]), sb("rowsum", [P, 2, HC]), sb("rinv", [P, 2, HC])
        st, mv, ve, rs = sb("st", [P, TT, 6]), sb("mv", [P, TT, 2]), sb("ve", [P, TT]), sb("rs", [P, TT])
        sty, mvy, vey, rsy = sb("sty", [P, TT, 6]), sb("mvy", [P, TT, 2]), sb("vey", [P, TT]), sb("rsy", [P, TT])
        g_e, g_s, g_w = sb("g_e", [P, TT, EXPERTS]), sb("g_s", [P, TT, EXPERTS]), sb("g_w", [P, TT, EXPERTS])
        g_two, g_top = sb("g_two", [P, TT * GROUPS, 6]), sb("g_top", [P, TT, GROUPS])
        g_a, g_b = sb("g_a", [P, TT, 16, 16]), sb("g_b", [P, TT, 16, 16])
        g_ok, g_okm, g_m = sb("g_ok", [P, TT * GROUPS]), sb("g_okm", [P, TT * GROUPS]), sb("g_m", [P, TT, EXPERTS])
        g_rank, g_sum = sb("g_rank", [P, TT, EXPERTS]), sb("g_sum", [P, TT])
        weight = sb("weight", [P, TT, SLOTS])

        ps_s = ctx.enter_context(nc.psum_tensor("e_ps_s", [P, HC, P], F32))
        ps_p = ctx.enter_context(nc.psum_tensor("e_ps_p", [P, HC, P], F32))
        ps_g = ctx.enter_context(nc.psum_tensor("e_ps_g", [P, T], F32))
        ps_u = ctx.enter_context(nc.psum_tensor("e_ps_u", [P, T], F32))
        ps_y = ctx.enter_context(nc.psum_tensor("e_ps_y", [P, 2, D], F32))
        ps_x = ctx.enter_context(nc.psum_tensor("e_ps_x", [P, T], F32))
        ps_q, ps_k = (ps_s[:, 4 * n:4 * n + 4, :].rearrange("p a t -> p (a t)") for n in range(2))
        ps_xT = [ps_p[:, 4 * j:4 * j + 4, :].rearrange("p (k i) t -> p k (i t)", k=KD) for j in range(2)]
        ps_v = [ps_p[:, 4 * j:4 * j + 4, :].rearrange("p (w a) t -> p w (a t)", w=2) for j in range(2)]
        ps_o = ps_x[:, 0:2 * P].rearrange("p (c t) -> p c t", c=2)
        ps_yT = ps_x[:, :].rearrange("p (k t) -> p k t", k=KD)
        ps_gate = ps_x[:, 0:TT * EXPERTS].rearrange("p (i e) -> p i e", i=TT)

        ident_in, consts_in, attn_in = sem("ident_in"), sem("consts_in"), sem("attn_in")
        x_in, out_done = sem("x_in"), sem("out_done")
        w_in = [sem(f"w_in{g}") for g in range(3)]
        half_ready, zeros_ready, ones_ready = sem("half_ready"), sem("zeros_ready"), sem("ones_ready")
        attn_hi, attn_lo = sem("attn_hi"), sem("attn_lo")
        st_ready, mv_ready, ve_ready = sem("st_ready"), sem("mv_ready"), sem("ve_ready")
        rs_ready, x_ready = sem("rs_ready"), sem("x_ready")
        hb_ready = sem("hb_ready")
        xT_ps, xT_hi, xT_lo = sem("xT_ps"), sem("xT_hi"), sem("xT_lo")
        q_ps, k_ps, q_ready, k_ready = sem("q_ps"), sem("k_ps"), sem("q_ready"), sem("k_ready")
        v_ps, v_ready = sem("v_ps"), sem("v_ready")
        qm_ready, scores, masked, negmax_ready = sem("qm_ready"), sem("scores"), sem("masked"), sem("negmax_ready")
        probs, rinv_ready, probs_ready = sem("probs"), sem("rinv_ready"), sem("probs_ready")
        pT_ps, pT_ready = sem("pT_ps"), sem("pT_ready")
        oT_ps, oT_hi, oT_lo = sem("oT_ps"), sem("oT_hi"), sem("oT_lo")
        wo_ps, h2_ready = sem("wo_ps"), sem("h2_ready")
        sty_ready, mvy_ready, vey_ready = sem("sty_ready"), sem("mvy_ready"), sem("vey_ready")
        rsy_ready, y_ready = sem("rsy_ready"), sem("y_ready")
        yT_ps, yT_hi, yT_lo = sem("yT_ps"), sem("yT_hi"), sem("yT_lo")
        moved_hi, moved_lo = sem("moved_hi"), sem("moved_lo")
        gate_ps, gate_exp, gate_step = sem("gate_ps"), sem("gate_exp"), sem("gate_step")
        w13_hi, w13_lo, w2_hi, w2_lo = sem("w13_hi"), sem("w13_lo"), sem("w2_hi"), sem("w2_lo")
        g_ps, u_ps, tanh_ready = sem("g_ps"), sem("u_ps"), sem("tanh_ready")
        silu_ready, act_ready = sem("silu_ready"), sem("act_ready")
        act_hi, act_lo, act_lo_pool = sem("act_hi"), sem("act_lo"), sem("act_lo_pool")
        y_ps, acc_ready = sem("y_ps"), sem("acc_ready")

        def wait(eng, sm, value):
            if not isinstance(value, int) or value > 0:
                eng.wait_ge(sm, value)

        def apart(e, attn):
            return not attn or e + 1 >= APART

        def y_bank(e, j, attn):
            if j == 1 and apart(e, attn):
                return ps_s[:, 4:8, :].rearrange("p (i a) t -> p i (a t)", i=2)
            return ps_y[:, :, :]

        def wait_act_low(eng, v, e):
            mine = [k for k in range(SLOTS) if (k in LOW_BY_POOL) == (e in LOW_BY_POOL)]
            eng.wait_ge(act_lo_pool if e in LOW_BY_POOL else act_lo, len(mine) * v + mine.index(e) + 1)

        def take_act_low(eng, v, e):
            eng.wait_ge(act_hi, 18 * v + e + 1)
            hi, lo = act[e % 2]
            eng.tensor_tensor(lo[:, :], act_f[:, :], hi[:, :].bitcast(F32),
                              ALU.subtract).then_inc(act_lo_pool if e in LOW_BY_POOL else act_lo, 1)

        def schedule(eng, begin, slots, end):
            begin()
            slots(0, -1, True, False, True)
            end(0, -1, True, False, True)
            with eng.Fori(0, BATCH - 2) as v:
                slots(v + 1, v, True, True, True)
                end(v + 1, v, True, True, True)
            slots(BATCH - 1, BATCH - 2, True, True, False)
            end(BATCH - 1, BATCH - 2, True, True, False)
            slots(BATCH, BATCH - 1, False, True, False)
            end(BATCH, BATCH - 1, False, True, False)

        block = ctx.enter_context(nc.Block())

        @block.sync
        def _(sp):
            def load_x(w):
                sp.dma_start(x[:, :, :], hidden[bass.ds(w, 1), :, :,
                                                :].rearrange("b p t d -> p (b t) d")).then_inc(x_in, 16)

            load_x(0)
            sp.dma_start(ident[:, :], ins["ident"]).then_inc(ident_in, 16)
            for dst, name in ((s[0][:, 0:4, :], "wq"), (s[0][:, 4:8, :], "wk"), (s[1][:, 0:4, :], "wv"),
                              (pT[:, :, :], "wo"), (s[1][:, 4, 0:2 * EXPERTS], "wg")):
                sp.dma_start(dst if name == "wg" else dst.rearrange("p a t -> p (a t)"), ins[name]).then_inc(attn_in,
                                                                                                             16)
            for dst, name in ((band[:, :, :], "band"), (hmask[:, :], "hmask"),
                              (before4[:, :, :], "before4"), (before16[:, :, :], "before16"),
                              (bq[:, :], "bq"), (bk[:, :], "bk"), (bv[:, :], "bv"), (bo[:, :], "bo")):
                src = ins[name] if name not in ("bv", "bo") else ins[name].broadcast_to([P, D])
                sp.dma_start(dst, src).then_inc(consts_in, 16)
            for g in range(3):
                sp.dma_start(w_raw[:, 6 * g:6 * g + 6, :], ins["moe"][:, 6 * g:6 * g + 6, :]).then_inc(w_in[g], 16)
            sp.wait_ge(hb_ready, 1)
            sp.wait_ge(xT_ps, 2)
            load_x(1)
            with sp.Fori(0, BATCH - 2) as v:
                sp.wait_ge(hb_ready, v + 2)
                sp.wait_ge(xT_ps, 2 * v + 4)
                load_x(v + 2)
                sp.wait_ge(acc_ready, 72 * v + 72)
                sp.dma_start(out[bass.ds(v, 1), :, :].rearrange("b (t p) d -> p (b t) d", p=P),
                             acc[:, :, :]).then_inc(out_done, 16)
            for v in (BATCH - 2, BATCH - 1):
                sp.wait_ge(acc_ready, 72 * v + 72)
                sp.dma_start(out[v, :, :].rearrange("(t p) d -> p t d", p=P), acc[:, :, :]).then_inc(out_done, 16)
            sp.wait_ge(out_done, 16 * BATCH)

        @block.gpsimd
        def _(pool):
            pool.memset(minus_half[:, :], -0.5).then_inc(half_ready, 1)
            pool.memset(vw[:, :, D:D + HD], 0.0).then_inc(zeros_ready, 1)
            pool.memset(weight[:, :, 0:SHARED], 1.0).then_inc(ones_ready, 1)
            pool.wait_ge(half_ready, 1)

            def rstd(w, i):
                pool.wait_ge(ve_ready, 4 * w + i + 1)
                pool.tensor_tensor(rs[:, i:i + 1], ve[:, i:i + 1], minus_half[:, :], ALU.pow).then_inc(rs_ready, 1)

            def rstd_y(w, i):
                pool.wait_ge(vey_ready, 4 * w + i + 1)
                pool.tensor_tensor(rsy[:, i:i + 1], vey[:, i:i + 1], minus_half[:, :], ALU.pow).then_inc(rsy_ready, 1)

            def add_bo(w):
                if isinstance(w, int) and w == 0:
                    pool.wait_ge(x_in, 16)
                    pool.wait_ge(consts_in, 16 * 8)
                else:
                    pool.wait_ge(x_in, 16 * w + 16)
                    pool.wait_ge(acc_ready, 72 * w - 68)
                pool.tensor_tensor(h2[:, :, :], x[:, :, :], bo[:, :].unsqueeze(1).broadcast_to([P, TT, D]),
                                   ALU.add).then_inc(hb_ready, 1)

            def mask_q(w, n):
                i, c = n // 2, n % 2
                pool.wait_ge(q_ready, 2 * w + 2)
                wait(pool, scores, 8 * w + n - 1)
                pool.tensor_tensor(qm[n % 2][:, :, :], qf[:, c, i * P:(i + 1) * P].unsqueeze(1).broadcast_to([P, HC,
                                                                                                              P]),
                                   hmask[:, :].unsqueeze(2).broadcast_to([P, HC, P]), ALU.mult).then_inc(qm_ready, 1)

            def normalize(w, n):
                pool.wait_ge(rinv_ready, 8 * w + n + 1)
                pool.tensor_tensor(s[n % 2][:, :, :], s[n % 2][:, :, :],
                                   rinv[:, n % 2, :].unsqueeze(2).broadcast_to([P, HC, P]),
                                   ALU.mult).then_inc(probs_ready, 1)

            def w_low(v, e):
                hi, lo = w13[e % 2]
                pool.wait_ge(w13_hi, 18 * v + e + 1)
                pool.tensor_tensor(lo[:, :], w_raw[:, e, 0:2 * D], hi[:, :].bitcast(F32),
                                   ALU.subtract).then_inc(w13_lo, 1)
                hi, lo = w2[e % 3]
                pool.wait_ge(w2_hi, 18 * v + e + 1)
                pool.tensor_tensor(lo[:, :], w_raw[:, e, 2 * D:3 * D], hi[:, :].bitcast(F32),
                                   ALU.subtract).then_inc(w2_lo, 1)

            def slots(w, v, attn, moe, more):
                for k in range(SLOTS):
                    if moe and k + 1 < SLOTS:
                        w_low(v, k + 1)
                    if moe and k in LOW_BY_POOL:
                        take_act_low(pool, v, k)
                    if attn:
                        if k == 2:
                            add_bo(w)
                        if 0 <= k - 2 < UNITS:
                            mask_q(w, k - 2)
                        if not moe and 0 <= k - 4 < UNITS:
                            normalize(w, k - 4)
                        if k in (8, 10, 12, 14):
                            rstd_y(w, (k - 8) // 2)
                        if more and 0 <= k - 11 < TT:
                            rstd(w + 1, k - 11)
                        if moe and 0 <= k - 4 < UNITS:
                            normalize(w, k - 4)

            def begin():
                for i in range(TT):
                    rstd(0, i)

            def end(w, v, attn, moe, more):
                if attn:
                    w_low(w, 0)

            schedule(pool, begin, slots, end)

        @block.scalar
        def _(act_e):
            def split_attention():
                act_e.wait_ge(attn_in, 16 * 5)
                for (hi, _), src in ((wq, s[0][:, 0:4, :]), (wk, s[0][:, 4:8, :]), (wv, s[1][:, 0:4, :]),
                                     (wo, pT[:, :, :])):
                    act_e.activation(hi[:, :, :].rearrange("p a b -> p (a b)"), src.rearrange("p a b -> p (a b)"),
                                     ACT.Copy).then_inc(attn_hi, 1)
                act_e.activation(wg[0][:, :, :].rearrange("p a b -> p (a b)"), s[1][:, 4, 0:2 * EXPERTS],
                                 ACT.Copy).then_inc(attn_hi, 1)

            def w_high(v, e):
                act_e.wait_ge(w_in[e // 6], 16)
                wait(act_e, u_ps, 18 * v + e - 1)
                act_e.activation(w13[e % 2][0][:, :], w_raw[:, e, 0:2 * D], ACT.Copy).then_inc(w13_hi, 1)
                wait(act_e, y_ps, 36 * v + (2 * e - 4 if e == 0 else max(2 * e - 4,
                                                                         0)))
                act_e.activation(w2[e % 3][0][:, :], w_raw[:, e, 2 * D:3 * D], ACT.Copy).then_inc(w2_hi, 1)

            def tanh(v, e):
                act_e.wait_ge(g_ps, 18 * v + e + 1)
                wait(act_e, act_ready, 18 * v + e)
                act_e.activation(th[:, :], ps_g[:, :], ACT.Tanh, scale=0.5).then_inc(tanh_ready, 1)

            def act_high(v, e):
                act_e.wait_ge(act_ready, 18 * v + e + 1)
                wait(act_e, y_ps, 36 * v + max(2 * e - 2, 0))
                act_e.activation(act[e % 2][0][:, :], act_f[:, :], ACT.Copy).then_inc(act_hi, 1)

            def xT_high(w, j):
                act_e.wait_ge(xT_ps, 2 * w + j + 1)
                wait(act_e, v_ps, 4 * w)
                act_e.activation(xT[0][:, :, 2 * j * P:(2 * j + 2) * P], ps_xT[j], ACT.Copy).then_inc(xT_hi, 1)

            def qk(w, c):
                act_e.wait_ge(q_ps, 2 * w + c + 1)
                act_e.activation(qf[:, c, :], ps_q, ACT.Identity, bias=bq[:, c:c + 1]).then_inc(q_ready, 1)
                act_e.wait_ge(k_ps, 2 * w + c + 1)
                act_e.activation(kf[:, c, :], ps_k, ACT.Identity, bias=bk[:, c:c + 1]).then_inc(k_ready, 1)

            def exp(w, n, half):
                if half == 0:
                    act_e.wait_ge(negmax_ready, 8 * w + n + 1)
                for h in range(4 * half, 4 * half + 4):
                    m = act_e.activation(s[n % 2][:, h, :], s[n % 2][:, h, :], ACT.Exp,
                                         bias=negmax[:, n % 2, h:h + 1],
                                         accum_out=rowsum[:, n % 2, h:h + 1])
                if half == 1:
                    m.then_inc(probs, 1)

            def pT_copy(w, n):
                act_e.wait_ge(pT_ps, 8 * w + n + 1)
                wait(act_e, oT_ps, 8 * w + n)
                act_e.activation(pT[:, :, :], ps_p[:, :, :], ACT.Copy).then_inc(pT_ready, 1)

            def oT_high(w, n):
                act_e.wait_ge(oT_ps, 8 * w + n + 1)
                wait(act_e, wo_ps, 4 * w + n // 2)
                c = n % 2
                act_e.activation(oT[0][:, 2 * c:2 * c + 2, :], ps_o, ACT.Copy).then_inc(oT_hi, 1)

            def yT_high(w, j):
                act_e.wait_ge(yT_ps, 2 * w + j + 1)
                act_e.activation(yT_next[0][:, :, 2 * j * P:(2 * j + 2) * P], ps_yT, ACT.Copy).then_inc(yT_hi, 1)

            def move(w):
                wait(act_e, u_ps, 18 * w)
                act_e.activation(yT[0][:, :, :], yT_next[0][:, :, :].bitcast(F32), ACT.Copy).then_inc(moved_hi, 1)

            def gate_exp_of(w):
                act_e.wait_ge(gate_ps, w + 1)
                wait(act_e, gate_step, GATE_OPS * w)
                act_e.activation(g_e[:, :, :], ps_gate, ACT.Exp, scale=-1.0).then_inc(gate_exp, 1)

            def slots(w, v, attn, moe, more):
                for k in range(SLOTS):
                    if attn:
                        if 0 <= k - 7 < UNITS:
                            oT_high(w, k - 7)
                        if 0 <= k - 6 < UNITS:
                            pT_copy(w, k - 6)
                    if moe:
                        if k + 1 < SLOTS:
                            w_high(v, k + 1)
                        tanh(v, k)
                    if attn and k in (12, 15):
                        yT_high(w, (k - 12) // 3)
                    if attn and k == 16:
                        gate_exp_of(w)
                    if attn and 0 <= k - 4 < UNITS:
                        exp(w, k - 4, 0)
                    if moe:
                        act_high(v, k)
                    if attn:
                        if 0 <= k - 4 < UNITS:
                            exp(w, k - 4, 1)
                        if k in (0, 1):
                            qk(w, k)
                        if k == 16 and more:
                            xT_high(w + 1, 0)
                            xT_high(w + 1, 1)

            def end(w, v, attn, moe, more):
                if attn:
                    w_high(w, 0)
                    move(w)

            def begin():
                split_attention()
                xT_high(0, 0)
                xT_high(0, 1)

            schedule(act_e, begin, slots, end)

        @block.vector
        def _(dve):
            def split_attention():
                for n, ((hi, lo), src) in enumerate(((wq, s[0][:, 0:4, :]), (wk, s[0][:, 4:8, :]),
                                                     (wv, s[1][:, 0:4, :]), (wo, pT[:, :, :]))):
                    dve.wait_ge(attn_hi, n + 1)
                    dve.tensor_tensor(lo[:, :, :].rearrange("p a b -> p (a b)"), src.rearrange("p a b -> p (a b)"),
                                      hi[:, :,
                                         :].rearrange("p a b -> p (a b)").bitcast(F32),
                                         ALU.subtract).then_inc(attn_lo, 1)
                dve.wait_ge(attn_hi, 5)
                dve.tensor_tensor(wg[1][:, :, :].rearrange("p a b -> p (a b)"), s[1][:, 4, 0:2 * EXPERTS],
                                  wg[0][:, :,
                                        :].rearrange("p a b -> p (a b)").bitcast(F32),
                                        ALU.subtract).then_inc(attn_lo, 1)

            def x_stats(w, i):
                n = 4 * w + i + 1
                dve.wait_ge(x_in, 16 * w + 16)
                dve.bn_stats(st[:, i, :], x[:, i, :]).then_inc(st_ready, 1)
                dve.wait_ge(st_ready, n)
                dve.memset(ve[:, i:i + 1], EPS)
                dve.bn_aggr(mv[:, i, :], st[:, i, :]).then_inc(mv_ready, 1)
                dve.wait_ge(mv_ready, n)
                dve.tensor_tensor(ve[:, i:i + 1], mv[:, i, 1:2], ve[:, i:i + 1], ALU.add).then_inc(ve_ready, 1)

            def x_norm(w, i):
                dve.wait_ge(rs_ready, 4 * w + i + 1)
                wait(dve, yT_ps, 2 * w)
                dve.tensor_scalar(y[:, i, :], x[:, i, :], mv[:, i, 0:1], rs[:, i:i + 1], ALU.subtract,
                                  ALU.mult).then_inc(x_ready, 1)

            def xT_low(w, j):
                dve.wait_ge(xT_hi, 2 * w + j + 1)
                sl = slice(2 * j * P, (2 * j + 2) * P)
                dve.tensor_tensor(xT[1][:, :, sl], ps_xT[j], xT[0][:, :, sl].bitcast(F32),
                                  ALU.subtract).then_inc(xT_lo, 1)

            def values(w, m):
                if m == 0:
                    wait(dve, oT_ps, 8 * w)
                    dve.wait_ge(zeros_ready, 1)
                dve.wait_ge(v_ps, 4 * w + m + 1)
                dve.tensor_tensor(vw[:, 2 * m:2 * m + 2, 0:D], ps_v[m % 2],
                                  bv[:, :].unsqueeze(1).broadcast_to([P, 2, D]), ALU.add).then_inc(v_ready, 1)

            def mask_scores(w, n):
                i = n // 2
                dve.wait_ge(scores, 8 * w + n + 1)
                wait(dve, pT_ps, 8 * w + n - 1)
                kind = 0 if i == 0 else 2 if i == TT - 1 else 1
                dve.tensor_tensor(s[n % 2][:, :, :], ps_s[:, :, :],
                                  band[:, kind, :].unsqueeze(1).broadcast_to([P, HC, P]), ALU.add).then_inc(masked, 1)

            def neg_max(w, n):
                dve.wait_ge(masked, 8 * w + n + 1)
                dve.tensor_reduce(negmax[:, n % 2, :], s[n % 2][:, :, :], AX_X, ALU.max,
                                  negate=True).then_inc(negmax_ready, 1)

            def inverse(w, n):
                dve.wait_ge(probs, 8 * w + n + 1)
                wait(dve, probs_ready, 8 * w + n - 1)
                dve.reciprocal(rinv[:, n % 2, :], rowsum[:, n % 2, :]).then_inc(rinv_ready, 1)

            def oT_low(w, n):
                dve.wait_ge(oT_hi, 8 * w + n + 1)
                c = n % 2
                dve.tensor_tensor(oT[1][:, 2 * c:2 * c + 2, :], ps_o, oT[0][:, 2 * c:2 * c + 2, :].bitcast(F32),
                                  ALU.subtract).then_inc(oT_lo, 1)

            def residual(w, i):
                dve.wait_ge(wo_ps, 4 * w + i + 1)
                dve.wait_ge(hb_ready, w + 1)
                dve.tensor_tensor(h2[:, i, :], ps_x[:, 0:D], h2[:, i, :], ALU.add).then_inc(h2_ready, 1)

            def y_stats(w, i):
                n = 4 * w + i + 1
                dve.wait_ge(h2_ready, n)
                dve.bn_stats(sty[:, i, :], h2[:, i, :]).then_inc(sty_ready, 1)
                dve.wait_ge(sty_ready, n)
                dve.memset(vey[:, i:i + 1], EPS)
                dve.bn_aggr(mvy[:, i, :], sty[:, i, :]).then_inc(mvy_ready, 1)
                dve.wait_ge(mvy_ready, n)
                dve.tensor_tensor(vey[:, i:i + 1], mvy[:, i, 1:2], vey[:, i:i + 1], ALU.add).then_inc(vey_ready, 1)

            def y_norm(w, i):
                dve.wait_ge(rsy_ready, 4 * w + i + 1)
                dve.tensor_scalar(y[:, i, :], h2[:, i, :], mvy[:, i, 0:1], rsy[:, i:i + 1], ALU.subtract,
                                  ALU.mult).then_inc(y_ready, 1)

            def yT_low(w, j):
                dve.wait_ge(yT_hi, 2 * w + j + 1)
                hi, lo = (yT_next[n][:, :, 2 * j * P:(2 * j + 2) * P] for n in range(2))
                dve.tensor_tensor(lo, ps_yT, hi.bitcast(F32), ALU.subtract).then_inc(yT_lo, 1)

            def move(w):
                wait(dve, u_ps, 18 * w)
                dve.tensor_copy(yT[1][:, :, :], yT_next[1][:, :, :].bitcast(F32)).then_inc(moved_lo, 1)

            def silu(v, e):
                n = 18 * v + e + 1
                dve.wait_ge(tanh_ready, n)
                dve.scalar_tensor_tensor(out=th[:, :], in0=th[:, :], scalar=1.0, in1=ps_g[:, :], op0=ALU.add,
                                         op1=ALU.mult).then_inc(silu_ready, 1)

            def times_u(v, e):
                n = 18 * v + e + 1
                if e - 1 in LOW_BY_POOL:
                    wait_act_low(dve, v, e - 1)
                dve.wait_ge(silu_ready, n)
                dve.wait_ge(u_ps, n)
                dve.scalar_tensor_tensor(out=act_f[:, :], in0=th[:, :], scalar=0.5, in1=ps_u[:, :], op0=ALU.mult,
                                         op1=ALU.mult).then_inc(act_ready, 1)

            def add_expert(v, e, j, attn):
                dve.wait_ge(y_ps, 36 * v + 2 * e + j + 1)
                if e == 0 and j == 0:
                    dve.wait_ge(ones_ready, 1)
                    wait(dve, out_done, 16 * v)
                if e == SHARED and j == 0:
                    dve.wait_ge(gate_step, GATE_OPS * v + GATE_OPS)
                for i in (2 * j, 2 * j + 1):
                    if e > 0:
                        dve.wait_ge(acc_ready, 72 * v + 4 * e - 4 + i + 1)
                    bank = y_bank(e, j, attn)
                    dve.scalar_tensor_tensor(out=acc[:, i, :], in0=bank[:, i % 2, :], scalar=weight[:, i, e:e + 1],
                                             in1=h2[:, i, :] if e == 0 else acc[:, i,
                                                                                :], op0=ALU.mult,
                                                                                op1=ALU.add).then_inc(acc_ready, 1)

            def gate(w, part):
                done = [0 if part == 0 else GATE_PARTS[part - 1]]

                def then(ins, last=False):
                    done[0] += 1
                    ins.then_inc(gate_step, 1)
                    if not last:
                        dve.wait_ge(gate_step, GATE_OPS * w + done[0])

                def ranks(out_, scores_, before, size, which=(0, 1, 2)):
                    g = g_a[:, :, 0:size, 0:size]
                    e = g_b[:, :, 0:size, 0:size]
                    other = scores_.unsqueeze(2).broadcast_to([P, TT, size, size])
                    own = scores_.unsqueeze(3).broadcast_to([P, TT, size, size])
                    if 0 in which:
                        then(dve.tensor_tensor(g, other, own, ALU.is_gt))
                        then(dve.tensor_tensor(e, other, own, ALU.is_ge))
                    if 1 in which:
                        then(dve.tensor_tensor(e, e, before.unsqueeze(1).broadcast_to([P, TT, size, size]), ALU.mult))
                        then(dve.tensor_tensor(g, g, e, ALU.max))
                    if 2 in which:
                        then(dve.tensor_reduce(out_, g, AX_X, ALU.add))

                four = g_s[:, :, :].rearrange("p i (g e) -> p (i g) e", e=4)
                if part == 0:
                    dve.wait_ge(gate_exp, w + 1)
                    then(dve.tensor_scalar(g_e[:, :, :], g_e[:, :, :], 1.0, None, ALU.add))
                    then(dve.reciprocal(g_s[:, :, :], g_e[:, :, :]))
                    then(dve.tensor_tensor(g_two[:, :, 0:3], four[:, :, 0:3], four[:, :, 1:4], ALU.add))
                    then(dve.tensor_tensor(g_two[:, :, 3:5], four[:, :, 0:2], four[:, :, 2:4], ALU.add))
                    then(dve.tensor_tensor(g_two[:, :, 5:6], four[:, :, 0:1], four[:, :, 3:4], ALU.add))
                    then(dve.tensor_reduce(g_top[:, :, :].rearrange("p i g -> p (i g)"), g_two[:, :, :], AX_X,
                                           ALU.max))
                elif part == 1:
                    ranks(g_rank[:, :, 0:GROUPS], g_top[:, :, :], before4[:, :, :], GROUPS)
                    ok3 = g_ok[:, :].rearrange("p (i g) -> p i g", i=TT)
                    then(dve.tensor_scalar(ok3, g_rank[:, :, 0:GROUPS], float(TOP_GROUPS), None, ALU.is_lt))
                    then(dve.tensor_scalar(g_okm[:, :], g_ok[:, :], 1.0, None, ALU.subtract))
                    m4 = g_m[:, :, :].rearrange("p i (g e) -> p (i g) e", e=4)
                    then(dve.tensor_tensor(m4, four, g_ok[:, :].unsqueeze(2).broadcast_to([P, TT * GROUPS, 4]),
                                           ALU.mult))
                    then(dve.tensor_tensor(m4, m4, g_okm[:, :].unsqueeze(2).broadcast_to([P, TT * GROUPS, 4]),
                                           ALU.add))
                else:
                    ranks(g_rank[:, :, :], g_m[:, :, :], before16[:, :, :], EXPERTS, (part - 2,))
                if part == 4:
                    then(dve.scalar_tensor_tensor(out=g_w[:, :, :], in0=g_rank[:, :, :], scalar=float(TOP),
                                                  in1=g_s[:, :, :],
                                                  op0=ALU.is_lt, op1=ALU.mult))
                    then(dve.tensor_reduce(g_sum[:, :], g_w[:, :, :], AX_X, ALU.add))
                    then(dve.tensor_scalar(g_sum[:, :], g_sum[:, :], 1e-6, None, ALU.add))
                    then(dve.reciprocal(g_sum[:, :], g_sum[:, :]))
                    ins = dve.tensor_tensor(weight[:, :, SHARED:SLOTS], g_w[:, :, :],
                                            g_sum[:, :].unsqueeze(2).broadcast_to([P, TT, EXPERTS]), ALU.mult)
                    then(ins, last=True)
                assert done[0] == GATE_PARTS[part], done[0]

            def slots(w, v, attn, moe, more):
                for k in range(SLOTS):
                    if moe and k == 0:
                        gate(v, 1)
                    if moe and k >= 2 and not (attn and 0 <= k - 4 < UNITS):
                        add_expert(v, k - 2, 1, attn)
                    if attn:
                        if 0 <= k - 7 < UNITS:
                            oT_low(w, k - 7)
                        if k in (9, 11, 13, 15):
                            y_norm(w, (k - 9) // 2)
                    if moe:
                        silu(v, k)
                    if attn and k in (12, 15):
                        yT_low(w, (k - 12) // 3)
                    if moe:
                        times_u(v, k)
                        if k == 0:
                            gate(v, 2)
                        if k >= 1:
                            add_expert(v, k - 1, 0, attn)
                        if k not in LOW_BY_POOL:
                            take_act_low(dve, v, k)
                    if attn:
                        if not moe and 0 <= k - 4 < UNITS:
                            inverse(w, k - 4)
                        if k in (8, 10, 12, 14):
                            residual(w, (k - 8) // 2)
                        if 0 <= k - 3 < UNITS:
                            mask_scores(w, k - 3)
                        if k in (8, 10, 12, 14):
                            y_stats(w, (k - 8) // 2)
                        if moe and 0 <= k - 4 < UNITS:
                            inverse(w, k - 4)
                        if 0 <= k - 3 < UNITS:
                            if moe:
                                add_expert(v, k - 1, 1, attn)
                            neg_max(w, k - 3)
                        if k in (1, 2):
                            values(w, 2 * k - 2)
                            values(w, 2 * k - 1)
                        if more and 0 <= k - 11 < TT:
                            x_stats(w + 1, k - 11)
                        if k == 15 and more:
                            for i in range(TT):
                                x_norm(w + 1, i)
                        if k == 16:
                            gate(w, 0)
                        if k == 16 and more:
                            xT_low(w + 1, 0)
                            xT_low(w + 1, 1)
                    if moe and k in (0, 1):
                        gate(v, k + 3)

            def end(w, v, attn, moe, more):
                if moe:
                    add_expert(v, SLOTS - 2, 1, attn)
                if attn:
                    move(w)
                if moe:
                    add_expert(v, SLOTS - 1, 0, attn)
                if moe:
                    add_expert(v, SLOTS - 1, 1, attn)

            def begin():
                for i in range(TT):
                    x_stats(0, i)
                for i in range(TT):
                    x_norm(0, i)
                split_attention()
                xT_low(0, 0)
                xT_low(0, 1)

            schedule(dve, begin, slots, end)

        @block.tensor
        def _(pe):
            def up(v, e, which):
                hi, lo = w13[e % 2]
                if which == 0:
                    if e == 0:
                        pe.wait_ge(moved_hi, v + 1)
                        pe.wait_ge(moved_lo, v + 1)
                    pe.wait_ge(w13_lo, 18 * v + e + 1)
                    wait(pe, silu_ready, 18 * v + e)
                else:
                    wait(pe, act_ready, 18 * v + e)
                bank, done = ((ps_g, g_ps), (ps_u, u_ps))[which]
                for k in range(KD):
                    c = (2 * which + k) * P
                    m = passes(pe, bank[:, :], (hi[:, c:c + P], lo[:, c:c + P]), (yT[0][:, k, :], yT[1][:, k, :]),
                               k == 0, k == KD - 1)
                m.then_inc(done, 1)

            def down(v, e, j, attn):
                hi, lo = w2[e % 3]
                if j == 0:
                    wait_act_low(pe, v, e)
                    pe.wait_ge(w2_lo, 18 * v + e + 1)
                if j == 0:
                    pe.wait_ge(acc_ready, 72 * v + (4 * e - 2 if e >= 1 and apart(e - 1, attn) else 4 * e))
                elif not apart(e, attn):
                    pe.wait_ge(acc_ready, 72 * v + 4 * e + 2)
                elif e == 0 or apart(e - 1, attn):
                    pe.wait_ge(acc_ready, 72 * v + 4 * e)
                else:
                    pe.wait_ge(masked, 8 * v + 16)
                bank = y_bank(e, j, attn)
                for i in (2 * j, 2 * j + 1):
                    sl = slice(i * P, (i + 1) * P)
                    m = passes(pe, bank[:, i % 2, :], (act[e % 2][0][:, sl], act[e % 2][1][:, sl]),
                               (hi[:, :], lo[:, :]))
                m.then_inc(y_ps, 1)

            def turn(src, j, bank):
                for k in range(KD):
                    for i in range(2):
                        m = pe.transpose(bank[:, k, i * P:(i + 1) * P], src[:, 2 * j + i, k * P:(k + 1) * P],
                                         ident[:, :])
                return m

            def turn_x(w, j):
                pe.wait_ge(x_ready, 4 * w + 2 * j + 2)
                wait(pe, pT_ready, 8 * w)
                turn(y, j, ps_xT[j]).then_inc(xT_ps, 1)

            def project(w, c, which):
                if c == 0 and which == 0:
                    pe.wait_ge(xT_lo, 2 * w + 2)
                    pe.wait_ge(attn_lo, 5)
                    wait(pe, masked, 8 * w)
                if c == 0 and which == 1:
                    wait(pe, acc_ready, 72 * w - 72)
                if c == 1:
                    pe.wait_ge((q_ready, k_ready)[which], 2 * w + 1)
                (hi, lo), bank, done = ((wq, ps_q, q_ps), (wk, ps_k, k_ps))[which]
                for k in range(KD):
                    m = passes(pe, bank, (hi[:, k, c * P:(c + 1) * P], lo[:, k, c * P:(c + 1) * P]),
                               (xT[0][:, k, :], xT[1][:, k, :]), k == 0, k == KD - 1)
                m.then_inc(done, 1)

            def values(w, n):
                wait(pe, v_ready, 4 * w + n - 1)
                for b in (2 * n, 2 * n + 1):
                    sl = slice(window(b), window(b) + WIN)
                    for k in range(KD):
                        m = passes(pe, ps_v[n % 2][:, b % 2, :], (xT[0][:, k, sl], xT[1][:, k, sl]),
                                   (wv[0][:, k, :], wv[1][:, k, :]), k == 0, k == KD - 1)
                m.then_inc(v_ps, 1)

            def score(w, n):
                i, c = n // 2, n % 2
                pe.wait_ge(qm_ready, 8 * w + n + 1)
                if n == 0:
                    pe.wait_ge(k_ready, 2 * w + 2)
                wait(pe, masked, 8 * w + n)
                for h in range(HC):
                    for b in range(2):
                        first = window(2 * i + b)
                        m = pe.matmul(ps_s[QB * b:QB * b + QB, h, :], qm[n % 2][:, h, QB * b:QB * b + QB],
                                      kf[:, c, first:first + WIN], start=True, stop=True)
                m.then_inc(scores, 1)

            def turn_probs(w, n):
                pe.wait_ge(probs_ready, 8 * w + n + 1)
                if n == 0:
                    pe.wait_ge(v_ready, 4 * w + 4)
                wait(pe, pT_ready, 8 * w + n)
                for h in range(HC):
                    m = pe.transpose(ps_p[:, h, :], s[n % 2][:, h, :], ident[:, :])
                m.then_inc(pT_ps, 1)

            def mix(w, n):
                i, c = n // 2, n % 2
                pe.wait_ge(pT_ready, 8 * w + n + 1)
                bank_x_free(w, n)
                for h in range(HC):
                    head = HC * c + h
                    for b in range(2):
                        m = pe.matmul(ps_o[32 * (h % HPC):32 * (h % HPC) + 32, h // HPC, QB * b:QB * b + QB],
                                      vw[:, 2 * i + b, HD * head:HD * head + 32], pT[:, h,
                                                                                     QB * b:QB * b + QB], start=True,
                                                                                     stop=True,
                                      skip_group_check=True)
                m.then_inc(oT_ps, 1)

            def bank_x_free(w, n):
                wait(pe, oT_lo, 8 * w + n)
                if n >= 2 and n % 2 == 0:
                    pe.wait_ge(h2_ready, 4 * w + n // 2)
                if n == 0:
                    wait(pe, gate_exp, w)

            def project_out(w, i):
                pe.wait_ge(oT_lo, 8 * w + 2 * i + 2)
                if i == 2:
                    pe.wait_ge(yT_lo, 2 * w + 1)
                for c in range(OC):
                    m = passes(pe, ps_x[:, 0:D], (oT[0][:, c, :], oT[1][:, c, :]), (wo[0][:, c, :], wo[1][:, c, :]),
                               c == 0, c == OC - 1)
                m.then_inc(wo_ps, 1)

            def turn_y(w, j):
                pe.wait_ge(y_ready, 4 * w + 2 * j + 2)
                if j == 0:
                    pe.wait_ge(oT_lo, 8 * w + 6)
                turn(y, j, ps_yT).then_inc(yT_ps, 1)

            def logits(w):
                pe.wait_ge(yT_lo, 2 * w + 2)
                for i in range(TT):
                    sl = slice(i * P, (i + 1) * P)
                    for k in range(KD):
                        m = passes(pe, ps_gate[:, i, :], (yT_next[0][:, k, sl], yT_next[1][:, k, sl]),
                                   (wg[0][:, k, :], wg[1][:, k, :]), k == 0, k == KD - 1)
                m.then_inc(gate_ps, 1)

            def slots(w, v, attn, moe, more):
                for k in range(SLOTS):
                    if moe:
                        up(v, k, 0)
                    if attn and k == 16:
                        logits(w)
                    if moe:
                        up(v, k, 1)
                    if attn and k in (12, 15):
                        turn_y(w, (k - 12) // 3)
                    if moe and k >= 1:
                        down(v, k - 1, 0, attn)
                    if attn:
                        if k == 0:
                            project(w, 0, 1)
                        if k == 1:
                            project(w, 1, 0)
                            project(w, 1, 1)
                        if k in (1, 2):
                            values(w, 2 * k - 2)
                            values(w, 2 * k - 1)
                        if not moe and 0 <= k - 3 < UNITS:
                            score(w, k - 3)
                        if 0 <= k - 5 < UNITS:
                            turn_probs(w, k - 5)
                        if k in (8, 10, 12, 14):
                            project_out(w, (k - 8) // 2)
                        if moe and 0 <= k - 3 < UNITS:
                            score(w, k - 3)
                        if 0 <= k - 6 < UNITS:
                            mix(w, k - 6)
                        if k == 16 and more:
                            turn_x(w + 1, 0)
                            turn_x(w + 1, 1)
                    if moe and k >= 1:
                        down(v, k - 1, 1, attn)

            def end(w, v, attn, moe, more):
                if more:
                    project(w + 1, 0, 0)
                if moe:
                    down(v, SLOTS - 1, 0, attn)
                    down(v, SLOTS - 1, 1, attn)

            def begin():
                turn_x(0, 0)
                turn_x(0, 1)
                pe.wait_ge(consts_in, 16 * 8)
                project(0, 0, 0)

            pe.wait_ge(ident_in, 16)
            schedule(pe, begin, slots, end)


def mixed_lm_kernel(nc, ins, out):
    hidden = nc.dram_tensor("hidden", [BATCH, P, TT, D], F32)
    with nc.sbuf_tensor("state", [P, BATCH, TT, D], F32) as state:
        encoder(nc, ins, state, hidden)
    experts(nc, ins, hidden, out)


def layout(x, _lenS, L0_tok_embed, L0_tok_ln1_g, L0_tok_ln1_b, L0_tok_ln2_g, L0_tok_ln2_b, L0_tok_W1, L0_tok_b1,
           L0_tok_W2, L0_tok_b2, L0_attn_Wq, L0_attn_bq, L0_attn_Wk, L0_attn_bk, L0_attn_Wv, L0_attn_bv, L0_attn_Wo,
           L0_attn_bo, L0_ffn_w_gate, L0_ffn_w1_e, L0_ffn_w3_e, L0_ffn_w2_e, L0_ffn_w1_s, L0_ffn_w3_s, L0_ffn_w2_s):
    def by_rows(w):
        return w.reshape(-1, P, w.shape[1]).transpose(1, 0, 2).reshape(P, -1)

    def up(w):
        return w.reshape(-1, P, KD, P).transpose(3, 0, 2, 1).reshape(P, -1, D)

    wo = np.zeros((OC, HPC, 32, D), np.float32)
    wo[:, :, :HD] = L0_attn_Wo.reshape(OC, HPC, HD, D)
    w1 = np.concatenate([L0_ffn_w1_s.reshape(2, P, D), L0_ffn_w1_e])
    w3 = np.concatenate([L0_ffn_w3_s.reshape(2, P, D), L0_ffn_w3_e])
    w2 = np.concatenate([L0_ffn_w2_s.reshape(D, 2, P).transpose(1, 0, 2), L0_ffn_w2_e])
    arrays = {
        "x": x.reshape(BATCH * TT, P).T, "embed": L0_tok_embed,
        "ln1_g": L0_tok_ln1_g, "ln1_b": L0_tok_ln1_b, "ln2_g": L0_tok_ln2_g, "ln2_b": L0_tok_ln2_b,
        "w1": L0_tok_W1, "w2": L0_tok_W2, "b1": L0_tok_b1.reshape(LAYERS, KF, P).transpose(0, 2, 1), "b2": L0_tok_b2,
        "wq": by_rows(L0_attn_Wq), "wk": by_rows(L0_attn_Wk), "wv": by_rows(L0_attn_Wv),
        "wo": by_rows(wo.reshape(OC * P, D)), "wg": by_rows(L0_ffn_w_gate.T),
        "bq": L0_attn_bq.reshape(KD, P).T, "bk": L0_attn_bk.reshape(KD,
                                                                    P).T, "bv": L0_attn_bv[None],
                                                                    "bo": L0_attn_bo[None],
        "moe": np.concatenate([up(w1), up(w3), w2.transpose(2, 0, 1)], axis=2),
    }

    i = np.arange(D, dtype=np.float32)
    t = np.arange(T, dtype=np.float32)[:, None]
    f = np.float32
    sin = np.sin(t / f(10) ** (f(4) * i / f(D)))
    cos = np.cos(t / f(10) ** (f(4) * (i - f(1)) / f(D)))
    arrays["pos"] = np.where(np.arange(D) % 2 == 0, sin, cos).astype(np.float32)
    arrays["ident"] = np.eye(P, dtype=np.float32)
    band = np.zeros((P, 3, P), np.float32)
    for kind, tile in enumerate((0, 1, TT - 1)):
        for b in range(2):
            q = QB * (2 * tile + b) + np.arange(QB)[:, None]
            k = window(2 * tile + b) + np.arange(WIN)[None, :]
            band[QB * b:QB * b + QB, kind] = np.where(np.abs(q - k) <= HALF, 0.0, -1e30)
    arrays["band"] = band
    arrays["hmask"] = np.where(np.arange(P)[:, None] // HD == np.arange(HC), np.float32(HD ** -0.5),
                               np.float32(0)).astype(np.float32)
    for n in (4, 16):
        arrays[f"before{n}"] = np.broadcast_to(np.tril(np.ones((n, n), np.float32), -1), (P, n, n))
    return {name: np.ascontiguousarray(a) for name, a in arrays.items()}


def kernel(**inputs):
    import concourse.bacc as bacc
    from concourse.bass_utils import run_bass_kernel_spmd

    nc = bacc.Bacc("TRN2", target_bir_lowering=False, num_devices=1)
    arrays = layout(**{name: np.asarray(a) for name, a in inputs.items()})
    ins = {name: nc.dram_tensor(f"in_{name}", a.shape, mybir.dt.from_np(a.dtype), kind="ExternalInput").ap() for name,
           a in arrays.items()}
    out = nc.dram_tensor("out", (BATCH, T, D), F32, kind="ExternalOutput").ap()
    mixed_lm_kernel(nc, ins, out)
    r = run_bass_kernel_spmd(nc, [{f"in_{name}": a for name, a in arrays.items()}], core_ids=[0])
    return r.results[0]["out"]
```
